# Optimizing a Trainium2 kernel written in Bass

```python
import numpy as np
import jax
import jax.numpy as jnp

def _softmax(x, axis=-1):
    return jax.nn.softmax(x, axis=axis)

def _gelu(x):
    return jax.nn.gelu(x, approximate=True)

def _silu(x):
    return jax.nn.silu(x)

def _sigmoid(x):
    return jax.nn.sigmoid(x)

def _layernorm(x, axis=-1, eps=1e-05):
    m = jnp.mean(x, axis=axis, keepdims=True)
    v = jnp.var(x, axis=axis, keepdims=True)
    return (x - m) / jnp.sqrt(v + eps)

def _scatter_add(tgt, idx, src, axis=0):
    return tgt.at[idx].add(src)

def _segment_sum(src, seg, n):
    return jax.ops.segment_sum(src, seg, n)
kernel_name = 'mk_hybrid_d1_jaxref_r8_973894'

def setup_inputs(seed: int=0):
    np.random.seed(seed)
    _w = jnp.asarray

    def _L0_attn_a_setup():
        import jax, jax.numpy as jnp
        import numpy as np
        D_MODEL = 128
        N_HEADS = 16
        WINDOW = 64
        HEAD_DIM = D_MODEL // N_HEADS
        HALF = WINDOW // 2
        NWIN = WINDOW + 1
        LN_EPS = 1e-05

        def _layernorm(x, g, b):
            mu = jnp.mean(x, axis=-1, keepdims=True)
            var = jnp.var(x, axis=-1, keepdims=True)
            return (x - mu) * jax.lax.rsqrt(var + LN_EPS) * g + b

        def _linear_attention(q, k, v):
            q = jax.nn.elu(q) + 1.0
            k = jax.nn.elu(k) + 1.0
            kv = jnp.einsum('bsd,bse->bde', k, v)
            num = jnp.einsum('bsd,bde->bse', q, kv)
            denom = jnp.einsum('bsd,bd->bs', q, k.sum(axis=1))
            return num / (denom[..., None] + 1e-06)

        def _window_attention(q, k, v, rel_bias):
            B, S, _ = q.shape
            qh = q.reshape(B, S, N_HEADS, HEAD_DIM).transpose(0, 2, 1, 3)
            kh = k.reshape(B, S, N_HEADS, HEAD_DIM).transpose(0, 2, 1, 3)
            vh = v.reshape(B, S, N_HEADS, HEAD_DIM).transpose(0, 2, 1, 3)
            kp = jnp.pad(kh, ((0, 0), (0, 0), (HALF, HALF), (0, 0)))
            vp = jnp.pad(vh, ((0, 0), (0, 0), (HALF, HALF), (0, 0)))
            pos = jnp.arange(S)
            scale = np.float32(1.0 / np.sqrt(HEAD_DIM))

            def score_step(_, w):
                off = w - HALF
                ks = jax.lax.dynamic_slice_in_dim(kp, w, S, axis=2)
                s = jnp.einsum('bhsd,bhsd->bhs', qh, ks) * scale
                s = s + rel_bias[off + WINDOW][None, :, None]
                valid = (pos + off >= 0) & (pos + off < S)
                s = jnp.where(valid[None, None, :], s, -jnp.inf)
                return (None, s)
            _, scores = jax.lax.scan(score_step, None, jnp.arange(NWIN))
            attn = jax.nn.softmax(scores, axis=0)

            def out_step(acc, aw):
                a, w = aw
                vs = jax.lax.dynamic_slice_in_dim(vp, w, S, axis=2)
                return (acc + a[..., None] * vs, None)
            out, _ = jax.lax.scan(out_step, jnp.zeros_like(qh), (attn, jnp.arange(NWIN)))
            return out.transpose(0, 2, 1, 3).reshape(B, S, D_MODEL)
        key = jax.random.key(seed)
        ks = jax.random.split(key, 16)

        def lin(k, fan_in, shape):
            return (jax.random.normal(k, shape, jnp.float32) / np.sqrt(fan_in)).astype(jnp.float32)
        D = D_MODEL
        inp = {'x': jax.random.normal(ks[0], (2, 256, D), jnp.float32), 'wq_lin': lin(ks[1], D, (D, D)), 'bq_lin': jnp.zeros((D,), jnp.float32), 'wk_lin': lin(ks[2], D, (D, D)), 'bk_lin': jnp.zeros((D,), jnp.float32), 'wv_lin': lin(ks[3], D, (D, D)), 'bv_lin': jnp.zeros((D,), jnp.float32), 'wq_loc': lin(ks[4], D, (D, D)), 'bq_loc': jnp.zeros((D,), jnp.float32), 'wk_loc': lin(ks[5], D, (D, D)), 'bk_loc': jnp.zeros((D,), jnp.float32), 'wv_loc': lin(ks[6], D, (D, D)), 'bv_loc': jnp.zeros((D,), jnp.float32), 'wo': lin(ks[7], D, (D, D)), 'bo': jnp.zeros((D,), jnp.float32), 'wg1': lin(ks[8], 3 * D, (3 * D, D)), 'bg1': jnp.zeros((D,), jnp.float32), 'wg2': lin(ks[9], D, (D, D)), 'bg2': jnp.zeros((D,), jnp.float32), 'rel_bias': jax.random.normal(ks[10], (2 * WINDOW + 1, N_HEADS), jnp.float32), 'ln_g': jnp.ones((D,), jnp.float32), 'ln_b': jnp.zeros((D,), jnp.float32)}
        return inp
    _L0_attn_a_in = _L0_attn_a_setup()

    def _L0_attn_b_setup():
        import jax, jax.numpy as jnp
        import numpy as np
        import math
        INPUT_WIDTH = 128
        KEY_WIDTH = 64
        VALUE_WIDTH = 64
        NUM_HEADS = 16
        NUM_GROUPS = 4
        HEADS_PER_GROUP = NUM_HEADS // NUM_GROUPS
        key = jax.random.key(seed)
        k_x, k_q, k_k, k_v, k_p = jax.random.split(key, 5)
        n, s = (2, 256)

        def lin(k, fan_in, fan_out):
            bound = 1.0 / math.sqrt(fan_in)
            return jax.random.uniform(k, (fan_in, fan_out), minval=-bound, maxval=bound, dtype=jnp.float32)
        return {'X': jax.random.normal(k_x, (n, s, INPUT_WIDTH), dtype=jnp.float32), 'Wq': lin(k_q, INPUT_WIDTH, NUM_HEADS * KEY_WIDTH), 'Wk': lin(k_k, INPUT_WIDTH, NUM_GROUPS * KEY_WIDTH), 'Wv': lin(k_v, INPUT_WIDTH, NUM_GROUPS * VALUE_WIDTH), 'Wpost': lin(k_p, NUM_HEADS * VALUE_WIDTH, INPUT_WIDTH)}
    _L0_attn_b_in = _L0_attn_b_setup()

    def _L0_ffn_setup():
        import jax, jax.numpy as jnp
        import numpy as np
        DIM = 128
        DEPTH = 2
        HEADS = 8
        DIM_HEAD = 64
        WINDOW = 64
        INNER = HEADS * DIM_HEAD
        HID = int(DIM * 4 * 2 / 3)
        B, N = (2, 1024)
        QK_SCALE = 8.0

        def shift_token(t):
            t1, t2 = jnp.split(t, 2, axis=-1)
            t2 = jnp.pad(t2, ((0, 0), (1, 0), (0, 0)))[:, :-1]
            return jnp.concatenate([t1, t2], axis=-1)

        def l2norm(t):
            return t / jnp.clip(jnp.linalg.norm(t, axis=-1, keepdims=True), 1e-12)

        def rotate_half(x):
            x1, x2 = jnp.split(x, 2, axis=-1)
            return jnp.concatenate([-x2, x1], axis=-1)

        def rotary_xpos(q, k):
            n = q.shape[-2]
            half_idx = jnp.arange(0, DIM_HEAD, 2, dtype=jnp.float32)
            inv_freq = 1.0 / 10000.0 ** (half_idx / DIM_HEAD)
            t = jnp.arange(n, dtype=jnp.float32)
            freqs = t[:, None] * inv_freq[None, :]
            freqs = jnp.concatenate([freqs, freqs], axis=-1)
            base = (half_idx + 0.4 * DIM_HEAD) / (1.4 * DIM_HEAD)
            power = (t - n // 2) / float(WINDOW // 2)
            scale = base[None, :] ** power[:, None]
            scale = jnp.concatenate([scale, scale], axis=-1)
            cos, sin = (jnp.cos(freqs), jnp.sin(freqs))
            q = q * cos * scale + rotate_half(q) * sin * scale
            k = k * cos / scale + rotate_half(k) * sin / scale
            return (q, k)

        def local_attention(q, k, v):
            b, h, n, d = q.shape
            w = n // WINDOW
            bq = q.reshape(b, h, w, WINDOW, d) * QK_SCALE
            bk = k.reshape(b, h, w, WINDOW, d)
            bv = v.reshape(b, h, w, WINDOW, d)

            def look_around(t):
                p = jnp.pad(t, ((0, 0), (0, 0), (1, 0), (0, 0), (0, 0)))
                return jnp.concatenate([p[:, :, :w], p[:, :, 1:]], axis=3)
            bk, bv = (look_around(bk), look_around(bv))
            bt = jnp.arange(n).reshape(w, WINDOW)
            btp = jnp.pad(bt, ((1, 0), (0, 0)), constant_values=-1)
            btk = jnp.concatenate([btp[:w], btp[1:]], axis=1)
            sim = jnp.einsum('bhwid,bhwjd->bhwij', bq, bk)
            i = bt[:, :, None]
            j = btk[:, None, :]
            mask = (i < j) | (i > j + WINDOW) | (j == -1)
            sim = jnp.where(mask, -jnp.finfo(sim.dtype).max, sim)
            attn = jax.nn.softmax(sim, axis=-1)
            out = jnp.einsum('bhwij,bhwjd->bhwid', attn, bv)
            return out.reshape(b, h, n, d)

        def _layer(x, wqkv, qs, ksc, wo, lg, lb, w1, b1, w2, b2):
            b, n, _ = x.shape
            h = shift_token(x)
            qkv = h @ wqkv
            q, k, v = jnp.split(qkv, 3, axis=-1)
            to_heads = lambda t: t.reshape(b, n, HEADS, DIM_HEAD).transpose(0, 2, 1, 3)
            q, k, v = (to_heads(q), to_heads(k), to_heads(v))
            q = l2norm(q) * qs
            k = l2norm(k) * ksc
            q, k = rotary_xpos(q, k)
            o = local_attention(q, k, v)
            o = o.transpose(0, 2, 1, 3).reshape(b, n, INNER)
            x = x + o @ wo
            h = shift_token(x)
            mu = h.mean(-1, keepdims=True)
            var = h.var(-1, keepdims=True)
            h = (h - mu) / jnp.sqrt(var + 1e-05) * lg + lb
            h = h @ w1 + b1
            a, g = jnp.split(h, 2, axis=-1)
            h = a * jax.nn.gelu(g, approximate=False)
            x = x + h @ w2 + b2
            return x
        key = jax.random.key(seed)
        ks = jax.random.split(key, 6)
        return {'x': jax.random.normal(ks[0], (B, N, DIM), jnp.float32), 'wqkv': jax.random.normal(ks[1], (DEPTH, DIM, 3 * INNER), jnp.float32) * 0.02, 'q_scale': jnp.ones((DEPTH, DIM_HEAD), jnp.float32), 'k_scale': jnp.ones((DEPTH, DIM_HEAD), jnp.float32), 'wo': jax.random.normal(ks[2], (DEPTH, INNER, DIM), jnp.float32) * 0.02, 'ln_g': jnp.ones((DEPTH, DIM), jnp.float32), 'ln_b': jnp.zeros((DEPTH, DIM), jnp.float32), 'w1': jax.random.normal(ks[3], (DEPTH, DIM, 2 * HID), jnp.float32) * 0.02, 'b1': jnp.zeros((DEPTH, 2 * HID), jnp.float32), 'w2': jax.random.normal(ks[4], (DEPTH, HID, DIM), jnp.float32) * 0.02, 'b2': jnp.zeros((DEPTH, DIM), jnp.float32)}
    _L0_ffn_in = _L0_ffn_setup()
    _d = {'L0_attn_a_x': _L0_attn_a_in['x'], 'L0_attn_a_wq_lin': _L0_attn_a_in['wq_lin'], 'L0_attn_a_bq_lin': _L0_attn_a_in['bq_lin'], 'L0_attn_a_wk_lin': _L0_attn_a_in['wk_lin'], 'L0_attn_a_bk_lin': _L0_attn_a_in['bk_lin'], 'L0_attn_a_wv_lin': _L0_attn_a_in['wv_lin'], 'L0_attn_a_bv_lin': _L0_attn_a_in['bv_lin'], 'L0_attn_a_wq_loc': _L0_attn_a_in['wq_loc'], 'L0_attn_a_bq_loc': _L0_attn_a_in['bq_loc'], 'L0_attn_a_wk_loc': _L0_attn_a_in['wk_loc'], 'L0_attn_a_bk_loc': _L0_attn_a_in['bk_loc'], 'L0_attn_a_wv_loc': _L0_attn_a_in['wv_loc'], 'L0_attn_a_bv_loc': _L0_attn_a_in['bv_loc'], 'L0_attn_a_wo': _L0_attn_a_in['wo'], 'L0_attn_a_bo': _L0_attn_a_in['bo'], 'L0_attn_a_wg1': _L0_attn_a_in['wg1'], 'L0_attn_a_bg1': _L0_attn_a_in['bg1'], 'L0_attn_a_wg2': _L0_attn_a_in['wg2'], 'L0_attn_a_bg2': _L0_attn_a_in['bg2'], 'L0_attn_a_rel_bias': _L0_attn_a_in['rel_bias'], 'L0_attn_a_ln_g': _L0_attn_a_in['ln_g'], 'L0_attn_a_ln_b': _L0_attn_a_in['ln_b'], 'L0_attn_b_Wq': _L0_attn_b_in['Wq'], 'L0_attn_b_Wk': _L0_attn_b_in['Wk'], 'L0_attn_b_Wv': _L0_attn_b_in['Wv'], 'L0_attn_b_Wpost': _L0_attn_b_in['Wpost'], 'L0_ffn_wqkv': _L0_ffn_in['wqkv'], 'L0_ffn_q_scale': _L0_ffn_in['q_scale'], 'L0_ffn_k_scale': _L0_ffn_in['k_scale'], 'L0_ffn_wo': _L0_ffn_in['wo'], 'L0_ffn_ln_g': _L0_ffn_in['ln_g'], 'L0_ffn_ln_b': _L0_ffn_in['ln_b'], 'L0_ffn_w1': _L0_ffn_in['w1'], 'L0_ffn_b1': _L0_ffn_in['b1'], 'L0_ffn_w2': _L0_ffn_in['w2'], 'L0_ffn_b2': _L0_ffn_in['b2']}
    _x0 = _d['L0_attn_a_x']
    _d['L0_attn_a_x'] = jax.random.normal(jax.random.fold_in(jax.random.key(seed), 1), (1, 2048, 128), dtype=_x0.dtype)
    del _x0
    return _d

def reference(L0_attn_a_x, L0_attn_a_wq_lin, L0_attn_a_bq_lin, L0_attn_a_wk_lin, L0_attn_a_bk_lin, L0_attn_a_wv_lin, L0_attn_a_bv_lin, L0_attn_a_wq_loc, L0_attn_a_bq_loc, L0_attn_a_wk_loc, L0_attn_a_bk_loc, L0_attn_a_wv_loc, L0_attn_a_bv_loc, L0_attn_a_wo, L0_attn_a_bo, L0_attn_a_wg1, L0_attn_a_bg1, L0_attn_a_wg2, L0_attn_a_bg2, L0_attn_a_rel_bias, L0_attn_a_ln_g, L0_attn_a_ln_b, L0_attn_b_Wq, L0_attn_b_Wk, L0_attn_b_Wv, L0_attn_b_Wpost, L0_ffn_wqkv, L0_ffn_q_scale, L0_ffn_k_scale, L0_ffn_wo, L0_ffn_ln_g, L0_ffn_ln_b, L0_ffn_w1, L0_ffn_b1, L0_ffn_w2, L0_ffn_b2):

    def _L0_attn_a_ref(x, wq_lin, bq_lin, wk_lin, bk_lin, wv_lin, bv_lin, wq_loc, bq_loc, wk_loc, bk_loc, wv_loc, bv_loc, wo, bo, wg1, bg1, wg2, bg2, rel_bias, ln_g, ln_b):
        import jax, jax.numpy as jnp
        import numpy as np
        D_MODEL = 128
        N_HEADS = 16
        WINDOW = 64
        HEAD_DIM = D_MODEL // N_HEADS
        HALF = WINDOW // 2
        NWIN = WINDOW + 1
        LN_EPS = 1e-05

        def _layernorm(x, g, b):
            mu = jnp.mean(x, axis=-1, keepdims=True)
            var = jnp.var(x, axis=-1, keepdims=True)
            return (x - mu) * jax.lax.rsqrt(var + LN_EPS) * g + b

        def _linear_attention(q, k, v):
            q = jax.nn.elu(q) + 1.0
            k = jax.nn.elu(k) + 1.0
            kv = jnp.einsum('bsd,bse->bde', k, v)
            num = jnp.einsum('bsd,bde->bse', q, kv)
            denom = jnp.einsum('bsd,bd->bs', q, k.sum(axis=1))
            return num / (denom[..., None] + 1e-06)

        def _window_attention(q, k, v, rel_bias):
            B, S, _ = q.shape
            qh = q.reshape(B, S, N_HEADS, HEAD_DIM).transpose(0, 2, 1, 3)
            kh = k.reshape(B, S, N_HEADS, HEAD_DIM).transpose(0, 2, 1, 3)
            vh = v.reshape(B, S, N_HEADS, HEAD_DIM).transpose(0, 2, 1, 3)
            kp = jnp.pad(kh, ((0, 0), (0, 0), (HALF, HALF), (0, 0)))
            vp = jnp.pad(vh, ((0, 0), (0, 0), (HALF, HALF), (0, 0)))
            pos = jnp.arange(S)
            scale = np.float32(1.0 / np.sqrt(HEAD_DIM))

            def score_step(_, w):
                off = w - HALF
                ks = jax.lax.dynamic_slice_in_dim(kp, w, S, axis=2)
                s = jnp.einsum('bhsd,bhsd->bhs', qh, ks) * scale
                s = s + rel_bias[off + WINDOW][None, :, None]
                valid = (pos + off >= 0) & (pos + off < S)
                s = jnp.where(valid[None, None, :], s, -jnp.inf)
                return (None, s)
            _, scores = jax.lax.scan(score_step, None, jnp.arange(NWIN))
            attn = jax.nn.softmax(scores, axis=0)

            def out_step(acc, aw):
                a, w = aw
                vs = jax.lax.dynamic_slice_in_dim(vp, w, S, axis=2)
                return (acc + a[..., None] * vs, None)
            out, _ = jax.lax.scan(out_step, jnp.zeros_like(qh), (attn, jnp.arange(NWIN)))
            return out.transpose(0, 2, 1, 3).reshape(B, S, D_MODEL)
        h = _layernorm(x, ln_g, ln_b)
        lin_out = _linear_attention(h @ wq_lin + bq_lin, h @ wk_lin + bk_lin, h @ wv_lin + bv_lin)
        win_out = _window_attention(h @ wq_loc + bq_loc, h @ wk_loc + bk_loc, h @ wv_loc + bv_loc, rel_bias)
        gate_in = jnp.concatenate([lin_out, win_out, h], axis=-1)
        gate = jax.nn.sigmoid(jnp.maximum(gate_in @ wg1 + bg1, 0.0) @ wg2 + bg2)
        out = gate * lin_out + (1.0 - gate) * win_out
        return out @ wo + bo + x

    def _L0_attn_b_ref(X, Wq, Wk, Wv, Wpost):
        import jax, jax.numpy as jnp
        import numpy as np
        import math
        INPUT_WIDTH = 128
        KEY_WIDTH = 64
        VALUE_WIDTH = 64
        NUM_HEADS = 16
        NUM_GROUPS = 4
        HEADS_PER_GROUP = NUM_HEADS // NUM_GROUPS
        n, s, _ = X.shape
        Q = (X @ Wq).reshape(n, s, NUM_GROUPS, HEADS_PER_GROUP, KEY_WIDTH)
        K = (X @ Wk).reshape(n, s, NUM_GROUPS, KEY_WIDTH)
        V = (X @ Wv).reshape(n, s, NUM_GROUPS, VALUE_WIDTH)
        scale = 1.0 / math.sqrt(KEY_WIDTH)
        raw = jnp.einsum('bsgwe,btge->bstgw', Q, K * scale)
        attn = jax.nn.softmax(raw, axis=2)
        A = jnp.einsum('bstgw,btge->bsgwe', attn, V).reshape(n, s, NUM_HEADS * VALUE_WIDTH)
        P = A @ Wpost
        return X + P

    def _L0_ffn_ref(x, wqkv, q_scale, k_scale, wo, ln_g, ln_b, w1, b1, w2, b2):
        import jax, jax.numpy as jnp
        import numpy as np
        DIM = 128
        DEPTH = 2
        HEADS = 8
        DIM_HEAD = 64
        WINDOW = 64
        INNER = HEADS * DIM_HEAD
        HID = int(DIM * 4 * 2 / 3)
        B, N = (2, 1024)
        QK_SCALE = 8.0

        def shift_token(t):
            t1, t2 = jnp.split(t, 2, axis=-1)
            t2 = jnp.pad(t2, ((0, 0), (1, 0), (0, 0)))[:, :-1]
            return jnp.concatenate([t1, t2], axis=-1)

        def l2norm(t):
            return t / jnp.clip(jnp.linalg.norm(t, axis=-1, keepdims=True), 1e-12)

        def rotate_half(x):
            x1, x2 = jnp.split(x, 2, axis=-1)
            return jnp.concatenate([-x2, x1], axis=-1)

        def rotary_xpos(q, k):
            n = q.shape[-2]
            half_idx = jnp.arange(0, DIM_HEAD, 2, dtype=jnp.float32)
            inv_freq = 1.0 / 10000.0 ** (half_idx / DIM_HEAD)
            t = jnp.arange(n, dtype=jnp.float32)
            freqs = t[:, None] * inv_freq[None, :]
            freqs = jnp.concatenate([freqs, freqs], axis=-1)
            base = (half_idx + 0.4 * DIM_HEAD) / (1.4 * DIM_HEAD)
            power = (t - n // 2) / float(WINDOW // 2)
            scale = base[None, :] ** power[:, None]
            scale = jnp.concatenate([scale, scale], axis=-1)
            cos, sin = (jnp.cos(freqs), jnp.sin(freqs))
            q = q * cos * scale + rotate_half(q) * sin * scale
            k = k * cos / scale + rotate_half(k) * sin / scale
            return (q, k)

        def local_attention(q, k, v):
            b, h, n, d = q.shape
            w = n // WINDOW
            bq = q.reshape(b, h, w, WINDOW, d) * QK_SCALE
            bk = k.reshape(b, h, w, WINDOW, d)
            bv = v.reshape(b, h, w, WINDOW, d)

            def look_around(t):
                p = jnp.pad(t, ((0, 0), (0, 0), (1, 0), (0, 0), (0, 0)))
                return jnp.concatenate([p[:, :, :w], p[:, :, 1:]], axis=3)
            bk, bv = (look_around(bk), look_around(bv))
            bt = jnp.arange(n).reshape(w, WINDOW)
            btp = jnp.pad(bt, ((1, 0), (0, 0)), constant_values=-1)
            btk = jnp.concatenate([btp[:w], btp[1:]], axis=1)
            sim = jnp.einsum('bhwid,bhwjd->bhwij', bq, bk)
            i = bt[:, :, None]
            j = btk[:, None, :]
            mask = (i < j) | (i > j + WINDOW) | (j == -1)
            sim = jnp.where(mask, -jnp.finfo(sim.dtype).max, sim)
            attn = jax.nn.softmax(sim, axis=-1)
            out = jnp.einsum('bhwij,bhwjd->bhwid', attn, bv)
            return out.reshape(b, h, n, d)

        def _layer(x, wqkv, qs, ksc, wo, lg, lb, w1, b1, w2, b2):
            b, n, _ = x.shape
            h = shift_token(x)
            qkv = h @ wqkv
            q, k, v = jnp.split(qkv, 3, axis=-1)
            to_heads = lambda t: t.reshape(b, n, HEADS, DIM_HEAD).transpose(0, 2, 1, 3)
            q, k, v = (to_heads(q), to_heads(k), to_heads(v))
            q = l2norm(q) * qs
            k = l2norm(k) * ksc
            q, k = rotary_xpos(q, k)
            o = local_attention(q, k, v)
            o = o.transpose(0, 2, 1, 3).reshape(b, n, INNER)
            x = x + o @ wo
            h = shift_token(x)
            mu = h.mean(-1, keepdims=True)
            var = h.var(-1, keepdims=True)
            h = (h - mu) / jnp.sqrt(var + 1e-05) * lg + lb
            h = h @ w1 + b1
            a, g = jnp.split(h, 2, axis=-1)
            h = a * jax.nn.gelu(g, approximate=False)
            x = x + h @ w2 + b2
            return x
        for l in range(DEPTH):
            x = _layer(x, wqkv[l], q_scale[l], k_scale[l], wo[l], ln_g[l], ln_b[l], w1[l], b1[l], w2[l], b2[l])
        return x
    x = L0_attn_a_x
    x = x + _L0_attn_a_ref(_layernorm(x, axis=-1), L0_attn_a_wq_lin, L0_attn_a_bq_lin, L0_attn_a_wk_lin, L0_attn_a_bk_lin, L0_attn_a_wv_lin, L0_attn_a_bv_lin, L0_attn_a_wq_loc, L0_attn_a_bq_loc, L0_attn_a_wk_loc, L0_attn_a_bk_loc, L0_attn_a_wv_loc, L0_attn_a_bv_loc, L0_attn_a_wo, L0_attn_a_bo, L0_attn_a_wg1, L0_attn_a_bg1, L0_attn_a_wg2, L0_attn_a_bg2, L0_attn_a_rel_bias, L0_attn_a_ln_g, L0_attn_a_ln_b)
    x = x + _L0_ffn_ref(_layernorm(x, axis=-1), L0_ffn_wqkv, L0_ffn_q_scale, L0_ffn_k_scale, L0_ffn_wo, L0_ffn_ln_g, L0_ffn_ln_b, L0_ffn_w1, L0_ffn_b1, L0_ffn_w2, L0_ffn_b2)
    x = x + _L0_attn_b_ref(_layernorm(x, axis=-1), L0_attn_b_Wq, L0_attn_b_Wk, L0_attn_b_Wv, L0_attn_b_Wpost)
    x = x + _L0_ffn_ref(_layernorm(x, axis=-1), L0_ffn_wqkv, L0_ffn_q_scale, L0_ffn_k_scale, L0_ffn_wo, L0_ffn_ln_g, L0_ffn_ln_b, L0_ffn_w1, L0_ffn_b1, L0_ffn_w2, L0_ffn_b2)
    return x

_drawn_inputs = setup_inputs


def setup_inputs(seed=0):
    import zlib

    import numpy as np

    out = dict(_drawn_inputs(seed))
    spreads = {'L0_attn_a_bq_lin': (0.0, 0.8),
     'L0_attn_a_bk_lin': (0.0, 0.8),
     'L0_attn_a_bv_lin': (0.0, 0.315),
     'L0_attn_a_bq_loc': (0.0, 0.8),
     'L0_attn_a_bk_loc': (0.0, 0.8),
     'L0_attn_a_bv_loc': (0.0, 0.293),
     'L0_attn_a_bo': (0.0, 0.1),
     'L0_attn_a_bg1': (0.0, 0.8),
     'L0_attn_a_bg2': (0.0, 0.8),
     'L0_attn_a_ln_g': (1.0, 0.6),
     'L0_attn_a_ln_b': (0.0, 0.1),
     'L0_ffn_q_scale': (1.0, 0.6),
     'L0_ffn_k_scale': (1.0, 0.6),
     'L0_ffn_ln_g': (1.0, 0.6),
     'L0_ffn_ln_b': (0.0, 0.8),
     'L0_ffn_b1': (0.0, 0.8),
     'L0_ffn_b2': (0.0, 0.1)}
    factors = {'L0_attn_a_wq_lin': 8.0,
     'L0_attn_a_wk_lin': 8.0,
     'L0_attn_a_wg1': 3.849,
     'L0_attn_a_wg2': 3.261,
     'L0_attn_b_Wq': 8.0,
     'L0_attn_b_Wk': 8.0,
     'L0_attn_b_Wv': 7.689,
     'L0_attn_b_Wpost': 6.989,
     'L0_ffn_wqkv': 3.561,
     'L0_ffn_wo': 3.592,
     'L0_ffn_w1': 5.827,
     'L0_ffn_w2': 5.74}
    for name, (base, spread) in spreads.items():
        noise = np.random.default_rng([zlib.crc32(name.encode()), seed]).standard_normal(out[name].shape)
        drawn = base * np.exp(spread * noise) if base else spread * noise
        out[name] = jnp.asarray(drawn.astype(out[name].dtype))
    for name, factor in factors.items():
        out[name] = (out[name] * factor).astype(out[name].dtype)
    return out
```

```python
import math
from contextlib import ExitStack

import concourse.bass as bass
import numpy as np
from concourse import mybir

F32 = mybir.dt.float32
F32R = mybir.dt.float32r
ACT = mybir.ActivationFunctionType
ALU = mybir.AluOpType
AX = mybir.AxisListType

P = 128
D = 128
S = 2048
NT = S // P
BANK = 512
BANDK = 192
HALO_A, HALO_F = 32, 64
NEG = -1.0e30

A_HEADS, A_HD = 16, 8
F_HEADS, F_HD, F_INNER, F_DEPTH = 8, 64, 512, 2
HID = int(D * 4 * 2 / 3)
HID_CUTS = [(0, 128), (128, 128), (256, HID - 256)]
B_GROUPS, B_HPG, B_HD = 4, 4, 64
EPS = 1e-5


def wait(eng, sem, n, base=0):
    if isinstance(n, int) and n <= 0:
        return
    eng.wait_ge(sem, n + base)


def wait_apart(eng, sem, n, base=0):
    if isinstance(n, int) and n <= 0:
        return
    eng.wait_ge(sem, n + base)
    if not isinstance(n + base, int):
        eng.sem_inc(LAUNCH.marks, 1)


def pipeline(eng, count, stages, tail=0):
    span = max(lag for _, lag in stages)
    first = min(count, (span + 3) // 2 * 2)
    last = max(first, count - tail)

    def step(i):
        for stage, lag in stages:
            if 0 <= i - lag < count:
                stage(i - lag, (i - lag) % 2)

    for i in range(first):
        step(i)
    if first < last:
        with eng.Fori(first // 2, last // 2) as pair:
            for k in range(2):
                for stage, lag in stages:
                    stage(pair * 2 + (k - lag), (k - lag) % 2)
    for i in range(last, count + span):
        step(i)


class Names:
    pass


LAUNCH = Names()


class Space:

    def __init__(self, nc, ctx, prefix):
        self.nc, self.ctx, self.prefix = nc, ctx, prefix

    def sb(self, name, shape, dt=F32):
        return self.ctx.enter_context(self.nc.sbuf_tensor(f"{self.prefix}_{name}", shape, dt))

    def ps(self, name, shape):
        return self.ctx.enter_context(self.nc.psum_tensor(f"{self.prefix}_{name}", shape, F32))

    def sem(self, name):
        return LAUNCH.ctx.enter_context(self.nc.semaphore(f"{self.prefix}_{name}"))


def sem_maker(nc, prefix):
    return lambda name: LAUNCH.ctx.enter_context(nc.semaphore(f"{prefix}_{name}"))


def bc(ap, axis, n):
    ap = ap.unsqueeze(axis)
    shape = list(ap.shape)
    shape[axis] = n
    return ap.broadcast_to(shape)


def load_phase(nc, g, dram):
    with ExitStack() as ctx:
        sp_ = Space(nc, ctx, "load")
        loaded, zeroed = sp_.sem("loaded"), sp_.sem("zeroed")
        block = ctx.enter_context(nc.Block())
        loads = [(g.x[:], dram["x"][0].rearrange("(t p) d -> p t d", p=P)),
                 (g.tab[:], dram["tables"].rearrange("(t p) a d -> p t a d", p=P)),
                 (g.bandmask[:], dram["bandmask"])]

        @block.sync
        def _(sp):
            for dst, src in loads:
                sp.dma_start(dst, src).then_inc(loaded, 16)
            sp.wait_ge(loaded, 16 * len(loads))

        @block.gpsimd
        def _(pool):
            pool.memset(g.ident[:], 0.0).then_inc(zeroed, 1)
            pool.memset(g.zcol[:], 0.0)
            pool.memset(g.mhalf[:], -0.5)
            pool.wait_ge(zeroed, 1)
            pool.affine_select(out=g.ident[:], in_=g.ident[:], compare_op=ALU.not_equal, fill=1.0, base=0,
                               pattern=[[-1, P]], channel_multiplier=1).then_inc(LAUNCH.constants_made, 1)


class NormSems:

    def __init__(self, sem):
        self.stats_done = sem("stats_done")
        self.mv_done = sem("mv_done")
        self.rstd_done = sem("rstd_done")
        self.eps_added = sem("eps_added")
        self.normed = sem("normed")
        self.transposed = sem("transposed")
        self.kept = sem("kept")
        self.evacuated = sem("evacuated")


def norm_phase(nc, prefix, src, dst, g, affine_T=None):
    with ExitStack() as ctx:
        m = Space(nc, ctx, prefix)
        stats = m.sb("stats", [P, NT, 6])
        mv = m.sb("mv", [P, NT, 2])
        rstd = m.sb("rstd", [P, NT])
        zs = m.sb("zs", [P, 2, D])
        psT = m.ps("psT", [P, 2, BANK])
        k = LAUNCH.norm
        run, base, base_T = k.runs, k.runs * NT, k.runs_T * NT
        k.runs += 1
        k.runs_T += affine_T is not None
        block = ctx.enter_context(nc.Block())

        @block.vector
        def _(dve):
            with dve.Fori(0, NT) as t:
                dve.bn_stats(stats[:, t, :], src[:, t, :]).then_inc(k.stats_done, 1)
            dve.wait_ge(k.stats_done, base + NT)
            for t in range(NT):
                dve.bn_aggr(mv[:, t, :], stats[:, t, :]).then_inc(k.mv_done, 1)
            dve.wait_ge(k.rstd_done, run + 1)

            def normalise(t, s):
                wait(dve, k.kept, t - 1, base)
                if affine_T is not None:
                    wait(dve, k.transposed, t - 1, base_T)
                dve.tensor_scalar(zs[:, s, :], src[:, t, :], mv[:, t, 0:1], rstd[:, bass.ds(t, 1)],
                                  ALU.subtract, ALU.mult).then_inc(k.normed, 1)

            pipeline(dve, NT, [(normalise, 0)])

        @block.gpsimd
        def _(pool):
            pool.wait_ge(k.mv_done, base + NT)
            pool.tensor_scalar(rstd[:], mv[:, :, 1], EPS, None, ALU.add).then_inc(k.eps_added, 1)
            pool.wait_ge(k.eps_added, run + 1)
            pool.tensor_tensor(rstd[:], rstd[:], bc(g.mhalf[:, 0], 1, NT), ALU.pow).then_inc(k.rstd_done, 1)

            def keep(t, s):
                wait_apart(pool, k.normed, t + 1, base)
                pool.tensor_copy(dst[:, t, :], zs[:, s, :]).then_inc(k.kept, 1)

            pipeline(pool, NT, [(keep, 0)])

        if affine_T is None:
            return
        out, scale, shift, pad = affine_T

        @block.tensor
        def _(pe):
            def transpose(t, s):
                wait(pe, k.normed, t + 1, base)
                wait(pe, k.evacuated, t - 1, base_T)
                pe.transpose(psT[:, s, 0:P], zs[:, s, :], g.ident[:]).then_inc(k.transposed, 1)

            pipeline(pe, NT, [(transpose, 0)])

        @block.scalar
        def _(act):
            def evacuate(t, s):
                wait(act, k.transposed, t + 1, base_T)
                place = out[:, bass.ds(t * P + pad, P)]
                if scale is None:
                    act.copy(place, psT[:, s, 0:P]).then_inc(k.evacuated, 1)
                else:
                    act.activation(place, psT[:, s, 0:P], ACT.Identity, bias=shift, scale=scale)\
                       .then_inc(k.evacuated, 1)

            pipeline(act, NT, [(evacuate, 0)])


def add_phase(nc, prefix, x, y):
    with ExitStack() as ctx:
        block = ctx.enter_context(nc.Block())
        half = NT * 3 // 4

        @block.vector
        def _(dve):
            dve.tensor_tensor(x[:, 0:half, :], x[:, 0:half, :], y[:, 0:half, :], ALU.add)

        @block.gpsimd
        def _(pool):
            pool.tensor_tensor(x[:, half:NT, :], x[:, half:NT, :], y[:, half:NT, :], ALU.add)


def band_phase(nc, prefix, g, w, sems, base):
    with ExitStack() as ctx:
        m = Space(nc, ctx, prefix)
        U, hd = w.units, w.hd
        qs = m.sb("qs", [P, 2, 8, P])
        masked = m.sb("masked", [P, 2, 8, BANDK])
        mx = m.sb("mx", [P, 2, 8])
        nb = m.sb("nb", [P, 2, 8])
        scs = m.sb("scs", [P, 2, 8])
        probs = m.sb("probs", [P, 2, 8, 2 * P])
        sums = m.sb("sums", [P, 2, 8])
        rs = m.sb("rs", [P, 2, 8])
        pts = m.sb("pts", [P, 4, BANK])
        on_width = max(P, 8 * hd)
        on = m.sb("on", [P, 2, on_width])
        ots = m.sb("ots", [P, 4, P])
        psS = m.ps("psS", [P, 4, BANK])
        psT = m.ps("psT", [P, 2, BANK])
        psO = m.ps("psO", [P, BANK])
        psW = m.ps("psW", [P, BANK])
        k = sems
        off = w.prob_offset
        block = ctx.enter_context(nc.Block())

        def S_of(h):
            return psS[:, h // 2, (h % 2) * BANDK:(h % 2 + 1) * BANDK]

        @block.gpsimd
        def _(pool):
            if w.zero_queries:
                pool.memset(qs[:], 0.0).then_inc(k.qs_zeroed, 1)
                wait_apart(pool, k.qs_zeroed, 1, w.run)

            def stage(u, s):
                wait_apart(pool, k.scored, 2 * (u - 1), 2 * base)
                wait_apart(pool, k.exped, 4 * (u - 1), 4 * base)
                w.stage(pool, u, s, qs, scs, k.staged)

            pipeline(pool, U, [(stage, 0)])

        @block.tensor
        def _(pe):
            def score(u, s, half):
                wait(pe, k.staged, w.stage_incs * (u + 1), w.stage_incs * base)
                wait(pe, k.masked, 2 * (u - 1) + half + 1, 2 * base)
                for h in range(4 * half, 4 * half + 4):
                    last = pe.matmul(S_of(h), qs[:, s, h, :], w.keys(u, s, h), start=True, stop=True)
                last.then_inc(k.scored, 1)

            def turn(u, s, q):
                wait(pe, k.exped, 4 * u + q + 1, 4 * base)
                wait(pe, (k.evac_act, k.evac_dve)[q % 2], 2 * u + q // 2, 2 * base)
                for j in range(4):
                    h, b = 2 * q + j // 2, j % 2
                    last = pe.transpose(psT[:, q % 2, j * P:(j + 1) * P],
                                        probs[:, s, h, b * P:(b + 1) * P], g.ident[:])
                last.then_inc(k.transposed, 1)

            def weigh(u, s, q):
                wait(pe, (k.evac_act, k.evac_dve)[q % 2], 2 * u + q // 2 + 1, 2 * base)
                if q == 0:
                    wait(pe, k.normed, u, base)
                for h in (2 * q, 2 * q + 1):
                    for b in range(2):
                        last = pe.matmul(psO[:, h * hd:(h + 1) * hd],
                                         pts[:, q, ((h % 2) * 2 + b) * P:((h % 2) * 2 + b + 1) * P],
                                         w.vals(u, s, h, b), start=b == 0, stop=b == 1)
                last.then_inc(k.weighed, 1)

            nout = w.out_tiles

            def turn_out(u, s):
                wait(pe, k.normed, u + 1, base)
                wait(pe, k.finished, u, base)
                for j in range(nout):
                    last = pe.transpose(psW[:, j * P:(j + 1) * P], on[:, s, j * P:(j + 1) * P], g.ident[:])
                last.then_inc(k.turned, 1)

            def project(u, s):
                wait(pe, k.turned_kept, u + 1, base)
                for j in range(nout):
                    last = pe.matmul(psW[:, 0:D], ots[:, j, :], w.wo[:, j, :], start=j == 0, stop=j == nout - 1)
                last.then_inc(k.projected, 1)

            def C(half, lag):
                return lambda u, s: score(u, s, half), lag

            def T(q, lag):
                return lambda u, s: turn(u, s, q), lag

            def W(q, lag):
                return lambda u, s: weigh(u, s, q), lag

            if w.wo is None:
                order = [T(2, 3), C(0, 1), C(1, 1), (turn_out, 4), W(0, 3), T(3, 3), W(1, 3), T(0, 2),
                         W(2, 3), W(3, 3), T(1, 2)]
            else:
                order = [W(3, 3), C(0, 0), T(1, 2), (turn_out, 3), W(0, 2), T(2, 2), C(1, 0), T(3, 2),
                         W(1, 2), T(0, 1), (project, 3), W(2, 2)]
            pipeline(pe, U, order, tail=w.tail)

        @block.vector
        def _(dve):
            dve.memset(probs[:], 0.0).then_inc(k.probs_zeroed, 1)
            if on_width > 8 * hd:
                dve.memset(on[:], 0.0).then_inc(k.on_zeroed, 1)
                dve.wait_ge(k.on_zeroed, 1)

            def evac(u, s, q):
                wait(dve, k.transposed, 4 * u + q + 1, 4 * base)
                wait(dve, k.weighed, 4 * (u - 1) + q + 1, 4 * base)
                dve.tensor_copy(pts[:, q, :], psT[:, 1, :]).then_inc(k.evac_dve, 1)

            def mask(u, s, half):
                wait(dve, k.scored, 2 * u + half + 1, 2 * base)
                wait(dve, k.exped, 4 * (u - 2) + 2 * half + 2, 4 * base)
                out4 = masked[:, s, 4 * half:4 * half + 4].rearrange("p (b h) n -> p b h n", b=2)
                in4 = psS[:, 2 * half:2 * half + 2, 0:2 * BANDK].rearrange("p b (h n) -> p b h n", h=2)
                w.mask(dve, u, s, half, out4, in4, masked[:, s, 4 * half:4 * half + 4], k.masked)

            def bias(u, s, half):
                cut = slice(4 * half, 4 * half + 4)
                wait(dve, k.masked, 2 * u + half + 1, 2 * base)
                dve.tensor_reduce(mx[:, s, cut], masked[:, s, cut], axis=AX.X, op=ALU.max).then_inc(k.maxed, 1)
                wait(dve, k.maxed, 2 * u + half + 1, 2 * base)
                if w.scaled:
                    wait(dve, k.staged, w.stage_incs * (u + 1), w.stage_incs * base)
                    dve.scalar_tensor_tensor(nb[:, s, cut], mx[:, s, cut], -1.0, scs[:, s, cut], ALU.mult, ALU.mult)\
                       .then_inc(k.biased, 1)
                else:
                    dve.tensor_scalar(nb[:, s, cut], mx[:, s, cut], -1.0, None, ALU.mult).then_inc(k.biased, 1)

            def recip(u, s):
                wait(dve, k.exped, 4 * u + 4, 4 * base)
                wait(dve, k.normed, u - 1, base)
                dve.reciprocal(rs[:, s, :], sums[:, s, :]).then_inc(k.recip, 1)

            def norm(u, s):
                wait(dve, k.recip, u + 1, base)
                wait(dve, k.weighed, 4 * u + 4, 4 * base)
                wait(dve, k.turned, u - 1, base)
                at = w.out_column(s)
                dve.tensor_tensor(on[:, s, at:at + 8 * hd].rearrange("p (h d) -> p h d", h=8),
                                  psO[:, 0:8 * hd].rearrange("p (h d) -> p h d", h=8),
                                  bc(rs[:, s, :], 2, hd), ALU.mult).then_inc(k.normed, 1)

            def finish(u, s):
                w.finish(dve, u, s, psW, k, base)

            def M(half, lag):
                return lambda u, s: mask(u, s, half), lag

            def X(half, lag):
                return lambda u, s: bias(u, s, half), lag

            def V(half, lag):
                return lambda u, s: evac(u, s, 2 * half + 1), lag

            if w.wo is None:
                order = [V(0, 2), (recip, 1), M(0, 0), V(1, 2), X(0, 0), M(1, 0), (norm, 2), X(1, 0)]
            else:
                order = [V(0, 2), M(0, 0), X(0, 0), M(1, 0), V(1, 2), X(1, 0), (norm, 2), (recip, 1),
                         (finish, 3)]
            pipeline(dve, U, order, tail=w.tail)

        @block.scalar
        def _(act):
            act.wait_ge(k.probs_zeroed, 1 + w.run)

            def evac(u, s, q):
                wait(act, k.transposed, 4 * u + q + 1, 4 * base)
                wait(act, k.weighed, 4 * (u - 1) + q + 1, 4 * base)
                act.copy(pts[:, q, :], psT[:, 0, :]).then_inc(k.evac_act, 1)

            def exp(u, s, q):
                wait(act, k.biased, 2 * u + q // 2 + 1, 2 * base)
                if q == 0:
                    wait(act, k.transposed, 4 * (u - 1), 4 * base)
                    wait(act, k.recip, u - 1, base)
                for h in (2 * q, 2 * q + 1):
                    last = act.activation(probs[:, s, h, off:off + BANDK], masked[:, s, h, :], ACT.Exp,
                                          bias=nb[:, s, h:h + 1],
                                          scale=scs[:, s, h:h + 1] if w.scaled else 1.0,
                                          accum_out=sums[:, s, h:h + 1])
                last.then_inc(k.exped, 1)

            def keep(u, s):
                wait(act, k.turned, u + 1, base)
                w.keep_turned(act, u, s, psW, ots, k, base)

            def A(half, lag):
                return lambda u, s: evac(u, s, 2 * half), lag

            def E(q, lag):
                return lambda u, s: exp(u, s, q), lag

            if w.wo is None:
                order = [(keep, 4), A(0, 2), E(0, 1), E(1, 1), A(1, 2), E(2, 1), E(3, 1)]
            else:
                order = [E(2, 1), A(0, 2), (keep, 3), E(3, 1), A(1, 2), E(0, 0), E(1, 0)]
            pipeline(act, U, order, tail=w.tail)


class BandSems:

    def __init__(self, sem):
        self.qs_zeroed = sem("qs_zeroed")
        self.probs_zeroed = sem("probs_zeroed")
        self.on_zeroed = sem("on_zeroed")
        self.staged = sem("staged")
        self.scored = sem("scored")
        self.masked = sem("masked")
        self.maxed = sem("maxed")
        self.biased = sem("biased")
        self.exped = sem("exped")
        self.transposed = sem("transposed")
        self.evac_act = sem("evac_act")
        self.evac_dve = sem("evac_dve")
        self.weighed = sem("weighed")
        self.recip = sem("recip")
        self.normed = sem("normed")
        self.turned = sem("turned")
        self.turned_kept = sem("turned_kept")
        self.projected = sem("projected")
        self.added = sem("added")
        self.finished = sem("finished")


def a_project_phase(nc, g, dram, hT, k):
    with ExitStack() as ctx:
        m = Space(nc, ctx, "ap")
        w5 = m.sb("w5", [P, 6, D])
        cols = m.sb("cols", [P, 3])
        rows = m.sb("rows", [P, 3, D])
        hs = m.sb("hs", [P, 2, 2, P])
        kb = m.sb("kb", [P, 2, D])
        kneg = m.sb("kneg", [P, 2, D])
        kexp = m.sb("kexp", [P, 2, D])
        kf = m.sb("kf", [P, 2, D])
        vb = m.sb("vb", [P, 2, D + 2])
        qb = m.sb("qb", [P, BANK])
        qneg = m.sb("qneg", [P, BANK])
        qexp = m.sb("qexp", [P, BANK])
        psKV = m.ps("psKV", [P, 2, BANK])
        psV = m.ps("psV", [P, 2, BANK])
        psA = m.ps("psA", [P, BANK])
        psQ = m.ps("psQ", [P, 3, BANK])
        loaded, staged, kv_done, v_done = m.sem("loaded"), m.sem("staged"), m.sem("kv_done"), m.sem("v_done")
        biased, kexped, featured, summed = m.sem("biased"), m.sem("kexped"), m.sem("featured"), m.sem("summed")
        v_kept, ones_set, kneg_done = m.sem("v_kept"), m.sem("ones_set"), m.sem("kneg_done")
        q_done, q_evac, qneg_done, qexped, q_kept = (m.sem("q_done"), m.sem("q_evac"), m.sem("qneg_done"),
                                                     m.sem("qexped"), m.sem("q_kept"))
        block = ctx.enter_context(nc.Block())
        n_v = NT + 2
        loads = [(w5[:, i, :], dram[n]) for i, n in enumerate(
            ["wk_lin", "wv_lin", "wv_loc", "wq_loc", "wk_loc", "wq_lin"])]
        loads += [(cols[:, i:i + 1], dram[n].unsqueeze(1)) for i, n in enumerate(["bq_loc", "bk_loc", "bq_lin"])]
        loads += [(rows[:, i, :], dram[n].partition_broadcast(P)) for i, n in enumerate(["bk_lin", "bv_lin", "bv_loc"])]
        n_loaded = 16 * len(loads)

        @block.sync
        def _(sp):
            for dst, src in loads:
                sp.dma_start(dst, src).then_inc(loaded, 16)

        @block.gpsimd
        def _(pool):
            pool.memset(vb[:], 1.0).then_inc(ones_set, 1)

            def stage(t, s):
                wait_apart(pool, v_done, t - 1)
                wait_apart(pool, kv_done, t - 1)
                pool.tensor_copy(hs[:, s, 0, :], hT[:, bass.ds(t * P + HALO_A, P)]).then_inc(staged, 1)
                pool.tensor_copy(hs[:, s, 1, :], hT[:, bass.ds(t * P, P)]).then_inc(staged, 1)

            pipeline(pool, n_v, [(stage, 0)])

        @block.tensor
        def _(pe):
            pe.wait_ge(loaded, n_loaded)

            def project(t, s):
                wait(pe, staged, 2 * t + 2)
                wait(pe, biased, 2 * (t - 1))
                wait(pe, v_kept, t - 1)
                pe.matmul(psKV[:, s, 0:2 * D], hs[:, s, 0, :], w5[:, 0:2, :], start=True, stop=True).then_inc(kv_done, 1)
                pe.matmul(psV[:, s, 0:D], hs[:, s, 1, :], w5[:, 2, :], start=True, stop=True).then_inc(v_done, 1)

            def accumulate(t, s):
                if isinstance(t, int) and t >= NT:
                    return
                wait(pe, featured, t + 1)
                first = isinstance(t, int) and t == 0
                last = isinstance(t, int) and t == NT - 1
                pe.matmul(psA[:, 0:D + 1], kf[:, s, :], vb[:, s, 0:D + 1], start=first, stop=last).then_inc(summed, 1)

            pipeline(pe, n_v, [(project, 0), (accumulate, 1)], tail=4)
            for c in range(S // BANK):
                wait(pe, q_evac, 3 * c)
                for j in range(3):
                    pe.matmul(psQ[:, j, :], w5[:, 3 + j, :], hT[:, HALO_A + c * BANK:HALO_A + (c + 1) * BANK],
                              start=True, stop=True).then_inc(q_done, 1)

        @block.vector
        def _(dve):
            dve.wait_ge(loaded, n_loaded)
            dve.wait_ge(ones_set, 1)

            def bias(t, s):
                wait(dve, kv_done, t + 1)
                wait(dve, summed, t - 1)
                wait(dve, kexped, t - 1)
                wait(dve, featured, t - 1)
                dve.tensor_tensor(kb[:, s, :], psKV[:, s, 0:D], rows[:, 0, :], ALU.add).then_inc(biased, 1)
                dve.tensor_tensor(vb[:, s, 0:D], psKV[:, s, D:2 * D], rows[:, 1, :], ALU.add).then_inc(biased, 1)
                wait(dve, v_done, t + 1)
                dve.tensor_tensor(g.vloc[:, t, :], psV[:, s, 0:D], rows[:, 2, :], ALU.add).then_inc(v_kept, 1)
                wait(dve, biased, 2 * t + 2)
                dve.tensor_scalar(kneg[:, s, :], kb[:, s, :], 0.0, None, ALU.min).then_inc(kneg_done, 1)

            def feature(t, s):
                wait(dve, kexped, t + 1)
                wait(dve, summed, t - 1)
                dve.scalar_tensor_tensor(kf[:, s, :], kb[:, s, :], 0.0, kexp[:, s, :], ALU.max, ALU.add)\
                   .then_inc(featured, 1)

            pipeline(dve, n_v, [(bias, 0), (feature, 1)], tail=4)
            dve.wait_ge(summed, NT)
            dve.tensor_copy(g.KV[:], psA[:, 0:D]).then_inc(biased, 1)
            dve.tensor_copy(g.KS[:], psA[:, D:D + 1].broadcast_to([P, P])).then_inc(biased, 1)
            for c in range(S // BANK):
                dve.wait_ge(q_evac, 3 * c + 3)
                wait(dve, qexped, c)
                dve.tensor_scalar(qneg[:], qb[:], 0.0, None, ALU.min).then_inc(qneg_done, 1)
                dve.wait_ge(qexped, c + 1)
                dve.scalar_tensor_tensor(g.qlinT[:, c * BANK:(c + 1) * BANK], qb[:], 0.0, qexp[:], ALU.max, ALU.add)\
                   .then_inc(q_kept, 1)

        @block.scalar
        def _(act):
            def exp(t, s):
                wait(act, kneg_done, t + 1)
                wait(act, featured, t - 1)
                act.activation(kexp[:, s, :], kneg[:, s, :], ACT.Exp).then_inc(kexped, 1)

            pipeline(act, n_v, [(exp, 0)])
            act.wait_ge(loaded, n_loaded)
            for c in range(S // BANK):
                act.wait_ge(q_done, 3 * c + 3)
                wait(act, q_kept, c)
                act.activation(g.qlocT[:, c * BANK:(c + 1) * BANK], psQ[:, 0, :], ACT.Identity,
                               bias=cols[:, 0:1]).then_inc(q_evac, 1)
                act.activation(g.klocT[:, HALO_A + c * BANK:HALO_A + (c + 1) * BANK], psQ[:, 1, :], ACT.Identity,
                               bias=cols[:, 1:2]).then_inc(q_evac, 1)
                act.activation(qb[:], psQ[:, 2, :], ACT.Identity, bias=cols[:, 2:3]).then_inc(q_evac, 1)
                act.wait_ge(qneg_done, c + 1)
                act.activation(qexp[:], qneg[:], ACT.Exp).then_inc(qexped, 1)


def a_window(nc, g, dram, ctx):
    m = Space(nc, ctx, "aw")
    w = Names()
    w.units, w.hd, w.run, w.tail = 2 * NT, A_HD, 0, 4
    w.prob_offset, w.zero_queries, w.scaled = 0, False, False
    w.stage_incs, w.out_tiles = 1, 1
    w.wo, w.finish = None, None
    w.out_column = lambda s: s * 8 * A_HD
    half = lambda u, s: (u - s) // 2 if isinstance(u, int) else (u - s) >> 1
    scale = float(np.float32(1.0 / np.sqrt(A_HD)))
    edge_done, tile_taken = m.sem("edge_done"), m.sem("tile_taken")
    tile = m.sb("tile", [P, 2, P])

    def stage(pool, u, s, qs, scs, staged):
        pool.tensor_copy(tile[:, s, :], g.qlocT[:, bass.ds(half(u, s) * P, P)]).then_inc(tile_taken, 1)
        wait_apart(pool, tile_taken, u + 1)
        pool.tensor_tensor(qs[:, s], bc(tile[:, s, :], 1, 8), bc(g.hmask[:, 8 * s:8 * s + 8], 2, P), ALU.mult).then_inc(staged, 1)

    def mask(dve, u, s, half_, out4, in4, out, masked):
        o = out.rearrange("p (b h) n -> p b (h n)", b=2)
        i = in4.rearrange("p b h n -> p b (h n)")
        at = 8 * s + 4 * half_
        b = g.relb[:, at:at + 4, :].rearrange("p (b h) n -> p b (h n)", b=2)
        edge = isinstance(u, int) and (u < 2 or u >= 2 * NT - 2)
        ins = dve.scalar_tensor_tensor(o, i, scale, b, ALU.mult, ALU.add)
        if edge:
            ins.then_inc(edge_done, 1)
            wait(dve, edge_done, 2 * (u if u < 2 else u - (2 * NT - 2) + 2) + half_ + 1)
            e = g.edge[:, 0 if u < 2 else 1, :]
            ins = dve.tensor_tensor(out, out, bc(e, 1, 4), ALU.add)
        ins.then_inc(masked, 1)

    def keep_turned(act, u, s, psW, ots, k, base):
        act.copy(g.winT[64 * s:64 * s + 64, bass.ds(half(u, s) * P, P)], psW[64 * s:64 * s + 64, 0:P]).then_inc(k.finished, 1)

    w.stage, w.mask, w.keep_turned = stage, mask, keep_turned
    w.keys = lambda u, s, h: g.klocT[:, bass.ds(half(u, s) * P, BANDK)]
    w.vals = lambda u, s, h, b: g.vloc[:, half(u, s) + b, (8 * s + h) * A_HD:(8 * s + h + 1) * A_HD]
    return w


def a_gate_phase(nc, g, dram, hT):
    with ExitStack() as ctx:
        m = Space(nc, ctx, "ag")
        wg1 = m.sb("wg1", [P, 3, D])
        wg2 = m.sb("wg2", [P, D])
        wo = m.sb("wo", [P, D])
        cols = m.sb("cols", [P, 2])
        nbg2 = m.sb("nbg2", [P, 1])
        bo = m.sb("bo", [P, D])
        den = m.sb("den", [P, BANK])
        rden = m.sb("rden", [P, BANK])
        lin = m.sb("lin", [P, BANK])
        g1 = m.sb("g1", [P, BANK])
        eg = m.sb("eg", [P, BANK])
        e1 = m.sb("e1", [P, BANK])
        gate = m.sb("gate", [P, BANK])
        diff = m.sb("diff", [P, BANK])
        gd = m.sb("gd", [P, BANK])
        mix = m.sb("mix", [P, BANK])
        res = m.sb("res", [P, 4, D])
        psN = m.ps("psN", [P, BANK])
        psD = m.ps("psD", [P, BANK])
        psG = m.ps("psG", [P, BANK])
        psH = m.ps("psH", [P, BANK])
        psY = m.ps("psY", [P, BANK])
        loaded, q, d, a = m.sem("loaded"), m.sem("products"), m.sem("dve_step"), m.sem("act_step")
        neg = m.sem("neg")
        stored = m.sem("x_updated")
        block = ctx.enter_context(nc.Block())
        loads = [(wg1[:], dram["wg1"].rearrange("(c p) n -> p c n", p=P)), (wg2[:], dram["wg2"]), (wo[:], dram["wo"]),
                 (cols[:, 0:1], dram["bg1"].unsqueeze(1)), (cols[:, 1:2], dram["bg2"].unsqueeze(1)),
                 (bo[:], dram["bo"].partition_broadcast(P))]
        n_loaded = 16 * len(loads)
        NC_, DV, AC = 5, 9, 2

        @block.sync
        def _(sp):
            for dst, src in loads:
                sp.dma_start(dst, src).then_inc(loaded, 16)

        @block.tensor
        def _(pe):
            pe.wait_ge(loaded, n_loaded)
            for c in range(S // BANK):
                cut = slice(c * BANK, (c + 1) * BANK)
                wait(pe, d, DV * c)
                pe.matmul(psN[:], g.KV[:], g.qlinT[:, cut], start=True, stop=True).then_inc(q, 1)
                pe.matmul(psD[:], g.KS[:], g.qlinT[:, cut], start=True, stop=True).then_inc(q, 1)
                pe.matmul(psG[:], wg1[:, 1, :], g.winT[:, cut], start=True, stop=False)
                pe.matmul(psG[:], wg1[:, 2, :], hT[:, HALO_A + c * BANK:HALO_A + (c + 1) * BANK], start=False, stop=False)
                pe.wait_ge(d, DV * c + 3)
                pe.matmul(psG[:], wg1[:, 0, :], lin[:], start=False, stop=True).then_inc(q, 1)
                pe.wait_ge(a, AC * c + 1)
                pe.matmul(psH[:], wg2[:], g1[:], start=True, stop=True).then_inc(q, 1)
                pe.wait_ge(d, DV * c + 8)
                for j in range(4):
                    last = pe.matmul(psY[:, j * D:(j + 1) * D], mix[:, j * P:(j + 1) * P], wo[:], start=True, stop=True)
                last.then_inc(q, 1)

        @block.scalar
        def _(act):
            act.wait_ge(neg, 1)
            for c in range(S // BANK):
                act.wait_ge(q, NC_ * c + 3)
                act.activation(g1[:], psG[:], ACT.Relu, bias=cols[:, 0:1]).then_inc(a, 1)
                act.wait_ge(q, NC_ * c + 4)
                act.activation(eg[:], psH[:], ACT.Exp, bias=nbg2[:], scale=-1.0).then_inc(a, 1)

        @block.vector
        def _(dve):
            dve.wait_ge(loaded, n_loaded)
            dve.tensor_scalar(nbg2[:], cols[:, 1:2], -1.0, None, ALU.mult).then_inc(neg, 1)
            for c in range(S // BANK):
                cut = slice(c * BANK, (c + 1) * BANK)
                n = DV * c
                dve.wait_ge(q, NC_ * c + 2)
                dve.tensor_scalar(den[:], psD[:], 1e-6, None, ALU.add).then_inc(d, 1)
                dve.wait_ge(d, n + 1)
                dve.reciprocal(rden[:], den[:]).then_inc(d, 1)
                dve.wait_ge(d, n + 2)
                dve.tensor_tensor(lin[:], psN[:], rden[:], ALU.mult).then_inc(d, 1)
                dve.wait_ge(d, n + 3)
                dve.tensor_tensor(diff[:], lin[:], g.winT[:, cut], ALU.subtract).then_inc(d, 1)
                dve.wait_ge(a, AC * c + 2)
                dve.tensor_scalar(e1[:], eg[:], 1.0, None, ALU.add).then_inc(d, 1)
                dve.wait_ge(d, n + 5)
                dve.reciprocal(gate[:], e1[:]).then_inc(d, 1)
                dve.wait_ge(d, n + 6)
                dve.tensor_tensor(gd[:], gate[:], diff[:], ALU.mult).then_inc(d, 1)
                dve.wait_ge(d, n + 7)
                dve.tensor_tensor(mix[:], gd[:], g.winT[:, cut], ALU.add).then_inc(d, 1)
                dve.wait_ge(q, NC_ * c + 5)
                dve.tensor_tensor(res[:], psY[:].rearrange("p (t d) -> p t d", t=4), bc(bo[:], 1, 4), ALU.add)\
                   .then_inc(d, 1)
                dve.wait_ge(d, n + 9)
                dve.tensor_tensor(g.x[:, 4 * c:4 * c + 4, :], g.x[:, 4 * c:4 * c + 4, :], res[:], ALU.add)\
                   .then_inc(stored, 1)


def attention_a(nc, g, dram):
    with ExitStack() as ctx:
        m = Space(nc, ctx, "a")
        z = m.sb("z", [P, NT, D])
        hT = m.sb("hT", [P, (NT + 2) * P + HALO_A + 96])
        g.vloc = m.sb("vloc", [P, NT + 2, D])
        g.qlocT = m.sb("qlocT", [P, S])
        g.klocT = m.sb("klocT", [P, HALO_A + S + BANDK])
        g.qlinT = m.sb("qlinT", [P, S])
        g.winT = m.sb("winT", [P, S])
        g.KV = m.sb("KV", [P, D])
        g.KS = m.sb("KS", [P, P])
        g.relb = m.sb("relb", [P, A_HEADS, BANDK])
        g.edge = m.sb("edge", [P, 2, BANDK])
        g.hmask = m.sb("hmask", [P, A_HEADS])
        ln = m.sb("ln", [P, 2])
        loaded, padded = m.sem("loaded"), m.sem("padded")
        with nc.Block() as block:
            loads = [(ln[:, 0:1], dram["ln_g"].unsqueeze(1)), (ln[:, 1:2], dram["ln_b"].unsqueeze(1)),
                     (g.hmask[:], dram["hmask"]), (g.edge[:], dram["edge"]), (g.relb[:], dram["relb"])]

            @block.sync
            def _(sp):
                for dst, src in loads:
                    sp.dma_start(dst, src).then_inc(loaded, 16)
                sp.wait_ge(loaded, 16 * len(loads))

            @block.gpsimd
            def _(pool):
                pool.memset(hT[:, 0:HALO_A], 0.0)
                pool.memset(hT[:, HALO_A + S:], 0.0)
                pool.memset(g.klocT[:, 0:HALO_A], 0.0)
                pool.memset(g.klocT[:, HALO_A + S:], 0.0).then_inc(padded, 1)

        norm_phase(nc, "anz", g.x, z, g)
        norm_phase(nc, "anh", z, g.vloc, g, (hT, ln[:, 0:1], ln[:, 1:2], HALO_A))
        a_project_phase(nc, g, dram, hT, None)
        add_phase(nc, "axz", g.x, z)
        k = BandSems(sem_maker(nc, "awk"))
        band_phase(nc, "awb", g, a_window(nc, g, dram, ctx), k, 0)
        a_gate_phase(nc, g, dram, hT)


def f_load_phase(nc, g, dram, layer, loaded, base):
    one = bass.ds(layer, 1)

    def of(name):
        return dram[name][one]

    loads = [(g.wqkv[:], of("wqkv")[0]), (g.fwo[:], of("fwo")[0].rearrange("(c p) n -> p c n", p=P)),
             (g.w1[:], of("w1")[0]), (g.lnc[:, 0:1], of("fln_g").rearrange("a p -> p a")),
             (g.lnc[:, 1:2], of("fln_b").rearrange("a p -> p a")), (g.b2[:], of("b2")[0].partition_broadcast(P))]
    h = F_HD // 2
    for j, name in enumerate(["q_scale", "k_scale"]):
        loads.append((g.sc4[:, j, :], of(name)[0].partition_broadcast(P)))
        loads.append((g.sc4[:, 2 + j, 0:h], of(name)[0, h:F_HD].partition_broadcast(P)))
        loads.append((g.sc4[:, 2 + j, h:F_HD], of(name)[0, 0:h].partition_broadcast(P)))
    for c, (at, n) in enumerate(HID_CUTS):
        loads.append((g.w2[0:n, c, :], of("w2")[0, at:at + n]))
        for j in range(2):
            loads.append((g.b1[0:n, 3 * j + c:3 * j + c + 1],
                          of("b1")[0, HID * j + at:HID * j + at + n].unsqueeze(1)))
    with nc.Block() as block:
        @block.sync
        def _(sp):
            for dst, src in loads:
                sp.dma_start(dst, src).then_inc(loaded, 16)

        @block.tensor
        def _(pe):
            pe.wait_ge(loaded, base * (16 * len(loads)) + 16 * len(loads))


class QkvSems:

    def __init__(self, sem):
        self.y_staged = sem("y_staged")
        self.yT_done = sem("yT_done")
        self.hT_ready = sem("hT_ready")
        self.qkv_done = sem("qkv_done")
        self.raw_ready = sem("raw_ready")
        self.v_ready = sem("v_ready")
        self.sq_ready = sem("sq_ready")
        self.ss_done = sem("ss_done")
        self.rot_part = sem("rot_part")
        self.rot_done = sem("rot_done")
        self.tab_ready = sem("tab_ready")
        self.ss_clipped = sem("ss_clipped")
        self.rn_done = sem("rn_done")
        self.k_scaled = sem("k_scaled")
        self.turned = sem("turned")
        self.q_kept = sem("q_kept")
        self.k_kept = sem("k_kept")
        self.padded = sem("padded")


class MlpSems:

    def __init__(self, sem):
        self.y_staged = sem("y_staged")
        self.yT_done = sem("yT_done")
        self.hT_ready = sem("hT_ready")
        self.h_back = sem("h_back")
        self.stats_done = sem("stats_done")
        self.mv_done = sem("mv_done")
        self.eps_added = sem("eps_added")
        self.rstd_done = sem("rstd_done")
        self.normed = sem("normed")
        self.hnT_done = sem("hnT_done")
        self.hnT_ready = sem("hnT_ready")
        self.up_done = sem("up_done")
        self.gelued = sem("gelued")
        self.gated = sem("gated")
        self.down_done = sem("down_done")
        self.b2_added = sem("b2_added")
        self.added = sem("added")


def shifted_copy(act, hT, psT, s, t, zcol, hT_ready, base):
    lo, hi = slice(0, D // 2), slice(D // 2, D)
    act.copy(hT[lo, s, 0:P], psT[lo, 0:P]).then_inc(hT_ready, 1)
    act.copy(hT[hi, s, 1:P + 1], psT[hi, 0:P]).then_inc(hT_ready, 1)
    if isinstance(t, int) and t == 0:
        act.copy(hT[hi, s, 0:1], zcol[hi, :]).then_inc(hT_ready, 1)
    else:
        wait(act, hT_ready, 3 * t, 3 * base)
        act.copy(hT[hi, s, 0:1], hT[hi, 1 - s, P:P + 1]).then_inc(hT_ready, 1)


def f_qkv_phase(nc, prefix, g, k, run):
    base = run * NT
    with ExitStack() as ctx:
        m = Space(nc, ctx, prefix)
        ys = m.sb("ys", [P, 2, D])
        hT = m.sb("hT", [P, 2, P + 1])
        raw = m.sb("raw", [P, 2, 2 * F_INNER])
        sq = m.sb("sq", [P, 2, 2 * F_INNER])
        ss = m.sb("ss", [P, 2, 2 * F_HEADS])
        ssc = m.sb("ssc", [P, 2 * F_HEADS])
        rn = m.sb("rn", [P, 2, 2 * F_HEADS])
        tabw = m.sb("tabw", [P, 2, 4, F_HD])
        part_c = m.sb("part_c", [P, 2 * F_INNER])
        part_s = m.sb("part_s", [P, 2 * F_INNER])
        rot = m.sb("rot", [P, 2, 2 * F_INNER])
        kn = m.sb("kn", [P, 2, F_INNER])
        psT = m.ps("psT", [P, BANK])
        psX = m.ps("psX", [P, 3, BANK])
        psR = m.ps("psR", [P, 2, 2, BANK])
        block = ctx.enter_context(nc.Block())
        H2 = F_HD // 2

        @block.gpsimd
        def _(pool):
            pool.memset(g.KT[:, :, 0:HALO_F], 0.0)
            pool.memset(g.V[:, 0, :], 0.0).then_inc(k.padded, 1)

            def stage(t, s):
                wait_apart(pool, k.yT_done, t - 1, base)
                wait_apart(pool, k.rot_part, 3 * (t - 1), 3 * base)
                pool.tensor_copy(ys[:, s, :], g.y[:, t, :]).then_inc(k.y_staged, 1)
                pool.tensor_tensor(tabw[:, s], g.tab[:, t], g.sc4[:], ALU.mult).then_inc(k.tab_ready, 1)

            def norms(t, s):
                wait_apart(pool, k.ss_done, t + 1, base)
                wait_apart(pool, k.rn_done, 2 * t, 2 * base)
                pool.tensor_scalar(ssc[:], ss[:, s, :], 1e-24, None, ALU.max).then_inc(k.ss_clipped, 1)
                wait_apart(pool, k.ss_clipped, t + 1, base)
                pool.tensor_tensor(rn[:, s, :], ssc[:], bc(g.mhalf[:, 0], 1, 2 * F_HEADS), ALU.pow).then_inc(k.rn_done, 1)
                wait_apart(pool, k.rn_done, 2 * t + 1, 2 * base)
                pool.tensor_copy(g.qscale[:, t, :], rn[:, s, 0:F_HEADS]).then_inc(k.rn_done, 1)

            def scale_k(t, s):
                wait_apart(pool, k.rot_done, t + 1, base)
                wait_apart(pool, k.turned, t - 1, base)
                pool.tensor_tensor(kn[:, s, :].rearrange("p (h d) -> p h d", h=F_HEADS),
                                   rot[:, s, F_INNER:].rearrange("p (h d) -> p h d", h=F_HEADS),
                                   bc(rn[:, s, F_HEADS:], 2, F_HD), ALU.mult).then_inc(k.k_scaled, 1)

            pipeline(pool, NT, [(stage, 0), (norms, 1), (scale_k, 1)])

        @block.tensor
        def _(pe):
            def turn_y(t, s):
                wait(pe, k.y_staged, t + 1, base)
                wait(pe, k.hT_ready, 3 * t, 3 * base)
                pe.transpose(psT[:, 0:P], ys[:, s, :], g.ident[:]).then_inc(k.yT_done, 1)

            def project(t, s):
                wait(pe, k.hT_ready, 3 * t + 3, 3 * base)
                wait(pe, k.raw_ready, t, base)
                wait(pe, k.v_ready, t, base)
                for c in range(3):
                    last = pe.matmul(psX[:, c, :], hT[:, s, 0:P], g.wqkv[:, c * BANK:(c + 1) * BANK],
                                     start=True, stop=True)
                last.then_inc(k.qkv_done, 1)

            def turn_qk(t, s):
                wait(pe, k.rot_done, t + 1, base)
                wait(pe, k.q_kept, t - 1, base)
                wait(pe, k.k_kept, t - 1, base)
                for j in range(4):
                    pe.transpose(psR[:, s, 0, j * P:(j + 1) * P], rot[:, s, j * P:(j + 1) * P], g.ident[:])
                wait(pe, k.k_scaled, t + 1, base)
                for j in range(4):
                    last = pe.transpose(psR[:, s, 1, j * P:(j + 1) * P], kn[:, s, j * P:(j + 1) * P], g.ident[:])
                last.then_inc(k.turned, 1)

            pipeline(pe, NT, [(turn_y, 0), (project, 0), (turn_qk, 2)])

        @block.scalar
        def _(act):
            act.wait_ge(k.padded, 1 + run)

            def take_y(t, s):
                wait(act, k.yT_done, t + 1, base)
                wait(act, k.qkv_done, t - 1, base)
                shifted_copy(act, hT, psT, s, t, g.zcol, k.hT_ready, base)

            def take_qkv(t, s):
                wait(act, k.qkv_done, t + 1, base)
                wait(act, k.rot_part, 3 * (t - 1), 3 * base)
                act.copy(raw[:, s, :].rearrange("p (a n) -> p a n", a=2), psX[:, 0:2, :]).then_inc(k.raw_ready, 1)
                act.copy(g.V[:, t + 1, :], psX[:, 2, :]).then_inc(k.v_ready, 1)
                wait(act, k.raw_ready, t + 1, base)
                wait(act, k.ss_done, t - 1, base)
                act.activation(sq[:, s, :], raw[:, s, :], ACT.Square).then_inc(k.sq_ready, 1)

            def keep(t, s):
                wait(act, k.turned, t + 1, base)
                act.copy(g.QT[:, :, bass.ds(t * P, P)], psR[:, s, 0, :].rearrange("p (c n) -> p c n", c=4))\
                   .then_inc(k.q_kept, 1)
                act.copy(g.KT[:, :, bass.ds(t * P + HALO_F, P)], psR[:, s, 1, :].rearrange("p (c n) -> p c n", c=4))\
                   .then_inc(k.k_kept, 1)

            pipeline(act, NT, [(take_y, 0), (take_qkv, 0), (keep, 2)])

        @block.vector
        def _(dve):
            def sums(t, s):
                wait(dve, k.sq_ready, t + 1, base)
                wait(dve, k.rn_done, 2 * (t - 1), 2 * base)
                dve.tensor_reduce(ss[:, s, :], sq[:, s, :].rearrange("p (h d) -> p h d", d=F_HD),
                                  axis=AX.X, op=ALU.add).then_inc(k.ss_done, 1)

            def rotate(t, s):
                r4 = raw[:, s, :].rearrange("p (a h d) -> p a h d", a=2, h=F_HEADS)
                c4 = part_c[:].rearrange("p (a h d) -> p a h d", a=2, h=F_HEADS)
                s4 = part_s[:].rearrange("p (a h d) -> p a h d", a=2, h=F_HEADS)
                cos = bc(tabw[:, s, 0:2, :], 2, F_HEADS)
                sin = bc(tabw[:, s, 2:4, :], 2, F_HEADS)
                wait(dve, k.tab_ready, t + 1, base)
                wait(dve, k.rot_done, t, base)
                dve.tensor_tensor(c4, r4, cos, ALU.mult).then_inc(k.rot_part, 1)
                dve.tensor_tensor(s4[:, :, :, 0:H2], r4[:, :, :, H2:], sin[:, :, :, 0:H2], ALU.mult).then_inc(k.rot_part, 1)
                dve.tensor_tensor(s4[:, :, :, H2:], r4[:, :, :, 0:H2], sin[:, :, :, H2:], ALU.mult).then_inc(k.rot_part, 1)
                wait(dve, k.rot_part, 3 * t + 3, 3 * base)
                wait(dve, k.turned, t - 1, base)
                dve.tensor_tensor(rot[:, s, :], part_c[:], part_s[:], ALU.add).then_inc(k.rot_done, 1)

            pipeline(dve, NT, [(sums, 0), (rotate, 0)])


def f_window(g, k, run):
    w = Names()
    w.units, w.hd, w.run, w.tail = NT, F_HD, run, 0
    w.prob_offset, w.zero_queries, w.scaled = HALO_F, True, True
    w.stage_incs, w.out_tiles = 3, 4
    w.wo = g.fwo
    w.out_column = lambda s: 0

    def stage(pool, u, s, qs, scs, staged):
        q = g.QT[:, :, bass.ds(u * P, P)]
        pairs = qs[:, s].rearrange("p (c b) n -> p c b n", b=2)
        wait_apart(pool, staged, 3 * u, 3 * run * NT)
        pool.tensor_copy(scs[:, s, :], g.qscale[:, u, :]).then_inc(staged, 1)
        pool.tensor_copy(pairs[0:64, :, 0, :], q[0:64]).then_inc(staged, 1)
        wait_apart(pool, staged, 3 * u + 2, 3 * run * NT)
        pool.tensor_copy(pairs[64:128, :, 1, :], q[64:128]).then_inc(staged, 1)

    def mask(dve, u, s, half, out4, in4, out, masked):
        b = g.bandmask[:, 1 if isinstance(u, int) and u == 0 else 0, :]
        dve.tensor_tensor(out4, in4, bc(bc(b, 1, 2), 1, 2), ALU.add).then_inc(masked, 1)

    def keep_turned(act, u, s, psW, ots, k, base):
        wait(act, k.projected, u, base)
        act.copy(ots[:].rearrange("p c n -> p (c n)"), psW[:]).then_inc(k.turned_kept, 1)

    def finish(dve, u, s, psW, k, base):
        wait(dve, k.projected, u + 1, base)
        dve.tensor_tensor(g.y[:, u, :], g.y[:, u, :], psW[:, 0:D], ALU.add).then_inc(k.finished, 1)

    w.stage, w.mask, w.keep_turned, w.finish = stage, mask, keep_turned, finish
    w.keys = lambda u, s, h: g.KT[:, h // 2, bass.ds(u * P, BANDK)]
    w.vals = lambda u, s, h, b: g.V[:, u + b, h * F_HD:(h + 1) * F_HD]
    return w


def f_mlp_phase(nc, prefix, g, k, run):
    base = run * NT
    with ExitStack() as ctx:
        m = Space(nc, ctx, prefix)
        ys = m.sb("ys", [P, 2, D])
        hT = m.sb("hT", [P, 2, P + 1])
        stats = m.sb("stats", [P, 2, 6])
        mv = m.sb("mv", [P, 2, 2])
        vare = m.sb("vare", [P, 1])
        rstd = m.sb("rstd", [P, 2])
        hn = m.sb("hn", [P, 2, D])
        hnT = m.sb("hnT", [P, 2, P])
        gg = m.sb("gg", [P, 2, 3, P])
        ug = m.sb("ug", [P, 2, 3, P])
        tmp = m.sb("tmp", [P, D])
        psA = m.ps("psA", [P, BANK])
        psB = m.ps("psB", [P, BANK])
        psC = m.ps("psC", [P, BANK])
        psU = m.ps("psU", [P, 2, 2, BANK])
        psF = m.ps("psF", [P, BANK])
        block = ctx.enter_context(nc.Block())

        @block.gpsimd
        def _(pool):
            def stage(t, s):
                wait_apart(pool, k.yT_done, t - 1, base)
                pool.tensor_copy(ys[:, s, :], g.y[:, t, :]).then_inc(k.y_staged, 1)

            def spread(t, s):
                wait_apart(pool, k.mv_done, t + 1, base)
                wait_apart(pool, k.rstd_done, t, base)
                pool.tensor_scalar(vare[:], mv[:, s, 1:2], EPS, None, ALU.add).then_inc(k.eps_added, 1)
                wait_apart(pool, k.eps_added, t + 1, base)
                wait_apart(pool, k.normed, t - 1, base)
                pool.tensor_tensor(rstd[:, s:s + 1], vare[:], g.mhalf[:], ALU.pow).then_inc(k.rstd_done, 1)

            pipeline(pool, NT, [(stage, 0), (spread, 0)])

        @block.tensor
        def _(pe):
            def turn_y(t, s):
                wait(pe, k.y_staged, t + 1, base)
                wait(pe, k.hT_ready, 3 * t, 3 * base)
                pe.transpose(psA[:, 0:P], ys[:, s, :], g.ident[:]).then_inc(k.yT_done, 1)

            def turn_back(t, s):
                wait(pe, k.hT_ready, 3 * t + 3, 3 * base)
                wait(pe, k.normed, t, base)
                pe.transpose(psB[:, 0:P], hT[:, s, 0:P], g.ident[:]).then_inc(k.h_back, 1)

            def turn_norm(t, s):
                wait(pe, k.normed, t + 1, base)
                wait(pe, k.hnT_ready, t, base)
                pe.transpose(psC[:, 0:P], hn[:, s, :], g.ident[:]).then_inc(k.hnT_done, 1)

            def up(t, s):
                wait(pe, k.hnT_ready, t + 1, base)
                wait(pe, k.gated, 3 * (t - 1), 3 * base)
                for j in (1, 0):
                    for c, (at, n) in enumerate(HID_CUTS):
                        last = pe.matmul(psU[0:n, s, j, c * P:(c + 1) * P], g.w1[:, HID * j + at:HID * j + at + n],
                                         hnT[:, s, :], start=True, stop=True)
                last.then_inc(k.up_done, 1)

            def down(t, s):
                wait(pe, k.gated, 3 * t + 3, 3 * base)
                wait(pe, k.b2_added, t, base)
                for c, (at, n) in enumerate(HID_CUTS):
                    last = pe.matmul(psF[:, 0:D], ug[0:n, s, c, :], g.w2[0:n, c, :], start=c == 0, stop=c == 2)
                last.then_inc(k.down_done, 1)

            pipeline(pe, NT, [(turn_y, 0), (down, 3), (turn_back, 0), (up, 2), (turn_norm, 1)])

        @block.scalar
        def _(act):
            def take_y(t, s):
                wait(act, k.yT_done, t + 1, base)
                wait(act, k.h_back, t - 1, base)
                shifted_copy(act, hT, psA, s, t, g.zcol, k.hT_ready, base)

            def take_norm(t, s):
                wait(act, k.hnT_done, t + 1, base)
                wait(act, k.up_done, t - 1, base)
                act.activation(hnT[:, s, :], psC[:, 0:P], ACT.Identity, bias=g.lnc[:, 1:2], scale=g.lnc[:, 0:1])\
                   .then_inc(k.hnT_ready, 1)

            def gelu(t, s):
                wait(act, k.up_done, t + 1, base)
                wait(act, k.gated, 3 * (t - 1), 3 * base)
                for c, (at, n) in enumerate(HID_CUTS):
                    act.activation(gg[0:n, s, c, :], psU[0:n, s, 1, c * P:(c + 1) * P], ACT.Gelu,
                                   bias=g.b1[0:n, 3 + c:4 + c]).then_inc(k.gelued, 1)

            pipeline(act, NT, [(take_y, 0), (gelu, 2), (take_norm, 1)])

        @block.vector
        def _(dve):
            def stats_of(t, s):
                wait(dve, k.h_back, t + 1, base)
                dve.bn_stats(stats[:, s, :], psB[:, 0:P]).then_inc(k.stats_done, 1)
                wait_apart(dve, k.stats_done, t + 1, base)
                dve.bn_aggr(mv[:, s, :], stats[:, s, :]).then_inc(k.mv_done, 1)

            def normalise(t, s):
                wait(dve, k.rstd_done, t + 1, base)
                wait(dve, k.hnT_done, t - 1, base)
                dve.tensor_scalar(hn[:, s, :], psB[:, 0:P], mv[:, s, 0:1], rstd[:, s:s + 1], ALU.subtract, ALU.mult)\
                   .then_inc(k.normed, 1)

            def gates(t, s):
                wait(dve, k.gelued, 3 * t + 3, 3 * base)
                wait(dve, k.down_done, t - 1, base)
                for c, (at, n) in enumerate(HID_CUTS):
                    dve.scalar_tensor_tensor(ug[0:n, s, c, :], psU[0:n, s, 0, c * P:(c + 1) * P],
                                             g.b1[0:n, c:c + 1], gg[0:n, s, c, :], ALU.add, ALU.mult)\
                       .then_inc(k.gated, 1)

            def finish(t, s):
                wait(dve, k.down_done, t + 1, base)
                wait(dve, k.added, t, base)
                dve.tensor_tensor(tmp[:], psF[:, 0:D], g.b2[:], ALU.add).then_inc(k.b2_added, 1)
                wait(dve, k.b2_added, t + 1, base)
                dve.tensor_tensor(g.y[:, t, :], g.y[:, t, :], tmp[:], ALU.add).then_inc(k.added, 1)

            pipeline(dve, NT, [(stats_of, 0), (finish, 3), (gates, 2), (normalise, 0)])


def ffn(nc, g, dram, app, k):
    with ExitStack() as ctx:
        m = Space(nc, ctx, f"f{app}")
        g.y = m.sb("y", [P, NT, D])
        g.V = m.sb("V", [P, NT + 1, F_INNER])
        g.QT = m.sb("QT", [P, 4, S])
        g.KT = m.sb("KT", [P, 4, HALO_F + S])
        g.qscale = m.sb("qscale", [P, NT, F_HEADS])
        g.wqkv = m.sb("wqkv", [P, 3 * F_INNER])
        g.fwo = m.sb("fwo", [P, 4, D])
        g.w1 = m.sb("w1", [P, 2 * HID])
        g.w2 = m.sb("w2", [P, 3, D])
        g.b1 = m.sb("b1", [P, 6])
        g.b2 = m.sb("b2", [P, D])
        g.lnc = m.sb("lnc", [P, 2])
        g.sc4 = m.sb("sc4", [P, 4, F_HD])
        norm_phase(nc, f"f{app}n", g.x, g.y, g)
        with nc.Fori(0, F_DEPTH) as layer:
            run = layer + app * F_DEPTH
            f_load_phase(nc, g, dram, layer, k.loaded, run)
            f_qkv_phase(nc, f"f{app}q", g, k.qkv, run)
            band_phase(nc, f"f{app}b", g, f_window(g, k.band, run), k.band, run * NT)
            f_mlp_phase(nc, f"f{app}m", g, k.mlp, run)
        add_phase(nc, f"f{app}x", g.x, g.y)


class GroupSems:

    def __init__(self, sem):
        self.k_done = sem("k_done")
        self.kh_done = sem("kh_done")
        self.kl_done = sem("kl_done")
        self.v_staged = sem("v_staged")
        self.v_done = sem("v_done")
        self.v_kept = sem("v_kept")
        self.q_done = sem("q_done")
        self.q_kept = sem("q_kept")
        self.q_taken = sem("q_taken")
        self.q_hi = sem("q_hi")
        self.q_top = sem("q_top")
        self.q_staged = sem("q_staged")
        self.scored = sem("scored")
        self.maxed = sem("maxed")
        self.biased = sem("biased")
        self.exped = sem("exped")
        self.transposed = sem("transposed")
        self.evac_act = sem("evac_act")
        self.evac_dve = sem("evac_dve")
        self.weighed = sem("weighed")
        self.summed = sem("summed")
        self.recip = sem("recip")
        self.normed = sem("normed")
        self.o_staged = sem("o_staged")
        self.o_turned = sem("o_turned")
        self.o_kept = sem("o_kept")
        self.projected = sem("projected")
        self.added = sem("added")


def attention_b(nc, g, dram):
    with ExitStack() as ctx:
        m = Space(nc, ctx, "b")
        y = m.sb("y", [P, NT, D])
        yT = m.sb("yT", [P, S])
        norm_phase(nc, "bn", g.x, y, g, (yT, None, None, 0))
        add_phase(nc, "bx", g.x, y)
        U = NT * B_HPG
        wk = m.sb("wk", [P, 2, B_HD])
        wv = m.sb("wv", [P, B_HD])
        wq = m.sb("wq", [P, B_HPG, 2, B_HD])
        wp = m.sb("wp", [P, 2, D])
        kh = m.sb("kh", [P, S], F32R)
        kl = m.sb("kl", [P, S], F32R)
        v = m.sb("v", [P, NT, B_HD])
        qd = m.sb("qd", [P, U, P])
        o = m.sb("o", [P, U, B_HD])
        loaded = m.sem("loaded")
        k = GroupSems(sem_maker(nc, "bk"))

        with nc.Fori(0, B_GROUPS) as grp:
            b_group_prepare(nc, g, dram, k, grp, loaded, wk, wv, wq, wp, yT, kh, kl, v, qd)
            b_group_attend(nc, g, k, grp, kh, kl, v, qd, o)
            b_group_project(nc, g, k, grp, wp, o)


def b_group_prepare(nc, g, dram, k, grp, loaded, wk, wv, wq, wp, yT, kh, kl, v, qd):
    NC = S // BANK
    with ExitStack() as ctx:
        m = Space(nc, ctx, "bp")
        yts = m.sb("yts", [P, 2, P])
        psK = m.ps("psK", [P, 2, BANK])
        psV = m.ps("psV", [P, 2, BANK])
        psQ = m.ps("psQ", [P, 2, BANK])
        block = ctx.enter_context(nc.Block())
        kv_cols, q_cols = bass.ds(grp * B_HD, B_HD), bass.ds(grp * (B_HPG * B_HD), B_HPG * B_HD)
        loads = [(wk[:, i, :], dram["Wk"][:, kv_cols]) for i in range(2)] + [(wv[:], dram["Wv"][:, kv_cols])]
        loads += [(wq[:, :, i, :], dram["Wq"][:, q_cols].rearrange("p (h e) -> p h e", h=B_HPG)) for i in range(2)]
        loads += [(wp[:], dram["Wpost"][q_cols, :].rearrange("(c p) n -> p c n", p=P))]
        n_loaded = 16 * len(loads)

        @block.sync
        def _(sp):
            for dst, src in loads:
                sp.dma_start(dst, src).then_inc(loaded, 16)

        @block.gpsimd
        def _(pool):
            base = grp * NT

            def stage(t, s):
                wait_apart(pool, k.v_done, t - 1, base)
                pool.tensor_copy(yts[:, s, :], yT[:, bass.ds(t * P, P)]).then_inc(k.v_staged, 1)

            pipeline(pool, NT, [(stage, 0)])

        @block.tensor
        def _(pe):
            pe.wait_ge(loaded, grp * n_loaded + n_loaded)
            for c in range(NC):
                wait(pe, k.kl_done, c - 1, grp * NC)
                pe.matmul(psK[:, c % 2, :], wk[:], yT[:, c * BANK:(c + 1) * BANK], start=True, stop=True).then_inc(k.k_done, 1)

            def value(t, s):
                wait(pe, k.v_staged, t + 1, grp * NT)
                wait(pe, k.v_kept, t - 1, grp * NT)
                pe.matmul(psV[:, s, 0:B_HD], yts[:, s, :], wv[:], start=True, stop=True).then_inc(k.v_done, 1)

            pipeline(pe, NT, [(value, 0)])
            for n in range(B_HPG * NC):
                h, c = n // NC, n % NC
                wait(pe, k.q_kept, n - 1, grp * (B_HPG * NC))
                pe.matmul(psQ[:, n % 2, :], wq[:, h], yT[:, c * BANK:(c + 1) * BANK], start=True, stop=True)\
                  .then_inc(k.q_done, 1)

        @block.scalar
        def _(act):
            for c in range(NC):
                act.wait_ge(k.k_done, grp * NC + c + 1)
                act.copy(kh[:, c * BANK:(c + 1) * BANK], psK[:, c % 2, :]).then_inc(k.kh_done, 1)
            q5 = qd[:].rearrange("p (t h) n -> p t h n", h=B_HPG)
            for n in range(B_HPG * NC):
                h, c = n // NC, n % NC
                act.wait_ge(k.q_done, grp * (B_HPG * NC) + n + 1)
                act.activation(q5[:, c * 4:(c + 1) * 4, h, :], psQ[:, n % 2, :].rearrange("p (t n) -> p t n", t=4),
                               ACT.Copy, scale=1.0 / math.sqrt(B_HD)).then_inc(k.q_kept, 1)

        @block.vector
        def _(dve):
            for c in range(NC):
                cut = slice(c * BANK, (c + 1) * BANK)
                dve.wait_ge(k.kh_done, grp * NC + c + 1)
                dve.tensor_tensor(kl[:, cut], psK[:, c % 2, :], kh[:, cut].bitcast(F32), ALU.subtract).then_inc(k.kl_done, 1)

            def value(t, s):
                wait(dve, k.v_done, t + 1, grp * NT)
                dve.tensor_copy(v[:, t, :], psV[:, s, 0:B_HD]).then_inc(k.v_kept, 1)

            pipeline(dve, NT, [(value, 0)])


def b_group_attend(nc, g, k, grp, kh, kl, v, qd, o):
    with ExitStack() as ctx:
        m = Space(nc, ctx, "bt")
        U = NT * B_HPG
        qf = m.sb("qf", [P, 2, P])
        qh = m.sb("qh", [P, 2, P], F32R)
        qs = m.sb("qs", [P, 2, P], F32R)
        mx = m.sb("mx", [P, 2, 4])
        nb = m.sb("nb", [P, 2])
        probs = m.sb("probs", [P, 2, S])
        sums = m.sb("sums", [P, 2, 2])
        sm = m.sb("sm", [P, 2])
        rs = m.sb("rs", [P, 2])
        pts = m.sb("pts", [P, 4, BANK])
        psS = m.ps("psS", [P, 4, BANK])
        psT = m.ps("psT", [P, 2, BANK])
        psO = m.ps("psO", [P, 2, BANK])
        block = ctx.enter_context(nc.Block())
        base = grp * U
        HI = slice(B_HD, P)

        @block.gpsimd
        def _(pool):
            def stage(u, s):
                wait_apart(pool, k.scored, 4 * (u - 1), 4 * base)
                wait_apart(pool, k.q_staged, u, base)
                pool.tensor_copy(qf[:, s, :], qd[:, u, :]).then_inc(k.q_taken, 1)
                wait_apart(pool, k.q_taken, u + 1, base)
                pool.tensor_copy(qh[HI, s, :], qf[HI, s, :]).then_inc(k.q_hi, 1)
                wait_apart(pool, k.q_hi, u + 1, base)
                pool.tensor_copy(qs[0:B_HD, s, :], qf[0:B_HD, s, :]).then_inc(k.q_top, 1)
                pool.tensor_tensor(qs[HI, s, :], qf[HI, s, :], qh[HI, s, :].bitcast(F32), ALU.subtract)\
                    .then_inc(k.q_staged, 1)

            pipeline(pool, U, [(stage, 0)])

        @block.tensor
        def _(pe):
            def score(u, s, c):
                cut = slice(c * BANK, (c + 1) * BANK)
                if c == 0:
                    wait(pe, k.q_staged, u + 1, base)
                    wait(pe, k.q_top, u + 1, base)
                wait(pe, k.exped, 2 * (u - 1) + c // 2 + 1, 2 * base)
                pe.matmul(psS[:, c, :], qs[:, s, :], kh[:, cut], start=True, stop=False)
                pe.matmul(psS[:, c, :], qs[:, s, :], kl[:, cut], start=False, stop=True).then_inc(k.scored, 1)

            def turn(u, s, q):
                wait(pe, k.exped, 2 * u + q // 2 + 1, 2 * base)
                wait(pe, (k.evac_act, k.evac_dve)[q % 2], 2 * u + q // 2, 2 * base)
                for j in range(4):
                    last = pe.transpose(psT[:, q % 2, j * P:(j + 1) * P], probs[:, s, (4 * q + j) * P:(4 * q + j + 1) * P],
                                        g.ident[:])
                last.then_inc(k.transposed, 1)

            def weigh(u, s, q):
                wait(pe, (k.evac_act, k.evac_dve)[q % 2], 2 * u + q // 2 + 1, 2 * base)
                if q == 0:
                    wait(pe, k.normed, u - 1, base)
                for j in range(4):
                    last = pe.matmul(psO[:, s, 0:B_HD], pts[:, q, j * P:(j + 1) * P], v[:, 4 * q + j, :],
                                     start=q == 0 and j == 0, stop=q == 3 and j == 3)
                last.then_inc(k.weighed, 1)

            def T(q):
                return lambda u, s: turn(u, s, q), 2

            def W(q):
                return lambda u, s: weigh(u, s, q), 2

            def C(c):
                return lambda u, s: score(u, s, c), 0

            stages = [T(0), T(1), W(0), T(2), W(1), C(0), C(1), T(3), W(2), C(2), C(3), W(3)]
            pipeline(pe, U, stages)

        @block.vector
        def _(dve):
            def top(u, s, c):
                wait(dve, k.scored, 4 * u + c + 1, 4 * base)
                if c == 0:
                    wait(dve, k.biased, u - 1, base)
                dve.tensor_reduce(mx[:, s, c:c + 1], psS[:, c, :], axis=AX.X, op=ALU.max).then_inc(k.maxed, 1)

            def bias(u, s):
                wait(dve, k.maxed, 4 * u + 4, 4 * base)
                wait(dve, k.exped, 2 * (u - 1), 2 * base)
                dve.tensor_reduce(nb[:, s:s + 1], mx[:, s, :], axis=AX.X, op=ALU.max, negate=True).then_inc(k.biased, 1)

            def evac(u, s, q):
                wait(dve, k.transposed, 4 * u + q + 1, 4 * base)
                wait(dve, k.weighed, 4 * (u - 1) + q + 1, 4 * base)
                dve.tensor_copy(pts[:, q, :], psT[:, 1, :]).then_inc(k.evac_dve, 1)

            def norm(u, s):
                wait(dve, k.exped, 2 * u + 2, 2 * base)
                dve.tensor_tensor(sm[:, s:s + 1], sums[:, s, 0:1], sums[:, s, 1:2], ALU.add).then_inc(k.summed, 1)
                wait(dve, k.summed, u + 1, base)
                dve.reciprocal(rs[:, s:s + 1], sm[:, s:s + 1]).then_inc(k.recip, 1)
                wait(dve, k.recip, u + 1, base)
                wait(dve, k.weighed, 4 * u + 4, 4 * base)
                dve.tensor_scalar(o[:, u, :], psO[:, s, 0:B_HD], rs[:, s:s + 1], None, ALU.mult).then_inc(k.normed, 1)

            pipeline(dve, U, [(lambda u, s: evac(u, s, 1), 2),
                              (lambda u, s: top(u, s, 0), 0), (lambda u, s: top(u, s, 1), 0),
                              (lambda u, s: evac(u, s, 3), 2),
                              (lambda u, s: top(u, s, 2), 0), (lambda u, s: top(u, s, 3), 0),
                              (bias, 0), (norm, 2)])

        @block.scalar
        def _(act):
            def exp(u, s, c):
                if c == 0:
                    wait(act, k.biased, u + 1, base)
                    wait(act, k.transposed, 4 * (u - 1), 4 * base)
                    wait(act, k.summed, u - 1, base)
                act.activation(probs[:, s, c * 2 * BANK:(c + 1) * 2 * BANK].rearrange("p (b n) -> p b n", b=2),
                               psS[:, 2 * c:2 * c + 2, :], ACT.Exp, bias=nb[:, s:s + 1],
                               accum_out=sums[:, s, c:c + 1]).then_inc(k.exped, 1)

            def evac(u, s, q):
                wait(act, k.transposed, 4 * u + q + 1, 4 * base)
                wait(act, k.weighed, 4 * (u - 1) + q + 1, 4 * base)
                act.copy(pts[:, q, :], psT[:, 0, :]).then_inc(k.evac_act, 1)

            pipeline(act, U, [(lambda u, s: evac(u, s, 0), 2), (lambda u, s: exp(u, s, 0), 1),
                              (lambda u, s: exp(u, s, 1), 1), (lambda u, s: evac(u, s, 2), 2)])


def b_group_project(nc, g, k, grp, wp, o):
    with ExitStack() as ctx:
        m = Space(nc, ctx, "bo")
        os_ = m.sb("os", [P, 2, 2, P])
        ot = m.sb("ot", [P, 2, 2, P])
        psT = m.ps("psT", [P, 2, BANK])
        psY = m.ps("psY", [P, 2, BANK])
        block = ctx.enter_context(nc.Block())
        base = grp * NT

        @block.gpsimd
        def _(pool):
            def stage(t, s):
                wait_apart(pool, k.o_turned, t - 1, base)
                pool.tensor_copy(os_[:, s].rearrange("p a n -> p (a n)"),
                                 o[:, bass.ds(t * B_HPG, B_HPG), :].rearrange("p h e -> p (h e)")).then_inc(k.o_staged, 1)

            pipeline(pool, NT, [(stage, 0)])

        @block.tensor
        def _(pe):
            def turn(t, s):
                wait(pe, k.o_staged, t + 1, base)
                wait(pe, k.o_kept, t - 1, base)
                for j in range(2):
                    last = pe.transpose(psT[:, s, j * P:(j + 1) * P], os_[:, s, j, :], g.ident[:])
                last.then_inc(k.o_turned, 1)

            def project(t, s):
                wait(pe, k.o_kept, t + 1, base)
                wait(pe, k.added, t - 1, base)
                for j in range(2):
                    last = pe.matmul(psY[:, s, 0:D], ot[:, s, j, :], wp[:, j, :], start=j == 0, stop=j == 1)
                last.then_inc(k.projected, 1)

            pipeline(pe, NT, [(turn, 0), (project, 1)])

        @block.scalar
        def _(act):
            def keep(t, s):
                wait(act, k.o_turned, t + 1, base)
                wait(act, k.projected, t - 1, base)
                act.copy(ot[:, s].rearrange("p a n -> p (a n)"), psT[:, s, 0:2 * P]).then_inc(k.o_kept, 1)

            pipeline(act, NT, [(keep, 0)])

        @block.vector
        def _(dve):
            def add(t, s):
                wait(dve, k.projected, t + 1, base)
                dve.tensor_tensor(g.x[:, t, :], g.x[:, t, :], psY[:, s, 0:D], ALU.add).then_inc(k.added, 1)

            pipeline(dve, NT, [(add, 0)])


def store_phase(nc, g, out):
    with nc.semaphore("stored") as stored, nc.Block() as block:
        @block.sync
        def _(sp):
            sp.dma_start(out[0].rearrange("(t p) d -> p t d", p=P), g.x[:]).then_inc(stored, 16)
            sp.wait_ge(stored, 16)


def build(nc, dram, out, parts="afbf"):
    g = Names()
    with ExitStack() as ctx:
        LAUNCH.ctx = ctx
        m = Space(nc, ctx, "g")
        g.x = m.sb("x", [P, NT, D])
        g.ident = m.sb("ident", [P, P])
        g.zcol = m.sb("zcol", [P, 1])
        g.mhalf = m.sb("mhalf", [P, 1])
        g.tab = m.sb("tab", [P, NT, 4, F_HD])
        g.bandmask = m.sb("bandmask", [P, 2, BANDK])
        LAUNCH.marks, LAUNCH.constants_made = m.sem("marks"), m.sem("constants_made")
        LAUNCH.norm = NormSems(sem_maker(nc, "n"))
        LAUNCH.norm.runs = LAUNCH.norm.runs_T = 0
        load_phase(nc, g, dram)
        if "a" in parts:
            attention_a(nc, g, dram)
        k = Names()
        k.loaded = m.sem("f_loaded")
        k.qkv, k.band, k.mlp = (QkvSems(sem_maker(nc, "fq")), BandSems(sem_maker(nc, "fb")),
                                MlpSems(sem_maker(nc, "fm")))
        if "f" in parts:
            ffn(nc, g, dram, 0, k)
        if "b" in parts:
            attention_b(nc, g, dram)
        if parts.count("f") > 1:
            ffn(nc, g, dram, 1, k)
        store_phase(nc, g, out)


_A = "L0_attn_a_"
_NAMES = {"x": _A + "x", "wq_lin": _A + "wq_lin", "bq_lin": _A + "bq_lin", "wk_lin": _A + "wk_lin",
          "bk_lin": _A + "bk_lin", "wv_lin": _A + "wv_lin", "bv_lin": _A + "bv_lin", "wq_loc": _A + "wq_loc",
          "bq_loc": _A + "bq_loc", "wk_loc": _A + "wk_loc", "bk_loc": _A + "bk_loc", "wv_loc": _A + "wv_loc",
          "bv_loc": _A + "bv_loc", "wo": _A + "wo", "bo": _A + "bo", "wg1": _A + "wg1", "bg1": _A + "bg1",
          "wg2": _A + "wg2", "bg2": _A + "bg2", "ln_g": _A + "ln_g", "ln_b": _A + "ln_b",
          "Wq": "L0_attn_b_Wq", "Wk": "L0_attn_b_Wk", "Wv": "L0_attn_b_Wv", "Wpost": "L0_attn_b_Wpost",
          "wqkv": "L0_ffn_wqkv", "q_scale": "L0_ffn_q_scale", "k_scale": "L0_ffn_k_scale", "fwo": "L0_ffn_wo",
          "fln_g": "L0_ffn_ln_g", "fln_b": "L0_ffn_ln_b", "w1": "L0_ffn_w1", "b1": "L0_ffn_b1",
          "w2": "L0_ffn_w2", "b2": "L0_ffn_b2"}


def constants():
    f = np.float32
    half = np.arange(0, F_HD, 2, dtype=f)
    inv = (f(1.0) / np.power(f(10000.0), half / f(F_HD))).astype(f)
    t = np.arange(S, dtype=f)
    fr = (t[:, None] * inv[None, :]).astype(f)
    b = ((half + f(0.4 * F_HD)) / f(1.4 * F_HD)).astype(f)
    scale = np.power(b[None, :], ((t - S // 2) / f(32.0)).astype(f)[:, None]).astype(f)
    cos, sin = np.cos(fr).astype(f), np.sin(fr).astype(f)
    tab = np.zeros((S, 4, F_HD), f)
    for j, sc in enumerate((scale, f(1.0) / scale)):
        gain = f((8.0, 1.0)[j])
        tab[:, j] = gain * np.concatenate([cos * sc, cos * sc], 1)
        tab[:, 2 + j] = gain * np.concatenate([-sin * sc, sin * sc], 1)
    r, c = np.arange(P)[:, None], np.arange(BANDK)[None, :]
    band = np.where((c >= r) & (c <= r + HALO_F), 0.0, NEG).astype(f)
    band0 = np.where(c >= HALO_F, band, f(NEG)).astype(f)
    edge = np.zeros((P, 2, BANDK), f)
    edge[:, 0, :HALO_A] = NEG
    edge[:, 1, HALO_A + P:] = NEG
    hmask = (np.arange(D)[:, None] // A_HD == np.arange(A_HEADS)[None, :]).astype(f)
    return {"tables": tab, "bandmask": np.stack([band, band0], 1), "edge": edge, "hmask": hmask}


def band_of(rel_bias):
    r, c = np.arange(P)[:, None], np.arange(BANDK)[None, :]
    inside = (c >= r) & (c <= r + 2 * HALO_A)
    at = np.where(inside, c - r + HALO_A, 0)
    rows = rel_bias[at]
    return np.ascontiguousarray(np.where(inside[:, :, None], rows, np.float32(NEG)).transpose(0, 2, 1))


def kernel(**inputs):
    import concourse.bacc as _bacc
    from concourse.bass_utils import run_bass_kernel_spmd as _run

    arrays = {n: np.ascontiguousarray(inputs[full]) for n, full in _NAMES.items()}
    arrays["relb"] = band_of(np.asarray(inputs[_A + "rel_bias"]))
    arrays.update({n: np.ascontiguousarray(a) for n, a in constants().items()})
    nc = _bacc.Bacc("TRN2", target_bir_lowering=False, num_devices=1)
    dram = {n: nc.dram_tensor(f"in_{n}", a.shape, F32, kind="ExternalInput").ap() for n, a in arrays.items()}
    shape = (1, S, D)
    out = nc.dram_tensor("out_x", shape, F32, kind="ExternalOutput").ap()
    build(nc, dram, out)
    r = _run(nc, [{f"in_{n}": a for n, a in arrays.items()}], core_ids=[0])
    return r.results[0]["out_x"]
```

```python
import math
from contextlib import ExitStack

import concourse.bass as bass
import numpy as np
from concourse import mybir

F32 = mybir.dt.float32
F32R = mybir.dt.float32r
ACT = mybir.ActivationFunctionType
ALU = mybir.AluOpType
AX = mybir.AxisListType

P = 128
D = 128
S = 2048
NT = S // P
BANK = 512
BANDK = 192
HALO_A, HALO_F = 32, 64
NEG = -1.0e30

A_HEADS, A_HD = 16, 8
F_HEADS, F_HD, F_INNER, F_DEPTH = 8, 64, 512, 2
HID = int(D * 4 * 2 / 3)
HID_CUTS = [(0, 128), (128, 128), (256, HID - 256)]
B_GROUPS, B_HPG, B_HD = 4, 4, 64
EXPS = 4
EPS = 1e-5


def wait(eng, sem, n, base=0):
    if isinstance(n, int) and n <= 0:
        return
    eng.wait_ge(sem, n + base)


def wait_apart(eng, sem, n, base=0):
    if isinstance(n, int) and n <= 0:
        return
    eng.wait_ge(sem, n + base)
    if not isinstance(n + base, int):
        eng.sem_inc(LAUNCH.marks, 1)


def pipeline(eng, count, stages, tail=0, unroll=2):
    span = max(lag for _, lag in stages)
    first = min(count, (span + 2 * unroll - 1) // unroll * unroll)
    last = max(first, count - tail)

    def step(i):
        for stage, lag in stages:
            if 0 <= i - lag < count:
                stage(i - lag, (i - lag) % unroll)

    for i in range(first):
        step(i)
    if first < last:
        with eng.Fori(first // unroll, last // unroll) as turn:
            for k in range(unroll):
                for stage, lag in stages:
                    stage(turn * unroll + (k - lag), (k - lag) % unroll)
    for i in range(last, count + span):
        step(i)


class Names:
    pass


LAUNCH = Names()


class Space:

    def __init__(self, nc, ctx, prefix):
        self.nc, self.ctx, self.prefix = nc, ctx, prefix

    def sb(self, name, shape, dt=F32):
        return self.ctx.enter_context(self.nc.sbuf_tensor(f"{self.prefix}_{name}", shape, dt))

    def ps(self, name, shape):
        return self.ctx.enter_context(self.nc.psum_tensor(f"{self.prefix}_{name}", shape, F32))

    def sem(self, name):
        return LAUNCH.ctx.enter_context(self.nc.semaphore(f"{self.prefix}_{name}"))


def sem_maker(nc, prefix):
    return lambda name: LAUNCH.ctx.enter_context(nc.semaphore(f"{prefix}_{name}"))


def bc(ap, axis, n):
    ap = ap.unsqueeze(axis)
    shape = list(ap.shape)
    shape[axis] = n
    return ap.broadcast_to(shape)


def load_phase(nc, g, dram):
    with ExitStack() as ctx:
        sp_ = Space(nc, ctx, "load")
        loaded, zeroed = sp_.sem("loaded"), sp_.sem("zeroed")
        block = ctx.enter_context(nc.Block())
        loads = [(g.x[:], dram["x"][0].rearrange("(t p) d -> p t d", p=P)),
                 (g.tab[:], dram["tables"].rearrange("(t p) a d -> p t a d", p=P)),
                 (g.bandmask[:], dram["bandmask"])]

        @block.sync
        def _(sp):
            for dst, src in loads:
                sp.dma_start(dst, src).then_inc(loaded, 16)
            sp.wait_ge(loaded, 16 * len(loads))

        @block.gpsimd
        def _(pool):
            pool.memset(g.ident[:], 0.0).then_inc(zeroed, 1)
            pool.memset(g.zcol[:], 0.0)
            pool.memset(g.mhalf[:], -0.5)
            pool.wait_ge(zeroed, 1)
            pool.affine_select(out=g.ident[:], in_=g.ident[:], compare_op=ALU.not_equal, fill=1.0, base=0,
                               pattern=[[-1, P]], channel_multiplier=1).then_inc(LAUNCH.constants_made, 1)


class NormSems:

    def __init__(self, sem):
        self.meaned = sem("meaned")
        self.negated = sem("negated")
        self.centred = sem("centred")
        self.squared = sem("squared")
        self.varied = sem("varied")
        self.eps_added = sem("eps_added")
        self.rstd_done = sem("rstd_done")
        self.normed = sem("normed")
        self.transposed = sem("transposed")
        self.evacuated = sem("evacuated")


def norm_phase(nc, prefix, src, dst, g, affine_T=None):
    with ExitStack() as ctx:
        m = Space(nc, ctx, prefix)
        sums = m.sb("sums", [P, NT])
        negmean = m.sb("negmean", [P, NT])
        var = m.sb("var", [P, NT])
        rstd = m.sb("rstd", [P, NT])
        sq = m.sb("sq", [P, NT, D])
        psT = m.ps("psT", [P, 4, BANK])
        k = LAUNCH.norm
        NC = NT // 4
        base, base_T = k.runs * NC, k.runs_T * NC
        k.runs += 1
        k.runs_T += affine_T is not None
        block = ctx.enter_context(nc.Block())

        @block.vector
        def _(dve):
            for c in range(NC):
                cut = slice(4 * c, 4 * c + 4)
                dve.tensor_reduce(sums[:, cut], src[:, cut, :], axis=AX.X, op=ALU.add).then_inc(k.meaned, 1)
                wait(dve, k.meaned, c + 1, base)
                dve.tensor_scalar(negmean[:, cut], sums[:, cut], -1.0 / D, None, ALU.mult).then_inc(k.negated, 1)
                wait(dve, k.negated, c + 1, base)
                dve.tensor_tensor(dst[:, cut, :], src[:, cut, :], bc(negmean[:, cut], 2, D), ALU.add)\
                   .then_inc(k.centred, 1)

            for c in range(NC):
                cut = slice(4 * c, 4 * c + 4)
                wait(dve, k.squared, c + 1, base)
                dve.tensor_reduce(var[:, cut], sq[:, cut, :], axis=AX.X, op=ALU.add).then_inc(k.varied, 1)
            for c in range(NC):
                cut = slice(4 * c, 4 * c + 4)
                wait(dve, k.rstd_done, c + 1, base)
                dve.tensor_tensor(dst[:, cut, :], dst[:, cut, :], bc(rstd[:, cut], 2, D), ALU.mult)\
                   .then_inc(k.normed, 1)

        @block.gpsimd
        def _(pool):
            for c in range(NC):
                cut = slice(4 * c, 4 * c + 4)
                wait(pool, k.varied, c + 1, base)
                pool.tensor_scalar(var[:, cut], var[:, cut], 1.0 / D, EPS, ALU.mult, ALU.add).then_inc(k.eps_added, 1)
                wait(pool, k.eps_added, c + 1, base)
                pool.tensor_tensor(rstd[:, cut], var[:, cut], bc(g.mhalf[:, 0], 1, 4), ALU.pow).then_inc(k.rstd_done, 1)

        if affine_T is not None:
            out, scale, shift, pad = affine_T

            @block.tensor
            def _(pe):
                for c in range(NC):
                    wait(pe, k.normed, c + 1, base)
                    for j in range(4):
                        last = pe.transpose(psT[:, c, j * P:(j + 1) * P], dst[:, 4 * c + j, :], g.ident[:])
                    last.then_inc(k.transposed, 1)

        @block.scalar
        def _(act):
            for c in range(NC):
                cut = slice(4 * c, 4 * c + 4)
                wait(act, k.centred, c + 1, base)
                act.activation(sq[:, cut, :], dst[:, cut, :], ACT.Square).then_inc(k.squared, 1)
            if affine_T is None:
                return
            for c in range(NC):
                wait(act, k.transposed, c + 1, base_T)
                place = out[:, c * BANK + pad:(c + 1) * BANK + pad]
                if scale is None:
                    act.copy(place, psT[:, c, :]).then_inc(k.evacuated, 1)
                else:
                    act.activation(place, psT[:, c, :], ACT.Identity, bias=shift, scale=scale)\
                       .then_inc(k.evacuated, 1)


def add_phase(nc, prefix, x, y):
    with ExitStack() as ctx:
        block = ctx.enter_context(nc.Block())
        half = NT * 3 // 4

        @block.vector
        def _(dve):
            dve.tensor_tensor(x[:, 0:half, :], x[:, 0:half, :], y[:, 0:half, :], ALU.add)

        @block.gpsimd
        def _(pool):
            pool.tensor_tensor(x[:, half:NT, :], x[:, half:NT, :], y[:, half:NT, :], ALU.add)


def band_phase(nc, prefix, g, w, sems, base):
    with ExitStack() as ctx:
        m = Space(nc, ctx, prefix)
        U, hd = w.units, w.hd
        qs = m.sb("qs", [P, 2, 8, P])
        masked = m.sb("masked", [P, 2, 8, BANDK])
        mx = m.sb("mx", [P, 2, 8])
        nb = m.sb("nb", [P, 2, 8])
        scs = m.sb("scs", [P, 2, 8])
        probs = m.sb("probs", [P, 2, 8, 2 * P])
        sums = m.sb("sums", [P, 2, 8])
        rs = m.sb("rs", [P, 2, 8])
        pts = m.sb("pts", [P, 4, BANK])
        on_width = max(P, 8 * hd)
        on = m.sb("on", [P, 2, on_width])
        ots = m.sb("ots", [P, 4, P])
        psS = m.ps("psS", [P, 4, BANK])
        psT = m.ps("psT", [P, 2, BANK])
        psO = m.ps("psO", [P, BANK])
        psW = m.ps("psW", [P, BANK])
        k = sems
        off = w.prob_offset
        block = ctx.enter_context(nc.Block())

        def S_of(h):
            return psS[:, h // 2, (h % 2) * BANDK:(h % 2 + 1) * BANDK]

        @block.gpsimd
        def _(pool):
            if w.zero_queries:
                pool.memset(qs[:], 0.0).then_inc(k.qs_zeroed, 1)
                wait_apart(pool, k.qs_zeroed, 1, w.run)

            def stage(u, s):
                wait_apart(pool, k.scored, 2 * (u - 1), 2 * base)
                wait_apart(pool, k.exped, 4 * (u - 1), 4 * base)
                w.stage(pool, u, s, qs, scs, k.staged)

            pipeline(pool, U, [(stage, 0)])

        @block.tensor
        def _(pe):
            def score(u, s, half):
                wait(pe, k.staged, w.stage_incs * (u + 1), w.stage_incs * base)
                wait(pe, k.masked, 2 * (u - 1) + half + 1, 2 * base)
                for h in range(4 * half, 4 * half + 4):
                    last = pe.matmul(S_of(h), qs[:, s, h, :], w.keys(u, s, h), start=True, stop=True)
                last.then_inc(k.scored, 1)

            def turn(u, s, q):
                wait(pe, k.exped, 4 * u + q + 1, 4 * base)
                wait(pe, (k.evac_act, k.evac_dve)[q % 2], 2 * u + q // 2, 2 * base)
                for j in range(4):
                    h, b = 2 * q + j // 2, j % 2
                    last = pe.transpose(psT[:, q % 2, j * P:(j + 1) * P],
                                        probs[:, s, h, b * P:(b + 1) * P], g.ident[:])
                last.then_inc(k.transposed, 1)

            def weigh(u, s, q):
                wait(pe, (k.evac_act, k.evac_dve)[q % 2], 2 * u + q // 2 + 1, 2 * base)
                if q == 0:
                    wait(pe, k.normed, u, base)
                for h in (2 * q, 2 * q + 1):
                    for b in range(2):
                        last = pe.matmul(psO[:, h * hd:(h + 1) * hd],
                                         pts[:, q, ((h % 2) * 2 + b) * P:((h % 2) * 2 + b + 1) * P],
                                         w.vals(u, s, h, b), start=b == 0, stop=b == 1)
                last.then_inc(k.weighed, 1)

            nout = w.out_tiles

            def turn_out(u, s):
                wait(pe, k.normed, u + 1, base)
                wait(pe, k.finished, u, base)
                for j in range(nout):
                    last = pe.transpose(psW[:, j * P:(j + 1) * P], on[:, s, j * P:(j + 1) * P], g.ident[:])
                last.then_inc(k.turned, 1)

            def project(u, s):
                wait(pe, k.turned_kept, u + 1, base)
                for j in range(nout):
                    last = pe.matmul(psW[:, 0:D], ots[:, j, :], w.wo[:, j, :], start=j == 0, stop=j == nout - 1)
                last.then_inc(k.projected, 1)

            def C(half, lag):
                return lambda u, s: score(u, s, half), lag

            def T(q, lag):
                return lambda u, s: turn(u, s, q), lag

            def W(q, lag):
                return lambda u, s: weigh(u, s, q), lag

            if w.wo is None:
                order = [T(2, 3), C(0, 1), C(1, 1), (turn_out, 4), W(0, 3), T(3, 3), W(1, 3), T(0, 2),
                         W(2, 3), W(3, 3), T(1, 2)]
            else:
                order = [W(3, 3), C(0, 0), T(1, 2), (turn_out, 3), W(0, 2), T(2, 2), C(1, 0), T(3, 2),
                         W(1, 2), T(0, 1), (project, 3), W(2, 2)]
            pipeline(pe, U, order, tail=w.tail)

        @block.vector
        def _(dve):
            dve.memset(probs[:], 0.0).then_inc(k.probs_zeroed, 1)
            if on_width > 8 * hd:
                dve.memset(on[:], 0.0).then_inc(k.on_zeroed, 1)
                dve.wait_ge(k.on_zeroed, 1)

            def evac(u, s, q):
                wait(dve, k.transposed, 4 * u + q + 1, 4 * base)
                wait(dve, k.weighed, 4 * (u - 1) + q + 1, 4 * base)
                dve.tensor_copy(pts[:, q, :], psT[:, 1, :]).then_inc(k.evac_dve, 1)

            def mask(u, s, half):
                wait(dve, k.scored, 2 * u + half + 1, 2 * base)
                wait(dve, k.exped, 4 * (u - 2) + 2 * half + 2, 4 * base)
                out4 = masked[:, s, 4 * half:4 * half + 4].rearrange("p (b h) n -> p b h n", b=2)
                in4 = psS[:, 2 * half:2 * half + 2, 0:2 * BANDK].rearrange("p b (h n) -> p b h n", h=2)
                w.mask(dve, u, s, half, out4, in4, masked[:, s, 4 * half:4 * half + 4], k.masked)

            def bias(u, s, half):
                cut = slice(4 * half, 4 * half + 4)
                wait(dve, k.masked, 2 * u + half + 1, 2 * base)
                dve.tensor_reduce(mx[:, s, cut], masked[:, s, cut], axis=AX.X, op=ALU.max).then_inc(k.maxed, 1)
                wait(dve, k.maxed, 2 * u + half + 1, 2 * base)
                if w.scaled:
                    wait(dve, k.staged, w.stage_incs * (u + 1), w.stage_incs * base)
                    dve.scalar_tensor_tensor(nb[:, s, cut], mx[:, s, cut], -1.0, scs[:, s, cut], ALU.mult, ALU.mult)\
                       .then_inc(k.biased, 1)
                else:
                    dve.tensor_scalar(nb[:, s, cut], mx[:, s, cut], -1.0, None, ALU.mult).then_inc(k.biased, 1)

            def recip(u, s):
                wait(dve, k.exped, 4 * u + 4, 4 * base)
                wait(dve, k.normed, u - 1, base)
                dve.reciprocal(rs[:, s, :], sums[:, s, :]).then_inc(k.recip, 1)

            def norm(u, s):
                wait(dve, k.recip, u + 1, base)
                wait(dve, k.weighed, 4 * u + 4, 4 * base)
                wait(dve, k.turned, u - 1, base)
                at = w.out_column(s)
                dve.tensor_tensor(on[:, s, at:at + 8 * hd].rearrange("p (h d) -> p h d", h=8),
                                  psO[:, 0:8 * hd].rearrange("p (h d) -> p h d", h=8),
                                  bc(rs[:, s, :], 2, hd), ALU.mult).then_inc(k.normed, 1)

            def finish(u, s):
                w.finish(dve, u, s, psW, k, base)

            def M(half, lag):
                return lambda u, s: mask(u, s, half), lag

            def X(half, lag):
                return lambda u, s: bias(u, s, half), lag

            def V(half, lag):
                return lambda u, s: evac(u, s, 2 * half + 1), lag

            if w.wo is None:
                order = [V(0, 2), (recip, 1), M(0, 0), V(1, 2), X(0, 0), M(1, 0), (norm, 2), X(1, 0)]
            else:
                order = [V(0, 2), M(0, 0), X(0, 0), M(1, 0), V(1, 2), X(1, 0), (norm, 2), (recip, 1),
                         (finish, 3)]
            pipeline(dve, U, order, tail=w.tail)

        @block.scalar
        def _(act):
            act.wait_ge(k.probs_zeroed, 1 + w.run)

            def evac(u, s, q):
                wait(act, k.transposed, 4 * u + q + 1, 4 * base)
                wait(act, k.weighed, 4 * (u - 1) + q + 1, 4 * base)
                act.copy(pts[:, q, :], psT[:, 0, :]).then_inc(k.evac_act, 1)

            def exp(u, s, q):
                wait(act, k.biased, 2 * u + q // 2 + 1, 2 * base)
                if q == 0:
                    wait(act, k.transposed, 4 * (u - 1), 4 * base)
                    wait(act, k.recip, u - 1, base)
                for h in (2 * q, 2 * q + 1):
                    last = act.activation(probs[:, s, h, off:off + BANDK], masked[:, s, h, :], ACT.Exp,
                                          bias=nb[:, s, h:h + 1],
                                          scale=scs[:, s, h:h + 1] if w.scaled else 1.0,
                                          accum_out=sums[:, s, h:h + 1])
                last.then_inc(k.exped, 1)

            def keep(u, s):
                wait(act, k.turned, u + 1, base)
                w.keep_turned(act, u, s, psW, ots, k, base)

            def A(half, lag):
                return lambda u, s: evac(u, s, 2 * half), lag

            def E(q, lag):
                return lambda u, s: exp(u, s, q), lag

            if w.wo is None:
                order = [(keep, 4), A(0, 2), E(0, 1), E(1, 1), A(1, 2), E(2, 1), E(3, 1)]
            else:
                order = [E(2, 1), A(0, 2), (keep, 3), E(3, 1), A(1, 2), E(0, 0), E(1, 0)]
            pipeline(act, U, order, tail=w.tail)


class BandSems:

    def __init__(self, sem):
        self.qs_zeroed = sem("qs_zeroed")
        self.probs_zeroed = sem("probs_zeroed")
        self.on_zeroed = sem("on_zeroed")
        self.staged = sem("staged")
        self.scored = sem("scored")
        self.masked = sem("masked")
        self.maxed = sem("maxed")
        self.biased = sem("biased")
        self.exped = sem("exped")
        self.transposed = sem("transposed")
        self.evac_act = sem("evac_act")
        self.evac_dve = sem("evac_dve")
        self.weighed = sem("weighed")
        self.recip = sem("recip")
        self.normed = sem("normed")
        self.turned = sem("turned")
        self.turned_kept = sem("turned_kept")
        self.projected = sem("projected")
        self.added = sem("added")
        self.finished = sem("finished")


def a_project_phase(nc, g, dram, hT, k):
    with ExitStack() as ctx:
        m = Space(nc, ctx, "ap")
        w5 = m.sb("w5", [P, 6, D])
        cols = m.sb("cols", [P, 3])
        rows = m.sb("rows", [P, 3, D])
        hs = m.sb("hs", [P, 2, 2, P])
        kb = m.sb("kb", [P, 2, D])
        kneg = m.sb("kneg", [P, 2, D])
        kexp = m.sb("kexp", [P, 2, D])
        kf = m.sb("kf", [P, 2, D])
        vb = m.sb("vb", [P, 2, D + 2])
        qb = m.sb("qb", [P, BANK])
        qneg = m.sb("qneg", [P, BANK])
        qexp = m.sb("qexp", [P, BANK])
        psKV = m.ps("psKV", [P, 2, BANK])
        psV = m.ps("psV", [P, 2, BANK])
        psA = m.ps("psA", [P, BANK])
        psQ = m.ps("psQ", [P, 3, BANK])
        loaded, staged, kv_done, v_done = m.sem("loaded"), m.sem("staged"), m.sem("kv_done"), m.sem("v_done")
        biased, kexped, featured, summed = m.sem("biased"), m.sem("kexped"), m.sem("featured"), m.sem("summed")
        v_kept, ones_set, kneg_done = m.sem("v_kept"), m.sem("ones_set"), m.sem("kneg_done")
        q_done, q_evac, qneg_done, qexped, q_kept = (m.sem("q_done"), m.sem("q_evac"), m.sem("qneg_done"),
                                                     m.sem("qexped"), m.sem("q_kept"))
        block = ctx.enter_context(nc.Block())
        n_v = NT + 2
        loads = [(w5[:, i, :], dram[n]) for i, n in enumerate(
            ["wk_lin", "wv_lin", "wv_loc", "wq_loc", "wk_loc", "wq_lin"])]
        loads += [(cols[:, i:i + 1], dram[n].unsqueeze(1)) for i, n in enumerate(["bq_loc", "bk_loc", "bq_lin"])]
        loads += [(rows[:, i, :], dram[n].partition_broadcast(P)) for i, n in enumerate(["bk_lin", "bv_lin", "bv_loc"])]
        n_loaded = 16 * len(loads)

        @block.sync
        def _(sp):
            for dst, src in loads:
                sp.dma_start(dst, src).then_inc(loaded, 16)

        @block.gpsimd
        def _(pool):
            pool.memset(vb[:], 1.0).then_inc(ones_set, 1)

            def stage(t, s):
                wait_apart(pool, v_done, t - 1)
                wait_apart(pool, kv_done, t - 1)
                pool.tensor_copy(hs[:, s, 0, :], hT[:, bass.ds(t * P + HALO_A, P)]).then_inc(staged, 1)
                pool.tensor_copy(hs[:, s, 1, :], hT[:, bass.ds(t * P, P)]).then_inc(staged, 1)

            pipeline(pool, n_v, [(stage, 0)])

        @block.tensor
        def _(pe):
            pe.wait_ge(loaded, n_loaded)

            def project(t, s):
                wait(pe, staged, 2 * t + 2)
                wait(pe, biased, 2 * (t - 1))
                wait(pe, v_kept, t - 1)
                pe.matmul(psKV[:, s, 0:2 * D], hs[:, s, 0, :], w5[:, 0:2, :], start=True, stop=True).then_inc(kv_done, 1)
                pe.matmul(psV[:, s, 0:D], hs[:, s, 1, :], w5[:, 2, :], start=True, stop=True).then_inc(v_done, 1)

            def accumulate(t, s):
                if isinstance(t, int) and t >= NT:
                    return
                wait(pe, featured, t + 1)
                first = isinstance(t, int) and t == 0
                last = isinstance(t, int) and t == NT - 1
                pe.matmul(psA[:, 0:D + 1], kf[:, s, :], vb[:, s, 0:D + 1], start=first, stop=last).then_inc(summed, 1)

            pipeline(pe, n_v, [(project, 0), (accumulate, 1)], tail=4)
            for c in range(S // BANK):
                wait(pe, q_evac, 3 * c)
                for j in range(3):
                    pe.matmul(psQ[:, j, :], w5[:, 3 + j, :], hT[:, HALO_A + c * BANK:HALO_A + (c + 1) * BANK],
                              start=True, stop=True).then_inc(q_done, 1)

        @block.vector
        def _(dve):
            dve.wait_ge(loaded, n_loaded)
            dve.wait_ge(ones_set, 1)

            def bias(t, s):
                wait(dve, kv_done, t + 1)
                wait(dve, summed, t - 1)
                wait(dve, kexped, t - 1)
                wait(dve, featured, t - 1)
                dve.tensor_tensor(kb[:, s, :], psKV[:, s, 0:D], rows[:, 0, :], ALU.add).then_inc(biased, 1)
                dve.tensor_tensor(vb[:, s, 0:D], psKV[:, s, D:2 * D], rows[:, 1, :], ALU.add).then_inc(biased, 1)
                wait(dve, v_done, t + 1)
                dve.tensor_tensor(g.vloc[:, t, :], psV[:, s, 0:D], rows[:, 2, :], ALU.add).then_inc(v_kept, 1)
                wait(dve, biased, 2 * t + 2)
                dve.tensor_scalar(kneg[:, s, :], kb[:, s, :], 0.0, None, ALU.min).then_inc(kneg_done, 1)

            def feature(t, s):
                wait(dve, kexped, t + 1)
                wait(dve, summed, t - 1)
                dve.scalar_tensor_tensor(kf[:, s, :], kb[:, s, :], 0.0, kexp[:, s, :], ALU.max, ALU.add)\
                   .then_inc(featured, 1)

            pipeline(dve, n_v, [(bias, 0), (feature, 1)], tail=4)
            dve.wait_ge(summed, NT)
            dve.tensor_copy(g.KV[:], psA[:, 0:D]).then_inc(biased, 1)
            dve.tensor_copy(g.KS[:], psA[:, D:D + 1].broadcast_to([P, P])).then_inc(biased, 1)
            for c in range(S // BANK):
                dve.wait_ge(q_evac, 3 * c + 3)
                wait(dve, qexped, c)
                dve.tensor_scalar(qneg[:], qb[:], 0.0, None, ALU.min).then_inc(qneg_done, 1)
                dve.wait_ge(qexped, c + 1)
                dve.scalar_tensor_tensor(g.qlinT[:, c * BANK:(c + 1) * BANK], qb[:], 0.0, qexp[:], ALU.max, ALU.add)\
                   .then_inc(q_kept, 1)

        @block.scalar
        def _(act):
            def exp(t, s):
                wait(act, kneg_done, t + 1)
                wait(act, featured, t - 1)
                act.activation(kexp[:, s, :], kneg[:, s, :], ACT.Exp).then_inc(kexped, 1)

            pipeline(act, n_v, [(exp, 0)])
            act.wait_ge(loaded, n_loaded)
            for c in range(S // BANK):
                act.wait_ge(q_done, 3 * c + 3)
                wait(act, q_kept, c)
                act.activation(g.qlocT[:, c * BANK:(c + 1) * BANK], psQ[:, 0, :], ACT.Identity,
                               bias=cols[:, 0:1]).then_inc(q_evac, 1)
                act.activation(g.klocT[:, HALO_A + c * BANK:HALO_A + (c + 1) * BANK], psQ[:, 1, :], ACT.Identity,
                               bias=cols[:, 1:2]).then_inc(q_evac, 1)
                act.activation(qb[:], psQ[:, 2, :], ACT.Identity, bias=cols[:, 2:3]).then_inc(q_evac, 1)
                act.wait_ge(qneg_done, c + 1)
                act.activation(qexp[:], qneg[:], ACT.Exp).then_inc(qexped, 1)


def a_window(nc, g, dram, ctx):
    m = Space(nc, ctx, "aw")
    w = Names()
    w.units, w.hd, w.run, w.tail = 2 * NT, A_HD, 0, 4
    w.prob_offset, w.zero_queries, w.scaled = 0, False, False
    w.stage_incs, w.out_tiles = 1, 1
    w.wo, w.finish = None, None
    w.out_column = lambda s: s * 8 * A_HD
    half = lambda u, s: (u - s) // 2 if isinstance(u, int) else (u - s) >> 1
    scale = float(np.float32(1.0 / np.sqrt(A_HD)))
    edge_done, tile_taken = m.sem("edge_done"), m.sem("tile_taken")
    tile = m.sb("tile", [P, 2, P])

    def stage(pool, u, s, qs, scs, staged):
        pool.tensor_copy(tile[:, s, :], g.qlocT[:, bass.ds(half(u, s) * P, P)]).then_inc(tile_taken, 1)
        wait_apart(pool, tile_taken, u + 1)
        pool.tensor_tensor(qs[:, s], bc(tile[:, s, :], 1, 8), bc(g.hmask[:, 8 * s:8 * s + 8], 2, P), ALU.mult).then_inc(staged, 1)

    def mask(dve, u, s, half_, out4, in4, out, masked):
        o = out.rearrange("p (b h) n -> p b (h n)", b=2)
        i = in4.rearrange("p b h n -> p b (h n)")
        at = 8 * s + 4 * half_
        b = g.relb[:, at:at + 4, :].rearrange("p (b h) n -> p b (h n)", b=2)
        edge = isinstance(u, int) and (u < 2 or u >= 2 * NT - 2)
        ins = dve.scalar_tensor_tensor(o, i, scale, b, ALU.mult, ALU.add)
        if edge:
            ins.then_inc(edge_done, 1)
            wait(dve, edge_done, 2 * (u if u < 2 else u - (2 * NT - 2) + 2) + half_ + 1)
            e = g.edge[:, 0 if u < 2 else 1, :]
            ins = dve.tensor_tensor(out, out, bc(e, 1, 4), ALU.add)
        ins.then_inc(masked, 1)

    def keep_turned(act, u, s, psW, ots, k, base):
        act.copy(g.winT[64 * s:64 * s + 64, bass.ds(half(u, s) * P, P)], psW[64 * s:64 * s + 64, 0:P]).then_inc(k.finished, 1)

    w.stage, w.mask, w.keep_turned = stage, mask, keep_turned
    w.keys = lambda u, s, h: g.klocT[:, bass.ds(half(u, s) * P, BANDK)]
    w.vals = lambda u, s, h, b: g.vloc[:, half(u, s) + b, (8 * s + h) * A_HD:(8 * s + h + 1) * A_HD]
    return w


def a_gate_phase(nc, g, dram, hT):
    with ExitStack() as ctx:
        m = Space(nc, ctx, "ag")
        wg1 = m.sb("wg1", [P, 3, D])
        wg2 = m.sb("wg2", [P, D])
        wo = m.sb("wo", [P, D])
        cols = m.sb("cols", [P, 2])
        nbg2 = m.sb("nbg2", [P, 1])
        bo = m.sb("bo", [P, D])
        den = m.sb("den", [P, BANK])
        rden = m.sb("rden", [P, BANK])
        lin = m.sb("lin", [P, BANK])
        g1 = m.sb("g1", [P, BANK])
        eg = m.sb("eg", [P, BANK])
        e1 = m.sb("e1", [P, BANK])
        gate = m.sb("gate", [P, BANK])
        diff = m.sb("diff", [P, BANK])
        gd = m.sb("gd", [P, BANK])
        mix = m.sb("mix", [P, BANK])
        res = m.sb("res", [P, 4, D])
        psN = m.ps("psN", [P, BANK])
        psD = m.ps("psD", [P, BANK])
        psG = m.ps("psG", [P, BANK])
        psH = m.ps("psH", [P, BANK])
        psY = m.ps("psY", [P, BANK])
        loaded, q, d, a = m.sem("loaded"), m.sem("products"), m.sem("dve_step"), m.sem("act_step")
        neg = m.sem("neg")
        stored = m.sem("x_updated")
        block = ctx.enter_context(nc.Block())
        loads = [(wg1[:], dram["wg1"].rearrange("(c p) n -> p c n", p=P)), (wg2[:], dram["wg2"]), (wo[:], dram["wo"]),
                 (cols[:, 0:1], dram["bg1"].unsqueeze(1)), (cols[:, 1:2], dram["bg2"].unsqueeze(1)),
                 (bo[:], dram["bo"].partition_broadcast(P))]
        n_loaded = 16 * len(loads)
        NC_, DV, AC = 5, 9, 2

        @block.sync
        def _(sp):
            for dst, src in loads:
                sp.dma_start(dst, src).then_inc(loaded, 16)

        @block.tensor
        def _(pe):
            pe.wait_ge(loaded, n_loaded)
            for c in range(S // BANK):
                cut = slice(c * BANK, (c + 1) * BANK)
                wait(pe, d, DV * c)
                pe.matmul(psN[:], g.KV[:], g.qlinT[:, cut], start=True, stop=True).then_inc(q, 1)
                pe.matmul(psD[:], g.KS[:], g.qlinT[:, cut], start=True, stop=True).then_inc(q, 1)
                pe.matmul(psG[:], wg1[:, 1, :], g.winT[:, cut], start=True, stop=False)
                pe.matmul(psG[:], wg1[:, 2, :], hT[:, HALO_A + c * BANK:HALO_A + (c + 1) * BANK], start=False, stop=False)
                pe.wait_ge(d, DV * c + 3)
                pe.matmul(psG[:], wg1[:, 0, :], lin[:], start=False, stop=True).then_inc(q, 1)
                pe.wait_ge(a, AC * c + 1)
                pe.matmul(psH[:], wg2[:], g1[:], start=True, stop=True).then_inc(q, 1)
                pe.wait_ge(d, DV * c + 8)
                for j in range(4):
                    last = pe.matmul(psY[:, j * D:(j + 1) * D], mix[:, j * P:(j + 1) * P], wo[:], start=True, stop=True)
                last.then_inc(q, 1)

        @block.scalar
        def _(act):
            act.wait_ge(neg, 1)
            for c in range(S // BANK):
                act.wait_ge(q, NC_ * c + 3)
                act.activation(g1[:], psG[:], ACT.Relu, bias=cols[:, 0:1]).then_inc(a, 1)
                act.wait_ge(q, NC_ * c + 4)
                act.activation(eg[:], psH[:], ACT.Exp, bias=nbg2[:], scale=-1.0).then_inc(a, 1)

        @block.vector
        def _(dve):
            dve.wait_ge(loaded, n_loaded)
            dve.tensor_scalar(nbg2[:], cols[:, 1:2], -1.0, None, ALU.mult).then_inc(neg, 1)
            for c in range(S // BANK):
                cut = slice(c * BANK, (c + 1) * BANK)
                n = DV * c
                dve.wait_ge(q, NC_ * c + 2)
                dve.tensor_scalar(den[:], psD[:], 1e-6, None, ALU.add).then_inc(d, 1)
                dve.wait_ge(d, n + 1)
                dve.reciprocal(rden[:], den[:]).then_inc(d, 1)
                dve.wait_ge(d, n + 2)
                dve.tensor_tensor(lin[:], psN[:], rden[:], ALU.mult).then_inc(d, 1)
                dve.wait_ge(d, n + 3)
                dve.tensor_tensor(diff[:], lin[:], g.winT[:, cut], ALU.subtract).then_inc(d, 1)
                dve.wait_ge(a, AC * c + 2)
                dve.tensor_scalar(e1[:], eg[:], 1.0, None, ALU.add).then_inc(d, 1)
                dve.wait_ge(d, n + 5)
                dve.reciprocal(gate[:], e1[:]).then_inc(d, 1)
                dve.wait_ge(d, n + 6)
                dve.tensor_tensor(gd[:], gate[:], diff[:], ALU.mult).then_inc(d, 1)
                dve.wait_ge(d, n + 7)
                dve.tensor_tensor(mix[:], gd[:], g.winT[:, cut], ALU.add).then_inc(d, 1)
                dve.wait_ge(q, NC_ * c + 5)
                dve.tensor_tensor(res[:], psY[:].rearrange("p (t d) -> p t d", t=4), bc(bo[:], 1, 4), ALU.add)\
                   .then_inc(d, 1)
                dve.wait_ge(d, n + 9)
                dve.tensor_tensor(g.x[:, 4 * c:4 * c + 4, :], g.x[:, 4 * c:4 * c + 4, :], res[:], ALU.add)\
                   .then_inc(stored, 1)


def attention_a(nc, g, dram):
    with ExitStack() as ctx:
        m = Space(nc, ctx, "a")
        z = m.sb("z", [P, NT, D])
        hT = m.sb("hT", [P, (NT + 2) * P + HALO_A + 96])
        g.vloc = m.sb("vloc", [P, NT + 2, D])
        g.qlocT = m.sb("qlocT", [P, S])
        g.klocT = m.sb("klocT", [P, HALO_A + S + BANDK])
        g.qlinT = m.sb("qlinT", [P, S])
        g.winT = m.sb("winT", [P, S])
        g.KV = m.sb("KV", [P, D])
        g.KS = m.sb("KS", [P, P])
        g.relb = m.sb("relb", [P, A_HEADS, BANDK])
        g.edge = m.sb("edge", [P, 2, BANDK])
        g.hmask = m.sb("hmask", [P, A_HEADS])
        ln = m.sb("ln", [P, 2])
        loaded, padded = m.sem("loaded"), m.sem("padded")
        with nc.Block() as block:
            loads = [(ln[:, 0:1], dram["ln_g"].unsqueeze(1)), (ln[:, 1:2], dram["ln_b"].unsqueeze(1)),
                     (g.hmask[:], dram["hmask"]), (g.edge[:], dram["edge"]), (g.relb[:], dram["relb"])]

            @block.sync
            def _(sp):
                for dst, src in loads:
                    sp.dma_start(dst, src).then_inc(loaded, 16)
                sp.wait_ge(loaded, 16 * len(loads))

            @block.gpsimd
            def _(pool):
                pool.memset(hT[:, 0:HALO_A], 0.0)
                pool.memset(hT[:, HALO_A + S:], 0.0)
                pool.memset(g.klocT[:, 0:HALO_A], 0.0)
                pool.memset(g.klocT[:, HALO_A + S:], 0.0).then_inc(padded, 1)

        norm_phase(nc, "anz", g.x, z, g)
        norm_phase(nc, "anh", z, g.vloc, g, (hT, ln[:, 0:1], ln[:, 1:2], HALO_A))
        a_project_phase(nc, g, dram, hT, None)
        add_phase(nc, "axz", g.x, z)
        k = BandSems(sem_maker(nc, "awk"))
        band_phase(nc, "awb", g, a_window(nc, g, dram, ctx), k, 0)
        a_gate_phase(nc, g, dram, hT)


def f_load_phase(nc, g, dram, layer, loaded, base):
    one = bass.ds(layer, 1)

    def of(name):
        return dram[name][one]

    loads = [(g.wqkv[:], of("wqkv")[0]), (g.fwo[:], of("fwo")[0].rearrange("(c p) n -> p c n", p=P)),
             (g.w1[:], of("w1")[0]), (g.lnc[:, 0:1], of("fln_g").rearrange("a p -> p a")),
             (g.lnc[:, 1:2], of("fln_b").rearrange("a p -> p a")), (g.b2[:], of("b2")[0].partition_broadcast(P))]
    h = F_HD // 2
    for j, name in enumerate(["q_scale", "k_scale"]):
        loads.append((g.sc4[:, j, :], of(name)[0].partition_broadcast(P)))
        loads.append((g.sc4[:, 2 + j, 0:h], of(name)[0, h:F_HD].partition_broadcast(P)))
        loads.append((g.sc4[:, 2 + j, h:F_HD], of(name)[0, 0:h].partition_broadcast(P)))
    for c, (at, n) in enumerate(HID_CUTS):
        loads.append((g.w2[0:n, c, :], of("w2")[0, at:at + n]))
        for j in range(2):
            loads.append((g.b1[0:n, 3 * j + c:3 * j + c + 1],
                          of("b1")[0, HID * j + at:HID * j + at + n].unsqueeze(1)))
    with nc.Block() as block:
        @block.sync
        def _(sp):
            for dst, src in loads:
                sp.dma_start(dst, src).then_inc(loaded, 16)

        @block.tensor
        def _(pe):
            pe.wait_ge(loaded, base * (16 * len(loads)) + 16 * len(loads))


class QkvSems:

    def __init__(self, sem):
        self.y_staged = sem("y_staged")
        self.yT_done = sem("yT_done")
        self.hT_ready = sem("hT_ready")
        self.qkv_done = sem("qkv_done")
        self.raw_ready = sem("raw_ready")
        self.v_ready = sem("v_ready")
        self.sq_ready = sem("sq_ready")
        self.ss_done = sem("ss_done")
        self.rot_part = sem("rot_part")
        self.rot_done = sem("rot_done")
        self.tab_ready = sem("tab_ready")
        self.ss_clipped = sem("ss_clipped")
        self.rn_done = sem("rn_done")
        self.k_scaled = sem("k_scaled")
        self.turned = sem("turned")
        self.q_kept = sem("q_kept")
        self.k_kept = sem("k_kept")
        self.padded = sem("padded")


class MlpSems:

    def __init__(self, sem):
        self.y_staged = sem("y_staged")
        self.yT_done = sem("yT_done")
        self.hT_ready = sem("hT_ready")
        self.h_back = sem("h_back")
        self.stats_done = sem("stats_done")
        self.mv_done = sem("mv_done")
        self.eps_added = sem("eps_added")
        self.rstd_done = sem("rstd_done")
        self.normed = sem("normed")
        self.hnT_done = sem("hnT_done")
        self.hnT_ready = sem("hnT_ready")
        self.up_done = sem("up_done")
        self.gelued = sem("gelued")
        self.gated = sem("gated")
        self.down_done = sem("down_done")
        self.b2_added = sem("b2_added")
        self.added = sem("added")


def shifted_copy(act, hT, psT, s, t, zcol, hT_ready, base):
    lo, hi = slice(0, D // 2), slice(D // 2, D)
    act.copy(hT[lo, s, 0:P], psT[lo, 0:P]).then_inc(hT_ready, 1)
    act.copy(hT[hi, s, 1:P + 1], psT[hi, 0:P]).then_inc(hT_ready, 1)
    if isinstance(t, int) and t == 0:
        act.copy(hT[hi, s, 0:1], zcol[hi, :]).then_inc(hT_ready, 1)
    else:
        wait(act, hT_ready, 3 * t, 3 * base)
        act.copy(hT[hi, s, 0:1], hT[hi, 1 - s, P:P + 1]).then_inc(hT_ready, 1)


def f_qkv_phase(nc, prefix, g, k, run):
    base = run * NT
    with ExitStack() as ctx:
        m = Space(nc, ctx, prefix)
        ys = m.sb("ys", [P, 2, D])
        hT = m.sb("hT", [P, 2, P + 1])
        raw = m.sb("raw", [P, 2, 2 * F_INNER])
        sq = m.sb("sq", [P, 2, 2 * F_INNER])
        ss = m.sb("ss", [P, 2, 2 * F_HEADS])
        ssc = m.sb("ssc", [P, 2 * F_HEADS])
        rn = m.sb("rn", [P, 2, 2 * F_HEADS])
        tabw = m.sb("tabw", [P, 2, 4, F_HD])
        part_c = m.sb("part_c", [P, 2 * F_INNER])
        part_s = m.sb("part_s", [P, 2 * F_INNER])
        rot = m.sb("rot", [P, 2, 2 * F_INNER])
        kn = m.sb("kn", [P, 2, F_INNER])
        psT = m.ps("psT", [P, BANK])
        psX = m.ps("psX", [P, 3, BANK])
        psR = m.ps("psR", [P, 2, 2, BANK])
        block = ctx.enter_context(nc.Block())
        H2 = F_HD // 2

        @block.gpsimd
        def _(pool):
            pool.memset(g.KT[:, :, 0:HALO_F], 0.0)
            pool.memset(g.V[:, 0, :], 0.0).then_inc(k.padded, 1)

            def stage(t, s):
                wait_apart(pool, k.yT_done, t - 1, base)
                pool.tensor_copy(ys[:, s, :], g.y[:, t, :]).then_inc(k.y_staged, 1)

            def tables(t, s):
                wait_apart(pool, k.rot_part, 3 * (t - 1), 3 * base)
                pool.tensor_tensor(tabw[:, s], g.tab[:, t], g.sc4[:], ALU.mult).then_inc(k.tab_ready, 1)

            def norms(t, s):
                wait_apart(pool, k.ss_done, t + 1, base)
                wait_apart(pool, k.rn_done, 2 * t, 2 * base)
                wait_apart(pool, k.k_scaled, t - 1, base)
                pool.tensor_scalar(ssc[:], ss[:, s, :], 1e-24, None, ALU.max).then_inc(k.ss_clipped, 1)
                wait_apart(pool, k.ss_clipped, t + 1, base)
                pool.tensor_tensor(rn[:, s, :], ssc[:], bc(g.mhalf[:, 0], 1, 2 * F_HEADS), ALU.pow).then_inc(k.rn_done, 1)
                wait_apart(pool, k.rn_done, 2 * t + 1, 2 * base)
                pool.tensor_copy(g.qscale[:, t, :], rn[:, s, 0:F_HEADS]).then_inc(k.rn_done, 1)

            pipeline(pool, NT, [(stage, 0), (norms, 3), (tables, 1)])

        @block.tensor
        def _(pe):
            def turn_y(t, s):
                wait(pe, k.y_staged, t + 1, base)
                wait(pe, k.hT_ready, 3 * t, 3 * base)
                pe.transpose(psT[:, 0:P], ys[:, s, :], g.ident[:]).then_inc(k.yT_done, 1)

            def project(t, s):
                wait(pe, k.hT_ready, 3 * t + 3, 3 * base)
                wait(pe, k.raw_ready, t, base)
                wait(pe, k.v_ready, t, base)
                for c in range(3):
                    last = pe.matmul(psX[:, c, :], hT[:, s, 0:P], g.wqkv[:, c * BANK:(c + 1) * BANK],
                                     start=True, stop=True)
                last.then_inc(k.qkv_done, 1)

            def turn_qk(t, s):
                wait(pe, k.rot_done, t + 1, base)
                wait(pe, k.q_kept, t - 1, base)
                wait(pe, k.k_kept, t - 1, base)
                for j in range(4):
                    pe.transpose(psR[:, s, 0, j * P:(j + 1) * P], rot[:, s, j * P:(j + 1) * P], g.ident[:])
                wait(pe, k.k_scaled, t + 1, base)
                for j in range(4):
                    last = pe.transpose(psR[:, s, 1, j * P:(j + 1) * P], kn[:, s, j * P:(j + 1) * P], g.ident[:])
                last.then_inc(k.turned, 1)

            pipeline(pe, NT, [(turn_y, 1), (project, 2), (turn_qk, 4)])

        @block.scalar
        def _(act):
            act.wait_ge(k.padded, 1 + run)

            def take_y(t, s):
                wait(act, k.yT_done, t + 1, base)
                wait(act, k.qkv_done, t - 1, base)
                shifted_copy(act, hT, psT, s, t, g.zcol, k.hT_ready, base)

            def take_qkv(t, s):
                wait(act, k.qkv_done, t + 1, base)
                wait(act, k.rot_part, 3 * (t - 1), 3 * base)
                act.copy(raw[:, s, :].rearrange("p (a n) -> p a n", a=2), psX[:, 0:2, :]).then_inc(k.raw_ready, 1)
                act.copy(g.V[:, t + 1, :], psX[:, 2, :]).then_inc(k.v_ready, 1)
                wait(act, k.raw_ready, t + 1, base)
                wait(act, k.ss_done, t - 1, base)
                act.activation(sq[:, s, :], raw[:, s, :], ACT.Square).then_inc(k.sq_ready, 1)

            def keep(t, s):
                wait(act, k.turned, t + 1, base)
                act.copy(g.QT[:, :, bass.ds(t * P, P)], psR[:, s, 0, :].rearrange("p (c n) -> p c n", c=4))\
                   .then_inc(k.q_kept, 1)
                act.copy(g.KT[:, :, bass.ds(t * P + HALO_F, P)], psR[:, s, 1, :].rearrange("p (c n) -> p c n", c=4))\
                   .then_inc(k.k_kept, 1)

            pipeline(act, NT, [(take_y, 1), (take_qkv, 2), (keep, 4)])

        @block.vector
        def _(dve):
            def sums(t, s):
                wait(dve, k.sq_ready, t + 1, base)
                wait(dve, k.rn_done, 2 * (t - 1), 2 * base)
                dve.tensor_reduce(ss[:, s, :], sq[:, s, :].rearrange("p (h d) -> p h d", d=F_HD),
                                  axis=AX.X, op=ALU.add).then_inc(k.ss_done, 1)

            def rotate(t, s):
                r4 = raw[:, s, :].rearrange("p (a h d) -> p a h d", a=2, h=F_HEADS)
                c4 = part_c[:].rearrange("p (a h d) -> p a h d", a=2, h=F_HEADS)
                s4 = part_s[:].rearrange("p (a h d) -> p a h d", a=2, h=F_HEADS)
                cos = bc(tabw[:, s, 0:2, :], 2, F_HEADS)
                sin = bc(tabw[:, s, 2:4, :], 2, F_HEADS)
                wait(dve, k.tab_ready, t + 1, base)
                wait(dve, k.rot_done, t, base)
                dve.tensor_tensor(c4, r4, cos, ALU.mult).then_inc(k.rot_part, 1)
                dve.tensor_tensor(s4[:, :, :, 0:H2], r4[:, :, :, H2:], sin[:, :, :, 0:H2], ALU.mult).then_inc(k.rot_part, 1)
                dve.tensor_tensor(s4[:, :, :, H2:], r4[:, :, :, 0:H2], sin[:, :, :, H2:], ALU.mult).then_inc(k.rot_part, 1)
                wait(dve, k.rot_part, 3 * t + 3, 3 * base)
                wait(dve, k.turned, t - 1, base)
                dve.tensor_tensor(rot[:, s, :], part_c[:], part_s[:], ALU.add).then_inc(k.rot_done, 1)

            def scale_k(t, s):
                wait(dve, k.rn_done, 2 * t + 1, 2 * base)
                wait(dve, k.rot_done, t + 1, base)
                wait(dve, k.turned, t - 1, base)
                dve.tensor_tensor(kn[:, s, :].rearrange("p (h d) -> p h d", h=F_HEADS),
                                  rot[:, s, F_INNER:].rearrange("p (h d) -> p h d", h=F_HEADS),
                                  bc(rn[:, s, F_HEADS:], 2, F_HD), ALU.mult).then_inc(k.k_scaled, 1)

            pipeline(dve, NT, [(sums, 2), (rotate, 2), (scale_k, 3)])


def f_window(g, k, run):
    w = Names()
    w.units, w.hd, w.run, w.tail = NT, F_HD, run, 0
    w.prob_offset, w.zero_queries, w.scaled = HALO_F, True, True
    w.stage_incs, w.out_tiles = 3, 4
    w.wo = g.fwo
    w.out_column = lambda s: 0

    def stage(pool, u, s, qs, scs, staged):
        q = g.QT[:, :, bass.ds(u * P, P)]
        pairs = qs[:, s].rearrange("p (c b) n -> p c b n", b=2)
        wait_apart(pool, staged, 3 * u, 3 * run * NT)
        pool.tensor_copy(scs[:, s, :], g.qscale[:, u, :]).then_inc(staged, 1)
        pool.tensor_copy(pairs[0:64, :, 0, :], q[0:64]).then_inc(staged, 1)
        wait_apart(pool, staged, 3 * u + 2, 3 * run * NT)
        pool.tensor_copy(pairs[64:128, :, 1, :], q[64:128]).then_inc(staged, 1)

    def mask(dve, u, s, half, out4, in4, out, masked):
        b = g.bandmask[:, 1 if isinstance(u, int) and u == 0 else 0, :]
        dve.tensor_tensor(out4, in4, bc(bc(b, 1, 2), 1, 2), ALU.add).then_inc(masked, 1)

    def keep_turned(act, u, s, psW, ots, k, base):
        wait(act, k.projected, u, base)
        act.copy(ots[:].rearrange("p c n -> p (c n)"), psW[:]).then_inc(k.turned_kept, 1)

    def finish(dve, u, s, psW, k, base):
        wait(dve, k.projected, u + 1, base)
        dve.tensor_tensor(g.y[:, u, :], g.y[:, u, :], psW[:, 0:D], ALU.add).then_inc(k.finished, 1)

    w.stage, w.mask, w.keep_turned, w.finish = stage, mask, keep_turned, finish
    w.keys = lambda u, s, h: g.KT[:, h // 2, bass.ds(u * P, BANDK)]
    w.vals = lambda u, s, h, b: g.V[:, u + b, h * F_HD:(h + 1) * F_HD]
    return w


def f_mlp_phase(nc, prefix, g, k, run):
    base = run * NT
    with ExitStack() as ctx:
        m = Space(nc, ctx, prefix)
        ys = m.sb("ys", [P, 2, D])
        hT = m.sb("hT", [P, 2, P + 1])
        stats = m.sb("stats", [P, 2, 6])
        mv = m.sb("mv", [P, 2, 2])
        vare = m.sb("vare", [P, 1])
        rstd = m.sb("rstd", [P, 2])
        hn = m.sb("hn", [P, 2, D])
        hnT = m.sb("hnT", [P, 2, P])
        gg = m.sb("gg", [P, 2, 3, P])
        ug = m.sb("ug", [P, 2, 3, P])
        tmp = m.sb("tmp", [P, D])
        psA = m.ps("psA", [P, BANK])
        psB = m.ps("psB", [P, BANK])
        psC = m.ps("psC", [P, BANK])
        psU = m.ps("psU", [P, 2, 2, BANK])
        psF = m.ps("psF", [P, BANK])
        block = ctx.enter_context(nc.Block())

        @block.gpsimd
        def _(pool):
            def stage(t, s):
                wait_apart(pool, k.yT_done, t - 1, base)
                pool.tensor_copy(ys[:, s, :], g.y[:, t, :]).then_inc(k.y_staged, 1)

            def spread(t, s):
                wait_apart(pool, k.mv_done, t + 1, base)
                wait_apart(pool, k.rstd_done, t, base)
                pool.tensor_scalar(vare[:], mv[:, s, 1:2], EPS, None, ALU.add).then_inc(k.eps_added, 1)
                wait_apart(pool, k.eps_added, t + 1, base)
                wait_apart(pool, k.normed, t - 1, base)
                pool.tensor_tensor(rstd[:, s:s + 1], vare[:], g.mhalf[:], ALU.pow).then_inc(k.rstd_done, 1)

            pipeline(pool, NT, [(stage, 0), (spread, 1)])

        @block.tensor
        def _(pe):
            def turn_y(t, s):
                wait(pe, k.y_staged, t + 1, base)
                wait(pe, k.hT_ready, 3 * t, 3 * base)
                pe.transpose(psA[:, 0:P], ys[:, s, :], g.ident[:]).then_inc(k.yT_done, 1)

            def turn_back(t, s):
                wait(pe, k.hT_ready, 3 * t + 3, 3 * base)
                wait(pe, k.normed, t, base)
                pe.transpose(psB[:, 0:P], hT[:, s, 0:P], g.ident[:]).then_inc(k.h_back, 1)

            def turn_norm(t, s):
                wait(pe, k.normed, t + 1, base)
                wait(pe, k.hnT_ready, t, base)
                pe.transpose(psC[:, 0:P], hn[:, s, :], g.ident[:]).then_inc(k.hnT_done, 1)

            def up(t, s):
                wait(pe, k.hnT_ready, t + 1, base)
                wait(pe, k.gated, 3 * (t - 1), 3 * base)
                for j in (1, 0):
                    for c, (at, n) in enumerate(HID_CUTS):
                        last = pe.matmul(psU[0:n, s, j, c * P:(c + 1) * P], g.w1[:, HID * j + at:HID * j + at + n],
                                         hnT[:, s, :], start=True, stop=True)
                last.then_inc(k.up_done, 1)

            def down(t, s):
                wait(pe, k.gated, 3 * t + 3, 3 * base)
                wait(pe, k.b2_added, t, base)
                for c, (at, n) in enumerate(HID_CUTS):
                    last = pe.matmul(psF[:, 0:D], ug[0:n, s, c, :], g.w2[0:n, c, :], start=c == 0, stop=c == 2)
                last.then_inc(k.down_done, 1)

            pipeline(pe, NT, [(turn_back, 1), (turn_y, 0), (turn_norm, 2), (up, 3), (down, 5)])

        @block.scalar
        def _(act):
            def take_y(t, s):
                wait(act, k.yT_done, t + 1, base)
                wait(act, k.h_back, t - 1, base)
                shifted_copy(act, hT, psA, s, t, g.zcol, k.hT_ready, base)

            def take_norm(t, s):
                wait(act, k.hnT_done, t + 1, base)
                wait(act, k.up_done, t - 1, base)
                act.activation(hnT[:, s, :], psC[:, 0:P], ACT.Identity, bias=g.lnc[:, 1:2], scale=g.lnc[:, 0:1])\
                   .then_inc(k.hnT_ready, 1)

            def gelu(t, s):
                wait(act, k.up_done, t + 1, base)
                wait(act, k.gated, 3 * (t - 1), 3 * base)
                for c, (at, n) in enumerate(HID_CUTS):
                    act.activation(gg[0:n, s, c, :], psU[0:n, s, 1, c * P:(c + 1) * P], ACT.Gelu,
                                   bias=g.b1[0:n, 3 + c:4 + c]).then_inc(k.gelued, 1)

            pipeline(act, NT, [(take_y, 0), (take_norm, 2), (gelu, 3)])

        @block.vector
        def _(dve):
            def stats_of(t, s):
                wait(dve, k.h_back, t + 1, base)
                dve.bn_stats(stats[:, s, :], psB[:, 0:P]).then_inc(k.stats_done, 1)
                wait_apart(dve, k.stats_done, t + 1, base)
                dve.bn_aggr(mv[:, s, :], stats[:, s, :]).then_inc(k.mv_done, 1)

            def normalise(t, s):
                wait(dve, k.rstd_done, t + 1, base)
                wait(dve, k.hnT_done, t - 1, base)
                dve.tensor_scalar(hn[:, s, :], psB[:, 0:P], mv[:, s, 0:1], rstd[:, s:s + 1], ALU.subtract, ALU.mult)\
                   .then_inc(k.normed, 1)

            def gates(t, s):
                wait(dve, k.gelued, 3 * t + 3, 3 * base)
                wait(dve, k.down_done, t - 1, base)
                for c, (at, n) in enumerate(HID_CUTS):
                    dve.scalar_tensor_tensor(ug[0:n, s, c, :], psU[0:n, s, 0, c * P:(c + 1) * P],
                                             g.b1[0:n, c:c + 1], gg[0:n, s, c, :], ALU.add, ALU.mult)\
                       .then_inc(k.gated, 1)

            def finish(t, s):
                wait(dve, k.down_done, t + 1, base)
                wait(dve, k.added, t, base)
                dve.tensor_tensor(tmp[:], psF[:, 0:D], g.b2[:], ALU.add).then_inc(k.b2_added, 1)
                wait(dve, k.b2_added, t + 1, base)
                dve.tensor_tensor(g.y[:, t, :], g.y[:, t, :], tmp[:], ALU.add).then_inc(k.added, 1)

            pipeline(dve, NT, [(stats_of, 1), (finish, 6), (gates, 4), (normalise, 1)])


def ffn(nc, g, dram, app, k):
    with ExitStack() as ctx:
        m = Space(nc, ctx, f"f{app}")
        g.y = m.sb("y", [P, NT, D])
        g.V = m.sb("V", [P, NT + 1, F_INNER])
        g.QT = m.sb("QT", [P, 4, S])
        g.KT = m.sb("KT", [P, 4, HALO_F + S])
        g.qscale = m.sb("qscale", [P, NT, F_HEADS])
        g.wqkv = m.sb("wqkv", [P, 3 * F_INNER])
        g.fwo = m.sb("fwo", [P, 4, D])
        g.w1 = m.sb("w1", [P, 2 * HID])
        g.w2 = m.sb("w2", [P, 3, D])
        g.b1 = m.sb("b1", [P, 6])
        g.b2 = m.sb("b2", [P, D])
        g.lnc = m.sb("lnc", [P, 2])
        g.sc4 = m.sb("sc4", [P, 4, F_HD])
        norm_phase(nc, f"f{app}n", g.x, g.y, g)
        with nc.Fori(0, F_DEPTH) as layer:
            run = layer + app * F_DEPTH
            f_load_phase(nc, g, dram, layer, k.loaded, run)
            f_qkv_phase(nc, f"f{app}q", g, k.qkv, run)
            band_phase(nc, f"f{app}b", g, f_window(g, k.band, run), k.band, run * NT)
            f_mlp_phase(nc, f"f{app}m", g, k.mlp, run)
        add_phase(nc, f"f{app}x", g.x, g.y)


class GroupSems:

    def __init__(self, sem):
        self.k_done = sem("k_done")
        self.kh_done = sem("kh_done")
        self.kl_done = sem("kl_done")
        self.v_staged = sem("v_staged")
        self.v_done = sem("v_done")
        self.v_high = sem("v_high")
        self.v_kept = sem("v_kept")
        self.q_done = sem("q_done")
        self.q_kept = sem("q_kept")
        self.q_taken = sem("q_taken")
        self.q_hi = sem("q_hi")
        self.q_top = sem("q_top")
        self.q_staged = sem("q_staged")
        self.scored = sem("scored")
        self.maxed = sem("maxed")
        self.biased = sem("biased")
        self.exped = sem("exped")
        self.transposed = sem("transposed")
        self.high_kept = sem("high_kept")
        self.low_kept = sem("low_kept")
        self.weighed = sem("weighed")
        self.summed = sem("summed")
        self.recip = sem("recip")
        self.out_kept = sem("out_kept")
        self.projected = sem("projected")
        self.added = sem("added")


def attention_b(nc, g, dram):
    with ExitStack() as ctx:
        m = Space(nc, ctx, "b")
        yT = m.sb("yT", [P, S])
        with ExitStack() as ctx_y:
            y = Space(nc, ctx_y, "by").sb("y", [P, NT, D])
            norm_phase(nc, "bn", g.x, y, g, (yT, None, None, 0))
            add_phase(nc, "bx", g.x, y)
        U = NT * B_HPG
        wk = m.sb("wk", [P, 2, B_HD])
        wv = m.sb("wv", [P, B_HD])
        wq = m.sb("wq", [P, B_HPG, 2, B_HD])
        wp = m.sb("wp", [P, B_HPG, D])
        kh = m.sb("kh", [P, S], F32R)
        kl = m.sb("kl", [P, S], F32R)
        v = m.sb("v", [P, NT, 2, B_HD], F32R)
        qd = m.sb("qd", [P, U, P])
        loaded = m.sem("loaded")
        k = GroupSems(sem_maker(nc, "bk"))

        with nc.Fori(0, B_GROUPS) as grp:
            b_group_prepare(nc, g, dram, k, grp, loaded, wk, wv, wq, wp, yT, kh, kl, v, qd)
            b_group_attend(nc, g, k, grp, kh, kl, v, qd, wp)


def b_group_prepare(nc, g, dram, k, grp, loaded, wk, wv, wq, wp, yT, kh, kl, v, qd):
    NC = S // BANK
    with ExitStack() as ctx:
        m = Space(nc, ctx, "bp")
        yts = m.sb("yts", [P, 2, P])
        psK = m.ps("psK", [P, 2, BANK])
        psV = m.ps("psV", [P, 2, BANK])
        psQ = m.ps("psQ", [P, 2, BANK])
        block = ctx.enter_context(nc.Block())
        kv_cols, q_cols = bass.ds(grp * B_HD, B_HD), bass.ds(grp * (B_HPG * B_HD), B_HPG * B_HD)
        loads = [(wk[:, i, :], dram["Wk"][:, kv_cols]) for i in range(2)] + [(wv[:], dram["Wv"][:, kv_cols])]
        loads += [(wq[:, :, i, :], dram["Wq"][:, q_cols].rearrange("p (h e) -> p h e", h=B_HPG)) for i in range(2)]
        loads += [(wp[i * B_HD:(i + 1) * B_HD], dram["Wpost"][q_cols, :].rearrange("(h e) n -> e h n", e=B_HD))
                  for i in range(2)]
        n_loaded = 16 * len(loads)

        @block.sync
        def _(sp):
            for dst, src in loads:
                sp.dma_start(dst, src).then_inc(loaded, 16)

        @block.gpsimd
        def _(pool):
            base = grp * NT

            def stage(t, s):
                wait_apart(pool, k.v_done, t - 1, base)
                pool.tensor_copy(yts[:, s, :], yT[:, bass.ds(t * P, P)]).then_inc(k.v_staged, 1)

            pipeline(pool, NT, [(stage, 0)])

        @block.tensor
        def _(pe):
            pe.wait_ge(loaded, grp * n_loaded + n_loaded)
            for c in range(NC):
                wait(pe, k.kl_done, c - 1, grp * NC)
                pe.matmul(psK[:, c % 2, :], wk[:], yT[:, c * BANK:(c + 1) * BANK], start=True, stop=True).then_inc(k.k_done, 1)

            def value(t, s):
                wait(pe, k.v_staged, t + 1, grp * NT)
                wait(pe, k.v_kept, t - 1, grp * NT)
                pe.matmul(psV[:, s, 0:B_HD], yts[:, s, :], wv[:], start=True, stop=True).then_inc(k.v_done, 1)

            pipeline(pe, NT, [(value, 0)])
            for n in range(B_HPG * NC):
                h, c = n // NC, n % NC
                wait(pe, k.q_kept, n - 1, grp * (B_HPG * NC))
                pe.matmul(psQ[:, n % 2, :], wq[:, h], yT[:, c * BANK:(c + 1) * BANK], start=True, stop=True)\
                  .then_inc(k.q_done, 1)

        @block.scalar
        def _(act):
            for c in range(NC):
                act.wait_ge(k.k_done, grp * NC + c + 1)
                act.copy(kh[:, c * BANK:(c + 1) * BANK], psK[:, c % 2, :]).then_inc(k.kh_done, 1)
            q5 = qd[:].rearrange("p (t h) n -> p t h n", h=B_HPG)
            for n in range(B_HPG * NC):
                h, c = n // NC, n % NC
                act.wait_ge(k.q_done, grp * (B_HPG * NC) + n + 1)
                act.activation(q5[:, c * 4:(c + 1) * 4, h, :], psQ[:, n % 2, :].rearrange("p (t n) -> p t n", t=4),
                               ACT.Copy, scale=1.0 / math.sqrt(B_HD)).then_inc(k.q_kept, 1)

        @block.vector
        def _(dve):
            for c in range(NC):
                cut = slice(c * BANK, (c + 1) * BANK)
                dve.wait_ge(k.kh_done, grp * NC + c + 1)
                dve.tensor_tensor(kl[:, cut], psK[:, c % 2, :], kh[:, cut].bitcast(F32), ALU.subtract).then_inc(k.kl_done, 1)

            def value(t, s):
                wait(dve, k.v_done, t + 1, grp * NT)
                dve.tensor_copy(v[:, t, 0, :], psV[:, s, 0:B_HD]).then_inc(k.v_high, 1)
                wait(dve, k.v_high, t + 1, grp * NT)
                dve.tensor_tensor(v[:, t, 1, :], psV[:, s, 0:B_HD], v[:, t, 0, :].bitcast(F32), ALU.subtract)\
                   .then_inc(k.v_kept, 1)

            pipeline(dve, NT, [(value, 0)])


def b_group_attend(nc, g, k, grp, kh, kl, v, qd, wp):
    with ExitStack() as ctx:
        m = Space(nc, ctx, "bt")
        U = NT * B_HPG
        qf = m.sb("qf", [P, 2, P])
        qh = m.sb("qh", [P, 2, P], F32R)
        qs = m.sb("qs", [P, 2, P], F32R)
        mx = m.sb("mx", [P, 2, 4])
        nb = m.sb("nb", [P, 2])
        probs = m.sb("probs", [P, 2, S])
        sums = m.sb("sums", [P, 4, EXPS])
        sm = m.sb("sm", [P, 1])
        rs = m.sb("rs", [P, 4])
        pth = m.sb("pth", [P, 2, NT, 2, P], F32R)
        ptl = m.sb("ptl", [P, 2, NT, 2, P], F32R)
        oT = m.sb("oT", [P, 2, 2 * P])
        psS = m.ps("psS", [P, 4, BANK])
        psT = m.ps("psT", [P, 2, BANK])
        psO = m.ps("psO", [P, BANK])
        psY = m.ps("psY", [P, BANK])
        block = ctx.enter_context(nc.Block())
        base = grp * U
        HI = slice(B_HD, P)

        @block.gpsimd
        def _(pool):
            def stage(u, s):
                wait_apart(pool, k.scored, 4 * (u - 1), 4 * base)
                wait_apart(pool, k.q_staged, u, base)
                pool.tensor_copy(qf[:, s, :], qd[:, u, :]).then_inc(k.q_taken, 1)
                wait_apart(pool, k.q_taken, u + 1, base)
                pool.tensor_copy(qh[HI, s, :], qf[HI, s, :]).then_inc(k.q_hi, 1)
                wait_apart(pool, k.q_hi, u + 1, base)
                pool.tensor_copy(qs[0:B_HD, s, :], qf[0:B_HD, s, :]).then_inc(k.q_top, 1)
                pool.tensor_tensor(qs[HI, s, :], qf[HI, s, :], qh[HI, s, :].bitcast(F32), ALU.subtract)\
                    .then_inc(k.q_staged, 1)

            pipeline(pool, U, [(stage, 0)])

        @block.tensor
        def _(pe):
            def score(u, s, c):
                cut = slice(c * BANK, (c + 1) * BANK)
                if c == 0:
                    wait(pe, k.q_staged, u + 1, base)
                    wait(pe, k.q_top, u + 1, base)
                wait(pe, k.exped, EXPS * (u - 1) + c * EXPS // 4 + 1, EXPS * base)
                pe.matmul(psS[:, c, :], qs[:, s % 2, :], kh[:, cut], start=True, stop=False)
                pe.matmul(psS[:, c, :], qs[:, s % 2, :], kl[:, cut], start=False, stop=True).then_inc(k.scored, 1)

            def turn(u, s, q):
                wait(pe, k.exped, EXPS * u + q * EXPS // 4 + 1, EXPS * base)
                wait(pe, k.low_kept, 4 * u + q - 1, 4 * base)
                for j in range(4):
                    last = pe.transpose(psT[:, q % 2, j * P:(j + 1) * P],
                                        probs[:, s % 2, (4 * q + j) * P:(4 * q + j + 1) * P], g.ident[:])
                last.then_inc(k.transposed, 1)

            def weigh(u, s, half):
                second = s % 2
                quarter = 2 * second + half
                wait(pe, k.low_kept, 4 * (u + 1 - second) + quarter + 1, 4 * base)
                if quarter == 0:
                    wait(pe, k.out_kept, u, base)
                for kt in range(4 * quarter, 4 * quarter + 4):
                    for part in (pth, ptl):
                        last = pe.matmul(psO[:, 0:2 * P], v[:, kt], part[:, s // 2, kt],
                                         start=kt == 0 and part is pth, stop=kt == NT - 1 and part is ptl)
                last.then_inc(k.weighed, 1)

            def project(u, s):
                wait(pe, k.out_kept, u + 2 - s % 2, base)
                wait(pe, k.added, u, base)
                pe.matmul(psY[:, 0:D], oT[:, s // 2, (s % 2) * P:(s % 2 + 1) * P], wp[:, s, :],
                          start=True, stop=True).then_inc(k.projected, 1)

            def C(c, lag):
                return lambda u, s: score(u, s, c), lag

            def T(q, lag):
                return lambda u, s: turn(u, s, q), lag

            def W(half, lag):
                return lambda u, s: weigh(u, s, half), lag

            order = [T(0, 3), W(0, 5), W(1, 5), T(1, 3), C(0, 1), C(1, 1), T(2, 3), (project, 6), C(2, 1),
                     T(3, 3), C(3, 1)]
            pipeline(pe, U, order, unroll=4)

        @block.vector
        def _(dve):
            def top(u, s, c):
                wait(dve, k.scored, 4 * u + c + 1, 4 * base)
                if c == 0:
                    wait(dve, k.biased, u - 1, base)
                dve.tensor_reduce(mx[:, s % 2, c:c + 1], psS[:, c, :], axis=AX.X, op=ALU.max).then_inc(k.maxed, 1)

            def bias(u, s):
                wait(dve, k.maxed, 4 * u + 4, 4 * base)
                wait(dve, k.exped, EXPS * (u - 1), EXPS * base)
                dve.tensor_reduce(nb[:, s % 2:s % 2 + 1], mx[:, s % 2, :], axis=AX.X, op=ALU.max, negate=True)\
                   .then_inc(k.biased, 1)

            def low(u, s, q):
                wait(dve, k.high_kept, 4 * u + q + 1, 4 * base)
                place = slice(4 * q, 4 * q + 4)
                dve.tensor_tensor(ptl[:, s // 2, place, s % 2, :], psT[:, q % 2, :].rearrange("p (t n) -> p t n", t=4),
                                  pth[:, s // 2, place, s % 2, :].bitcast(F32), ALU.subtract).then_inc(k.low_kept, 1)

            def recip(u, s):
                wait(dve, k.exped, EXPS * u + EXPS, EXPS * base)
                wait(dve, k.recip, u, base)
                dve.tensor_reduce(sm[:], sums[:, s, :], axis=AX.X, op=ALU.add).then_inc(k.summed, 1)
                wait(dve, k.summed, u + 1, base)
                wait(dve, k.added, u - 3, base)
                dve.reciprocal(rs[:, s:s + 1], sm[:]).then_inc(k.recip, 1)

            def add(u, s):
                tile = (u - s) // 4 if isinstance(u, int) else (u - s) >> 2
                wait(dve, k.projected, u + 1, base)
                wait(dve, k.recip, u + 1, base)
                wait(dve, k.added, u, base)
                dve.scalar_tensor_tensor(g.x[:, tile, :], psY[:, 0:D], rs[:, s:s + 1], g.x[:, tile, :],
                                         ALU.mult, ALU.add).then_inc(k.added, 1)

            def L(q, lag):
                return lambda u, s: low(u, s, q), lag

            def M(c, lag):
                return lambda u, s: top(u, s, c), lag

            order = [(add, 6), L(0, 2), (recip, 4), M(0, 0), L(1, 2), M(1, 0), L(2, 2), M(2, 0), M(3, 0),
                     (bias, 0), L(3, 2)]
            pipeline(dve, U, order, unroll=4)

        @block.scalar
        def _(act):
            def exp(u, s, c):
                if c == 0:
                    wait(act, k.biased, u + 1, base)
                    wait(act, k.transposed, 4 * (u - 1), 4 * base)
                    wait(act, k.recip, u - 3, base)
                n = 4 // EXPS
                act.activation(probs[:, s % 2, c * n * BANK:(c + 1) * n * BANK].rearrange("p (b n) -> p b n", b=n),
                               psS[:, n * c:n * (c + 1), :], ACT.Exp, bias=nb[:, s % 2:s % 2 + 1],
                               accum_out=sums[:, s, c:c + 1]).then_inc(k.exped, 1)

            def high(u, s, q):
                wait(act, k.transposed, 4 * u + q + 1, 4 * base)
                wait(act, k.weighed, 2 * (u - s % 2 - 4) + q + 1, 2 * base)
                act.copy(pth[:, s // 2, 4 * q:4 * q + 4, s % 2, :], psT[:, q % 2, :].rearrange("p (t n) -> p t n", t=4))\
                   .then_inc(k.high_kept, 1)

            def keep(u, s):
                if s % 2 == 0:
                    return
                wait(act, k.weighed, 2 * u + 2, 2 * base)
                wait(act, k.projected, u - 3, base)
                act.copy(oT[:, s // 2, :], psO[:, 0:2 * P]).then_inc(k.out_kept, 2)

            def H(q, lag):
                return lambda u, s: high(u, s, q), lag

            def E(c, lag):
                return lambda u, s: exp(u, s, c), lag

            order = [(keep, 5), H(1, 3), E(2, 2), H(2, 3), E(3, 2), H(3, 3), H(0, 2), E(0, 1), E(1, 1)]
            pipeline(act, U, order, unroll=4)


def store_phase(nc, g, out):
    with nc.semaphore("stored") as stored, nc.Block() as block:
        @block.sync
        def _(sp):
            sp.dma_start(out[0].rearrange("(t p) d -> p t d", p=P), g.x[:]).then_inc(stored, 16)
            sp.wait_ge(stored, 16)


def build(nc, dram, out, parts="afbf"):
    g = Names()
    with ExitStack() as ctx:
        LAUNCH.ctx = ctx
        m = Space(nc, ctx, "g")
        g.x = m.sb("x", [P, NT, D])
        g.ident = m.sb("ident", [P, P])
        g.zcol = m.sb("zcol", [P, 1])
        g.mhalf = m.sb("mhalf", [P, 1])
        g.tab = m.sb("tab", [P, NT, 4, F_HD])
        g.bandmask = m.sb("bandmask", [P, 2, BANDK])
        LAUNCH.marks, LAUNCH.constants_made = m.sem("marks"), m.sem("constants_made")
        LAUNCH.norm = NormSems(sem_maker(nc, "n"))
        LAUNCH.norm.runs = LAUNCH.norm.runs_T = 0
        load_phase(nc, g, dram)
        if "a" in parts:
            attention_a(nc, g, dram)
        k = Names()
        k.loaded = m.sem("f_loaded")
        k.qkv, k.band, k.mlp = (QkvSems(sem_maker(nc, "fq")), BandSems(sem_maker(nc, "fb")),
                                MlpSems(sem_maker(nc, "fm")))
        if "f" in parts:
            ffn(nc, g, dram, 0, k)
        if "b" in parts:
            attention_b(nc, g, dram)
        if parts.count("f") > 1:
            ffn(nc, g, dram, 1, k)
        store_phase(nc, g, out)


_A = "L0_attn_a_"
_NAMES = {"x": _A + "x", "wq_lin": _A + "wq_lin", "bq_lin": _A + "bq_lin", "wk_lin": _A + "wk_lin",
          "bk_lin": _A + "bk_lin", "wv_lin": _A + "wv_lin", "bv_lin": _A + "bv_lin", "wq_loc": _A + "wq_loc",
          "bq_loc": _A + "bq_loc", "wk_loc": _A + "wk_loc", "bk_loc": _A + "bk_loc", "wv_loc": _A + "wv_loc",
          "bv_loc": _A + "bv_loc", "wo": _A + "wo", "bo": _A + "bo", "wg1": _A + "wg1", "bg1": _A + "bg1",
          "wg2": _A + "wg2", "bg2": _A + "bg2", "ln_g": _A + "ln_g", "ln_b": _A + "ln_b",
          "Wq": "L0_attn_b_Wq", "Wk": "L0_attn_b_Wk", "Wv": "L0_attn_b_Wv", "Wpost": "L0_attn_b_Wpost",
          "wqkv": "L0_ffn_wqkv", "q_scale": "L0_ffn_q_scale", "k_scale": "L0_ffn_k_scale", "fwo": "L0_ffn_wo",
          "fln_g": "L0_ffn_ln_g", "fln_b": "L0_ffn_ln_b", "w1": "L0_ffn_w1", "b1": "L0_ffn_b1",
          "w2": "L0_ffn_w2", "b2": "L0_ffn_b2"}


def constants():
    f = np.float32
    half = np.arange(0, F_HD, 2, dtype=f)
    inv = (f(1.0) / np.power(f(10000.0), half / f(F_HD))).astype(f)
    t = np.arange(S, dtype=f)
    fr = (t[:, None] * inv[None, :]).astype(f)
    b = ((half + f(0.4 * F_HD)) / f(1.4 * F_HD)).astype(f)
    scale = np.power(b[None, :], ((t - S // 2) / f(32.0)).astype(f)[:, None]).astype(f)
    cos, sin = np.cos(fr).astype(f), np.sin(fr).astype(f)
    tab = np.zeros((S, 4, F_HD), f)
    for j, sc in enumerate((scale, f(1.0) / scale)):
        gain = f((8.0, 1.0)[j])
        tab[:, j] = gain * np.concatenate([cos * sc, cos * sc], 1)
        tab[:, 2 + j] = gain * np.concatenate([-sin * sc, sin * sc], 1)
    r, c = np.arange(P)[:, None], np.arange(BANDK)[None, :]
    band = np.where((c >= r) & (c <= r + HALO_F), 0.0, NEG).astype(f)
    band0 = np.where(c >= HALO_F, band, f(NEG)).astype(f)
    edge = np.zeros((P, 2, BANDK), f)
    edge[:, 0, :HALO_A] = NEG
    edge[:, 1, HALO_A + P:] = NEG
    hmask = (np.arange(D)[:, None] // A_HD == np.arange(A_HEADS)[None, :]).astype(f)
    return {"tables": tab, "bandmask": np.stack([band, band0], 1), "edge": edge, "hmask": hmask}


def band_of(rel_bias):
    r, c = np.arange(P)[:, None], np.arange(BANDK)[None, :]
    inside = (c >= r) & (c <= r + 2 * HALO_A)
    at = np.where(inside, c - r + HALO_A, 0)
    rows = rel_bias[at]
    return np.ascontiguousarray(np.where(inside[:, :, None], rows, np.float32(NEG)).transpose(0, 2, 1))


def kernel(**inputs):
    import concourse.bacc as _bacc
    from concourse.bass_utils import run_bass_kernel_spmd as _run

    arrays = {n: np.ascontiguousarray(inputs[full]) for n, full in _NAMES.items()}
    arrays["relb"] = band_of(np.asarray(inputs[_A + "rel_bias"]))
    arrays.update({n: np.ascontiguousarray(a) for n, a in constants().items()})
    nc = _bacc.Bacc("TRN2", target_bir_lowering=False, num_devices=1)
    dram = {n: nc.dram_tensor(f"in_{n}", a.shape, F32, kind="ExternalInput").ap() for n, a in arrays.items()}
    shape = (1, S, D)
    out = nc.dram_tensor("out_x", shape, F32, kind="ExternalOutput").ap()
    build(nc, dram, out)
    r = _run(nc, [{f"in_{n}": a for n, a in arrays.items()}], core_ids=[0])
    return r.results[0]["out_x"]
```

```python
import math
from contextlib import ExitStack

import concourse.bass as bass
import numpy as np
from concourse import mybir

F32 = mybir.dt.float32
F32R = mybir.dt.float32r
ACT = mybir.ActivationFunctionType
ALU = mybir.AluOpType
AX = mybir.AxisListType

P = 128
D = 128
S = 2048
NT = S // P
BANK = 512
BANDK = 192
HALO_A, HALO_F = 32, 64
NEG = -1.0e30

A_HEADS, A_HD = 16, 8
F_HEADS, F_HD, F_INNER, F_DEPTH = 8, 64, 512, 2
HID = int(D * 4 * 2 / 3)
HID_CUTS = [(0, 128), (128, 128), (256, HID - 256)]
B_GROUPS, B_HPG, B_HD = 4, 4, 64
EXPS = 4
EPS = 1e-5


def wait(eng, sem, n, base=0):
    if isinstance(n, int) and n <= 0:
        return
    eng.wait_ge(sem, n + base)


def wait_apart(eng, sem, n, base=0):
    if isinstance(n, int) and n <= 0:
        return
    eng.wait_ge(sem, n + base)
    if not isinstance(n + base, int):
        eng.sem_inc(LAUNCH.marks, 1)


def pipeline(eng, count, stages, tail=0, unroll=2):
    span = max(lag for _, lag in stages)
    first = min(count, (span + 2 * unroll - 1) // unroll * unroll)
    last = max(first, count - tail)

    def step(i):
        for stage, lag in stages:
            if 0 <= i - lag < count:
                stage(i - lag, (i - lag) % unroll)

    for i in range(first):
        step(i)
    if first < last:
        with eng.Fori(first // unroll, last // unroll) as turn:
            for k in range(unroll):
                for stage, lag in stages:
                    stage(turn * unroll + (k - lag), (k - lag) % unroll)
    for i in range(last, count + span):
        step(i)


class Names:
    pass


LAUNCH = Names()


class Space:

    def __init__(self, nc, ctx, prefix):
        self.nc, self.ctx, self.prefix = nc, ctx, prefix

    def sb(self, name, shape, dt=F32):
        return self.ctx.enter_context(self.nc.sbuf_tensor(f"{self.prefix}_{name}", shape, dt))

    def ps(self, name, shape):
        return self.ctx.enter_context(self.nc.psum_tensor(f"{self.prefix}_{name}", shape, F32))

    def sem(self, name):
        return LAUNCH.ctx.enter_context(self.nc.semaphore(f"{self.prefix}_{name}"))


def sem_maker(nc, prefix):
    return lambda name: LAUNCH.ctx.enter_context(nc.semaphore(f"{prefix}_{name}"))


def bc(ap, axis, n):
    ap = ap.unsqueeze(axis)
    shape = list(ap.shape)
    shape[axis] = n
    return ap.broadcast_to(shape)


def load_phase(nc, g, loads):
    with ExitStack() as ctx:
        sp_ = Space(nc, ctx, "load")
        loaded, zeroed = sp_.sem("loaded"), sp_.sem("zeroed")
        block = ctx.enter_context(nc.Block())

        @block.sync
        def _(sp):
            for dst, src in loads:
                sp.dma_start(dst, src).then_inc(loaded, 16)
            sp.wait_ge(loaded, 16 * len(loads))

        @block.gpsimd
        def _(pool):
            pool.memset(g.ident[:], 0.0).then_inc(zeroed, 1)
            pool.memset(g.zcol[:], 0.0)
            pool.memset(g.mhalf[:], -0.5)
            pool.wait_ge(zeroed, 1)
            pool.affine_select(out=g.ident[:], in_=g.ident[:], compare_op=ALU.not_equal, fill=1.0, base=0,
                               pattern=[[-1, P]], channel_multiplier=1).then_inc(LAUNCH.constants_made, 1)


class NormSems:

    def __init__(self, sem):
        self.meaned = sem("meaned")
        self.negated = sem("negated")
        self.centred = sem("centred")
        self.squared = sem("squared")
        self.varied = sem("varied")
        self.eps_added = sem("eps_added")
        self.rstd_done = sem("rstd_done")
        self.normed = sem("normed")
        self.transposed = sem("transposed")
        self.evacuated = sem("evacuated")


def norm_phase(nc, prefix, src, dst, g, affine_T=None, loads=(), loaded=None, loaded_before=0):
    with ExitStack() as ctx:
        m = Space(nc, ctx, prefix)
        sums = m.sb("sums", [P, NT])
        negmean = m.sb("negmean", [P, NT])
        var = m.sb("var", [P, NT])
        rstd = m.sb("rstd", [P, NT])
        sq = m.sb("sq", [P, NT, D])
        psT = m.ps("psT", [P, 4, BANK])
        k = LAUNCH.norm
        NC = NT // 4
        base, base_T = k.runs * NC, k.runs_T * NC
        k.runs += 1
        k.runs_T += affine_T is not None
        block = ctx.enter_context(nc.Block())

        @block.vector
        def _(dve):
            def centre(c, s):
                cut = slice(4 * c, 4 * c + 4)
                dve.tensor_reduce(sums[:, cut], src[:, cut, :], axis=AX.X, op=ALU.add).then_inc(k.meaned, 1)
                dve.wait_ge(k.meaned, c + 1 + base)
                dve.tensor_scalar(negmean[:, cut], sums[:, cut], -1.0 / D, None, ALU.mult).then_inc(k.negated, 1)
                dve.wait_ge(k.negated, c + 1 + base)
                dve.tensor_tensor(dst[:, cut, :], src[:, cut, :], bc(negmean[:, cut], 2, D), ALU.add)\
                   .then_inc(k.centred, 1)

            def vary(c, s):
                cut = slice(4 * c, 4 * c + 4)
                dve.wait_ge(k.squared, c + 1 + base)
                dve.tensor_reduce(var[:, cut], sq[:, cut, :], axis=AX.X, op=ALU.add).then_inc(k.varied, 1)

            def scale_rows(c, s):
                cut = slice(4 * c, 4 * c + 4)
                dve.wait_ge(k.rstd_done, c + 1 + base)
                dve.tensor_tensor(dst[:, cut, :], dst[:, cut, :], bc(rstd[:, cut], 2, D), ALU.mult)\
                   .then_inc(k.normed, 1)

            pipeline(dve, NC, [(centre, 0), (vary, 1), (scale_rows, 2)])

        @block.gpsimd
        def _(pool):
            for c in range(NC):
                cut = slice(4 * c, 4 * c + 4)
                pool.wait_ge(k.varied, c + 1 + base)
                pool.tensor_scalar(var[:, cut], var[:, cut], 1.0 / D, EPS, ALU.mult, ALU.add).then_inc(k.eps_added, 1)
                pool.wait_ge(k.eps_added, c + 1 + base)
                pool.tensor_tensor(rstd[:, cut], var[:, cut], bc(g.mhalf[:, 0], 1, 4), ALU.pow).then_inc(k.rstd_done, 1)

        if loads:
            @block.sync
            def _(sp):
                for place, source in loads:
                    sp.dma_start(place, source).then_inc(loaded, 16)
                sp.wait_ge(loaded, 16 * len(loads) + loaded_before)

        if affine_T is not None:
            out, scale, shift, pad = affine_T

            @block.tensor
            def _(pe):
                for c in range(NC):
                    pe.wait_ge(k.normed, c + 1 + base)
                    for j in range(4):
                        last = pe.transpose(psT[:, c, j * P:(j + 1) * P], dst[:, 4 * c + j, :], g.ident[:])
                    last.then_inc(k.transposed, 1)

        @block.scalar
        def _(act):
            for c in range(NC):
                cut = slice(4 * c, 4 * c + 4)
                act.wait_ge(k.centred, c + 1 + base)
                act.activation(sq[:, cut, :], dst[:, cut, :], ACT.Square).then_inc(k.squared, 1)
            if affine_T is None:
                return
            for c in range(NC):
                act.wait_ge(k.transposed, c + 1 + base_T)
                place = out[:, c * BANK + pad:(c + 1) * BANK + pad]
                if scale is None:
                    act.copy(place, psT[:, c, :]).then_inc(k.evacuated, 1)
                else:
                    act.activation(place, psT[:, c, :], ACT.Identity, bias=shift, scale=scale)\
                       .then_inc(k.evacuated, 1)


def add_phase(nc, prefix, x, y):
    with ExitStack() as ctx:
        block = ctx.enter_context(nc.Block())
        half = NT * 3 // 4

        @block.vector
        def _(dve):
            dve.tensor_tensor(x[:, 0:half, :], x[:, 0:half, :], y[:, 0:half, :], ALU.add)

        @block.gpsimd
        def _(pool):
            pool.tensor_tensor(x[:, half:NT, :], x[:, half:NT, :], y[:, half:NT, :], ALU.add)


def band_phase(nc, prefix, g, w, sems, base):
    with ExitStack() as ctx:
        m = Space(nc, ctx, prefix)
        U, hd = w.units, w.hd
        qs = m.sb("qs", [P, 2, 8, P])
        masked = m.sb("masked", [P, 2, 8, BANDK])
        mx = m.sb("mx", [P, 2, 8])
        nb = m.sb("nb", [P, 2, 8])
        scs = m.sb("scs", [P, 2, 8])
        probs = m.sb("probs", [P, 2, 8, 2 * P])
        sums = m.sb("sums", [P, 2, 8])
        rs = m.sb("rs", [P, 2, 8])
        pts = m.sb("pts", [P, 4, BANK])
        on_width = max(P, 8 * hd)
        on = m.sb("on", [P, 2, on_width])
        ots = m.sb("ots", [P, 4, P])
        psS = m.ps("psS", [P, 4, BANK])
        psT = m.ps("psT", [P, 2, BANK])
        psO = m.ps("psO", [P, BANK])
        psW = m.ps("psW", [P, BANK])
        k = sems
        off = w.prob_offset
        block = ctx.enter_context(nc.Block())

        def S_of(h):
            return psS[:, h // 2, (h % 2) * BANDK:(h % 2 + 1) * BANDK]

        @block.gpsimd
        def _(pool):
            if w.zero_queries:
                pool.memset(qs[:], 0.0).then_inc(k.qs_zeroed, 1)
                wait_apart(pool, k.qs_zeroed, 1, w.run)

            def stage(u, s):
                wait_apart(pool, k.scored, 2 * (u - 1), 2 * base)
                wait_apart(pool, k.exped, 4 * (u - 1), 4 * base)
                w.stage(pool, u, s, qs, scs, k.staged)

            pipeline(pool, U, [(stage, 0)])

        @block.tensor
        def _(pe):
            def score(u, s, half):
                pe.wait_ge(k.staged, w.stage_incs * (u + 1) + w.stage_incs * base)
                wait(pe, k.masked, 2 * (u - 1) + half + 1, 2 * base)
                for h in range(4 * half, 4 * half + 4):
                    last = pe.matmul(S_of(h), qs[:, s, h, :], w.keys(u, s, h), start=True, stop=True)
                last.then_inc(k.scored, 1)

            def turn(u, s, q):
                pe.wait_ge(k.exped, 4 * u + q + 1 + 4 * base)
                wait(pe, (k.evac_act, k.evac_dve)[q % 2], 2 * u + q // 2, 2 * base)
                for j in range(4):
                    h, b = 2 * q + j // 2, j % 2
                    last = pe.transpose(psT[:, q % 2, j * P:(j + 1) * P],
                                        probs[:, s, h, b * P:(b + 1) * P], g.ident[:])
                last.then_inc(k.transposed, 1)

            def weigh(u, s, q):
                pe.wait_ge((k.evac_act, k.evac_dve)[q % 2], 2 * u + q // 2 + 1 + 2 * base)
                if q == 0:
                    wait(pe, k.normed, u, base)
                for h in (2 * q, 2 * q + 1):
                    for b in range(2):
                        last = pe.matmul(psO[:, h * hd:(h + 1) * hd],
                                         pts[:, q, ((h % 2) * 2 + b) * P:((h % 2) * 2 + b + 1) * P],
                                         w.vals(u, s, h, b), start=b == 0, stop=b == 1)
                last.then_inc(k.weighed, 1)

            nout = w.out_tiles

            def turn_out(u, s):
                pe.wait_ge(k.normed, u + 1 + base)
                wait(pe, k.finished, u, base)
                for j in range(nout):
                    last = pe.transpose(psW[:, j * P:(j + 1) * P], on[:, s, j * P:(j + 1) * P], g.ident[:])
                last.then_inc(k.turned, 1)

            def project(u, s):
                pe.wait_ge(k.turned_kept, u + 1 + base)
                for j in range(nout):
                    last = pe.matmul(psW[:, 0:D], ots[:, j, :], w.wo[:, j, :], start=j == 0, stop=j == nout - 1)
                last.then_inc(k.projected, 1)

            def C(half, lag):
                return lambda u, s: score(u, s, half), lag

            def T(q, lag):
                return lambda u, s: turn(u, s, q), lag

            def W(q, lag):
                return lambda u, s: weigh(u, s, q), lag

            if w.wo is None:
                order = [T(3, 3), W(1, 3), T(0, 2), (turn_out, 5), W(2, 3), C(0, 1), W(3, 3), T(1, 2),
                         C(1, 1), T(2, 2), W(0, 2)]
            else:
                order = [T(3, 3), W(1, 3), W(2, 3), C(0, 1), W(3, 3), T(0, 2), T(1, 2), C(1, 1),
                         (turn_out, 3), T(2, 2), W(0, 2), (project, 3)]
            pipeline(pe, U, order, tail=w.tail)

        @block.vector
        def _(dve):
            empty = slice(0, off) if off else slice(BANDK, 2 * P)
            dve.memset(probs[:, :, :, empty], 0.0).then_inc(k.probs_zeroed, 1)
            if on_width > 8 * hd:
                dve.memset(on[:], 0.0).then_inc(k.on_zeroed, 1)
                dve.wait_ge(k.on_zeroed, 1)

            def evac(u, s, q):
                dve.wait_ge(k.transposed, 4 * u + q + 1 + 4 * base)
                wait(dve, k.weighed, 4 * (u - 1) + q + 1, 4 * base)
                dve.tensor_copy(pts[:, q, :], psT[:, 1, :]).then_inc(k.evac_dve, 1)

            def mask(u, s, half):
                dve.wait_ge(k.scored, 2 * u + half + 1 + 2 * base)
                wait(dve, k.exped, 4 * (u - 2) + 2 * half + 2, 4 * base)
                out4 = masked[:, s, 4 * half:4 * half + 4].rearrange("p (b h) n -> p b h n", b=2)
                in4 = psS[:, 2 * half:2 * half + 2, 0:2 * BANDK].rearrange("p b (h n) -> p b h n", h=2)
                w.mask(dve, u, s, half, out4, in4, masked[:, s, 4 * half:4 * half + 4], k.masked)

            def bias(u, s, half):
                cut = slice(4 * half, 4 * half + 4)
                dve.wait_ge(k.masked, 2 * u + half + 1 + 2 * base)
                dve.tensor_reduce(mx[:, s, cut], masked[:, s, cut], axis=AX.X, op=ALU.max).then_inc(k.maxed, 1)
                dve.wait_ge(k.maxed, 2 * u + half + 1 + 2 * base)
                if w.scaled:
                    dve.wait_ge(k.staged, w.stage_incs * (u + 1) + w.stage_incs * base)
                    dve.scalar_tensor_tensor(nb[:, s, cut], mx[:, s, cut], -1.0, scs[:, s, cut], ALU.mult, ALU.mult)\
                       .then_inc(k.biased, 1)
                else:
                    dve.tensor_scalar(nb[:, s, cut], mx[:, s, cut], -1.0, None, ALU.mult).then_inc(k.biased, 1)

            def recip(u, s):
                dve.wait_ge(k.exped, 4 * u + 4 + 4 * base)
                wait(dve, k.normed, u - 1, base)
                dve.reciprocal(rs[:, s, :], sums[:, s, :]).then_inc(k.recip, 1)

            def norm(u, s):
                dve.wait_ge(k.recip, u + 1 + base)
                dve.wait_ge(k.weighed, 4 * u + 4 + 4 * base)
                wait(dve, k.turned, u - 1, base)
                at = w.out_column(s)
                dve.tensor_tensor(on[:, s, at:at + 8 * hd].rearrange("p (h d) -> p h d", h=8),
                                  psO[:, 0:8 * hd].rearrange("p (h d) -> p h d", h=8),
                                  bc(rs[:, s, :], 2, hd), ALU.mult).then_inc(k.normed, 1)

            def finish(u, s):
                w.finish(dve, u, s, psW, k, base)

            def M(half, lag):
                return lambda u, s: mask(u, s, half), lag

            def X(half, lag):
                return lambda u, s: bias(u, s, half), lag

            def V(half, lag):
                return lambda u, s: evac(u, s, 2 * half + 1), lag

            if w.wo is None:
                order = [V(1, 2), M(0, 0), (recip, 2), (norm, 2), X(0, 0), V(0, 1), M(1, 0), X(1, 0)]
            else:
                order = [M(1, 1), X(1, 1), V(1, 2), (finish, 3), M(0, 0), (norm, 2), X(0, 0), (recip, 1),
                         V(0, 1)]
            pipeline(dve, U, order, tail=w.tail)

        @block.scalar
        def _(act):
            act.wait_ge(k.probs_zeroed, 1 + w.run)

            def evac(u, s, q):
                act.wait_ge(k.transposed, 4 * u + q + 1 + 4 * base)
                wait(act, k.weighed, 4 * (u - 1) + q + 1, 4 * base)
                act.copy(pts[:, q, :], psT[:, 0, :]).then_inc(k.evac_act, 1)

            def exp(u, s, q):
                act.wait_ge(k.biased, 2 * u + q // 2 + 1 + 2 * base)
                if q == 0:
                    wait(act, k.transposed, 4 * (u - 1), 4 * base)
                    wait(act, k.recip, u - 1, base)
                for h in (2 * q, 2 * q + 1):
                    last = act.activation(probs[:, s, h, off:off + BANDK], masked[:, s, h, :], ACT.Exp,
                                          bias=nb[:, s, h:h + 1],
                                          scale=scs[:, s, h:h + 1] if w.scaled else 1.0,
                                          accum_out=sums[:, s, h:h + 1])
                last.then_inc(k.exped, 1)

            def keep(u, s):
                act.wait_ge(k.turned, u + 1 + base)
                w.keep_turned(act, u, s, psW, ots, k, base)

            def A(half, lag):
                return lambda u, s: evac(u, s, 2 * half), lag

            def E(q, lag):
                return lambda u, s: exp(u, s, q), lag

            if w.wo is None:
                order = [E(2, 1), A(0, 1), E(3, 1), E(0, 0), (keep, 4), A(1, 1), E(1, 0)]
            else:
                order = [(keep, 3), E(0, 1), A(1, 2), E(1, 1), E(2, 1), E(3, 1), A(0, 1)]
            pipeline(act, U, order, tail=w.tail)


class BandSems:

    def __init__(self, sem):
        self.qs_zeroed = sem("qs_zeroed")
        self.probs_zeroed = sem("probs_zeroed")
        self.on_zeroed = sem("on_zeroed")
        self.staged = sem("staged")
        self.scored = sem("scored")
        self.masked = sem("masked")
        self.maxed = sem("maxed")
        self.biased = sem("biased")
        self.exped = sem("exped")
        self.transposed = sem("transposed")
        self.evac_act = sem("evac_act")
        self.evac_dve = sem("evac_dve")
        self.weighed = sem("weighed")
        self.recip = sem("recip")
        self.normed = sem("normed")
        self.turned = sem("turned")
        self.turned_kept = sem("turned_kept")
        self.projected = sem("projected")
        self.added = sem("added")
        self.finished = sem("finished")


def a_project_phase(nc, g, hT, weights, ahead):
    with ExitStack() as ctx:
        m = Space(nc, ctx, "ap")
        w5, cols, rows = weights
        hs = m.sb("hs", [P, 2, 2, P])
        kb = m.sb("kb", [P, 2, D])
        kneg = m.sb("kneg", [P, 2, D])
        kexp = m.sb("kexp", [P, 2, D])
        kf = m.sb("kf", [P, 2, D])
        vb = m.sb("vb", [P, 2, D + 2])
        qb = m.sb("qb", [P, 2, BANK])
        qneg = m.sb("qneg", [P, 2, BANK])
        qexp = m.sb("qexp", [P, 2, BANK])
        psKV = m.ps("psKV", [P, 2, BANK])
        psV = m.ps("psV", [P, 2, BANK])
        psA = m.ps("psA", [P, BANK])
        psQ = m.ps("psQ", [P, 3, BANK])
        ahead_loaded = m.sem("ahead_loaded")
        staged, kv_done, v_done = m.sem("staged"), m.sem("kv_done"), m.sem("v_done")
        biased, kexped, featured, summed = m.sem("biased"), m.sem("kexped"), m.sem("featured"), m.sem("summed")
        v_kept, ones_set, kneg_done = m.sem("v_kept"), m.sem("ones_set"), m.sem("kneg_done")
        q_done, q_evac, qneg_done, qexped, q_kept = (m.sem("q_done"), m.sem("q_evac"), m.sem("qneg_done"),
                                                     m.sem("qexped"), m.sem("q_kept"))
        block = ctx.enter_context(nc.Block())
        n_v = NT + 2

        @block.sync
        def _(sp):
            for dst, src in ahead:
                sp.dma_start(dst, src).then_inc(ahead_loaded, 16)
            sp.wait_ge(ahead_loaded, 16 * len(ahead))

        @block.gpsimd
        def _(pool):
            pool.memset(vb[:], 1.0).then_inc(ones_set, 1)

            def stage(t, s):
                wait_apart(pool, v_done, t - 1)
                wait_apart(pool, kv_done, t - 1)
                pool.tensor_copy(hs[:, s, 0, :], hT[:, bass.ds(t * P + HALO_A, P)]).then_inc(staged, 1)
                pool.tensor_copy(hs[:, s, 1, :], hT[:, bass.ds(t * P, P)]).then_inc(staged, 1)

            pipeline(pool, n_v, [(stage, 0)])

        @block.tensor
        def _(pe):
            def project(t, s):
                pe.wait_ge(staged, 2 * t + 2)
                wait(pe, biased, 2 * (t - 1))
                wait(pe, v_kept, t - 1)
                pe.matmul(psKV[:, s, 0:2 * D], hs[:, s, 0, :], w5[:, 0:2, :], start=True, stop=True).then_inc(kv_done, 1)
                pe.matmul(psV[:, s, 0:D], hs[:, s, 1, :], w5[:, 2, :], start=True, stop=True).then_inc(v_done, 1)

            def accumulate(t, s):
                if isinstance(t, int) and t >= NT:
                    return
                pe.wait_ge(featured, t + 1)
                first = isinstance(t, int) and t == 0
                last = isinstance(t, int) and t == NT - 1
                pe.matmul(psA[:, 0:D + 1], kf[:, s, :], vb[:, s, 0:D + 1], start=first, stop=last).then_inc(summed, 1)

            pipeline(pe, n_v, [(accumulate, 2), (project, 0)], tail=4)
            for c in range(S // BANK):
                for j in range(3):
                    wait(pe, q_evac, 3 * (c - 1) + j + 1)
                    pe.matmul(psQ[:, j, :], w5[:, 3 + j, :], hT[:, HALO_A + c * BANK:HALO_A + (c + 1) * BANK],
                              start=True, stop=True).then_inc(q_done, 1)

        @block.vector
        def _(dve):
            dve.wait_ge(ones_set, 1)

            def bias(t, s):
                dve.wait_ge(kv_done, t + 1)
                wait(dve, summed, t - 1)
                wait(dve, kexped, t - 1)
                wait(dve, featured, t - 1)
                dve.tensor_tensor(kb[:, s, :], psKV[:, s, 0:D], rows[:, 0, :], ALU.add).then_inc(biased, 1)
                dve.tensor_tensor(vb[:, s, 0:D], psKV[:, s, D:2 * D], rows[:, 1, :], ALU.add).then_inc(biased, 1)
                dve.wait_ge(v_done, t + 1)
                dve.tensor_tensor(g.vloc[:, t, :], psV[:, s, 0:D], rows[:, 2, :], ALU.add).then_inc(v_kept, 1)
                dve.wait_ge(biased, 2 * t + 2)
                dve.tensor_scalar(kneg[:, s, :], kb[:, s, :], 0.0, None, ALU.min).then_inc(kneg_done, 1)

            def feature(t, s):
                dve.wait_ge(kexped, t + 1)
                wait(dve, summed, t - 1)
                dve.scalar_tensor_tensor(kf[:, s, :], kb[:, s, :], 0.0, kexp[:, s, :], ALU.max, ALU.add)\
                   .then_inc(featured, 1)

            pipeline(dve, n_v, [(feature, 1), (bias, 0)], tail=4)
            dve.wait_ge(summed, NT)
            dve.tensor_copy(g.KV[:], psA[:, 0:D]).then_inc(biased, 1)
            dve.tensor_copy(g.KS[:], psA[:, D:D + 1].broadcast_to([P, P])).then_inc(biased, 1)

            def negative(c, s):
                dve.wait_ge(q_evac, 3 * c + 3)
                wait(dve, qexped, c - 1)
                dve.tensor_scalar(qneg[:, s, :], qb[:, s, :], 0.0, None, ALU.min).then_inc(qneg_done, 1)

            def query_feature(c, s):
                dve.wait_ge(qexped, c + 1)
                dve.scalar_tensor_tensor(g.qlinT[:, c * BANK:(c + 1) * BANK], qb[:, s, :], 0.0, qexp[:, s, :],
                                         ALU.max, ALU.add).then_inc(q_kept, 1)

            pipeline(dve, S // BANK, [(query_feature, 1), (negative, 0)])

        @block.scalar
        def _(act):
            def exp(t, s):
                act.wait_ge(kneg_done, t + 1)
                wait(act, featured, t - 1)
                act.activation(kexp[:, s, :], kneg[:, s, :], ACT.Exp).then_inc(kexped, 1)

            pipeline(act, n_v, [(exp, 0)])

            def evacuate(c, s):
                act.wait_ge(q_done, 3 * c + 3)
                act.activation(g.qlocT[:, c * BANK:(c + 1) * BANK], psQ[:, 0, :], ACT.Identity,
                               bias=cols[:, 0:1]).then_inc(q_evac, 1)
                act.activation(g.klocT[:, HALO_A + c * BANK:HALO_A + (c + 1) * BANK], psQ[:, 1, :], ACT.Identity,
                               bias=cols[:, 1:2]).then_inc(q_evac, 1)
                wait(act, q_kept, c - 1)
                act.activation(qb[:, s, :], psQ[:, 2, :], ACT.Identity, bias=cols[:, 2:3]).then_inc(q_evac, 1)

            def query_exp(c, s):
                act.wait_ge(qneg_done, c + 1)
                act.activation(qexp[:, s, :], qneg[:, s, :], ACT.Exp).then_inc(qexped, 1)

            pipeline(act, S // BANK, [(query_exp, 1), (evacuate, 0)])


def a_window(nc, g, dram, ctx):
    m = Space(nc, ctx, "aw")
    w = Names()
    w.units, w.hd, w.run, w.tail = 2 * NT, A_HD, 0, 4
    w.prob_offset, w.zero_queries, w.scaled = 0, False, False
    w.stage_incs, w.out_tiles = 1, 1
    w.wo, w.finish = None, None
    w.out_column = lambda s: s * 8 * A_HD
    half = lambda u, s: (u - s) // 2 if isinstance(u, int) else (u - s) >> 1
    scale = float(np.float32(1.0 / np.sqrt(A_HD)))
    edge_done, tile_taken = m.sem("edge_done"), m.sem("tile_taken")
    tile = m.sb("tile", [P, 2, P])

    def stage(pool, u, s, qs, scs, staged):
        pool.tensor_copy(tile[:, s, :], g.qlocT[:, bass.ds(half(u, s) * P, P)]).then_inc(tile_taken, 1)
        wait_apart(pool, tile_taken, u + 1)
        pool.tensor_tensor(qs[:, s], bc(tile[:, s, :], 1, 8), bc(g.hmask[:, 8 * s:8 * s + 8], 2, P), ALU.mult).then_inc(staged, 1)

    def mask(dve, u, s, half_, out4, in4, out, masked):
        o = out.rearrange("p (b h) n -> p b (h n)", b=2)
        i = in4.rearrange("p b h n -> p b (h n)")
        at = 8 * s + 4 * half_
        b = g.relb[:, at:at + 4, :].rearrange("p (b h) n -> p b (h n)", b=2)
        edge = isinstance(u, int) and (u < 2 or u >= 2 * NT - 2)
        ins = dve.scalar_tensor_tensor(o, i, scale, b, ALU.mult, ALU.add)
        if edge:
            ins.then_inc(edge_done, 1)
            wait(dve, edge_done, 2 * (u if u < 2 else u - (2 * NT - 2) + 2) + half_ + 1)
            e = g.edge[:, 0 if u < 2 else 1, :]
            ins = dve.tensor_tensor(out, out, bc(e, 1, 4), ALU.add)
        ins.then_inc(masked, 1)

    def keep_turned(act, u, s, psW, ots, k, base):
        act.copy(g.winT[64 * s:64 * s + 64, bass.ds(half(u, s) * P, P)], psW[64 * s:64 * s + 64, 0:P]).then_inc(k.finished, 1)

    w.stage, w.mask, w.keep_turned = stage, mask, keep_turned
    w.keys = lambda u, s, h: g.klocT[:, bass.ds(half(u, s) * P, BANDK)]
    w.vals = lambda u, s, h, b: g.vloc[:, half(u, s) + b, (8 * s + h) * A_HD:(8 * s + h + 1) * A_HD]
    return w


def a_gate_phase(nc, g, hT, weights):
    with ExitStack() as ctx:
        m = Space(nc, ctx, "ag")
        wg1, wg2, wo, cols, bo = weights
        nbg2 = m.sb("nbg2", [P, 1])
        den = m.sb("den", [P, BANK])
        rden = m.sb("rden", [P, BANK])
        lin = m.sb("lin", [P, 2, BANK])
        g1 = m.sb("g1", [P, BANK])
        eg = m.sb("eg", [P, 2, BANK])
        e1 = m.sb("e1", [P, BANK])
        gate = m.sb("gate", [P, BANK])
        diff = m.sb("diff", [P, 2, BANK])
        gd = m.sb("gd", [P, BANK])
        mix = m.sb("mix", [P, 2, BANK])
        res = m.sb("res", [P, 4, D])
        psN = m.ps("psN", [P, 2, BANK])
        psD = m.ps("psD", [P, 2, BANK])
        psG = m.ps("psG", [P, BANK])
        psH = m.ps("psH", [P, BANK])
        psY = m.ps("psY", [P, BANK])
        bias_negated = m.sem("bias_negated")
        sums_done, quotient_step, lin_done = m.sem("sums_done"), m.sem("quotient_step"), m.sem("lin_done")
        diff_done, gate_in_done, relu_done = m.sem("diff_done"), m.sem("gate_in_done"), m.sem("relu_done")
        gate_out_done, exp_done, mix_step = m.sem("gate_out_done"), m.sem("exp_done"), m.sem("mix_step")
        mix_done, y_done, bo_added, x_updated = m.sem("mix_done"), m.sem("y_done"), m.sem("bo_added"), m.sem("x_updated")
        block = ctx.enter_context(nc.Block())
        NC = S // BANK

        @block.tensor
        def _(pe):
            def sums(c, s):
                cut = slice(c * BANK, (c + 1) * BANK)
                wait(pe, lin_done, c - 1)
                pe.matmul(psN[:, s, :], g.KV[:], g.qlinT[:, cut], start=True, stop=True)
                pe.matmul(psD[:, s, :], g.KS[:], g.qlinT[:, cut], start=True, stop=True).then_inc(sums_done, 1)

            def gate_in(c, s):
                cut = slice(c * BANK, (c + 1) * BANK)
                wait(pe, relu_done, c)
                pe.matmul(psG[:], wg1[:, 1, :], g.winT[:, cut], start=True, stop=False)
                pe.matmul(psG[:], wg1[:, 2, :], hT[:, HALO_A + c * BANK:HALO_A + (c + 1) * BANK], start=False, stop=False)
                pe.wait_ge(lin_done, c + 1)
                pe.matmul(psG[:], wg1[:, 0, :], lin[:, s, :], start=False, stop=True).then_inc(gate_in_done, 1)

            def gate_out(c, s):
                pe.wait_ge(relu_done, c + 1)
                wait(pe, exp_done, c)
                pe.matmul(psH[:], wg2[:], g1[:], start=True, stop=True).then_inc(gate_out_done, 1)

            def project(c, s):
                pe.wait_ge(mix_done, c + 1)
                wait(pe, bo_added, c)
                for j in range(4):
                    last = pe.matmul(psY[:, j * D:(j + 1) * D], mix[:, s, j * P:(j + 1) * P], wo[:], start=True, stop=True)
                last.then_inc(y_done, 1)

            pipeline(pe, NC, [(sums, 0), (gate_in, 1), (project, 2), (gate_out, 1)])

        @block.scalar
        def _(act):
            act.wait_ge(bias_negated, 1)

            def gates(c, s):
                act.wait_ge(gate_in_done, c + 1)
                act.activation(g1[:], psG[:], ACT.Relu, bias=cols[:, 0:1]).then_inc(relu_done, 1)
                act.wait_ge(gate_out_done, c + 1)
                wait(act, mix_done, c - 1)
                act.activation(eg[:, s, :], psH[:], ACT.Exp, bias=nbg2[:], scale=-1.0).then_inc(exp_done, 1)

            pipeline(act, NC, [(gates, 1)])

        @block.vector
        def _(dve):
            dve.tensor_scalar(nbg2[:], cols[:, 1:2], -1.0, None, ALU.mult).then_inc(bias_negated, 1)

            def quotient(c, s):
                dve.wait_ge(sums_done, c + 1)
                wait(dve, gate_in_done, c - 1)
                dve.tensor_scalar(den[:], psD[:, s, :], 1e-6, None, ALU.add).then_inc(quotient_step, 1)
                dve.wait_ge(quotient_step, 2 * c + 1)
                dve.reciprocal(rden[:], den[:]).then_inc(quotient_step, 1)
                dve.wait_ge(quotient_step, 2 * c + 2)
                dve.tensor_tensor(lin[:, s, :], psN[:, s, :], rden[:], ALU.mult).then_inc(lin_done, 1)
                dve.wait_ge(lin_done, c + 1)
                dve.tensor_tensor(diff[:, s, :], lin[:, s, :], g.winT[:, c * BANK:(c + 1) * BANK], ALU.subtract)\
                   .then_inc(diff_done, 1)

            def mixed(c, s):
                dve.wait_ge(exp_done, c + 1)
                dve.tensor_scalar(e1[:], eg[:, s, :], 1.0, None, ALU.add).then_inc(mix_step, 1)
                dve.wait_ge(mix_step, 3 * c + 1)
                dve.reciprocal(gate[:], e1[:]).then_inc(mix_step, 1)
                dve.wait_ge(mix_step, 3 * c + 2)
                dve.wait_ge(diff_done, c + 1)
                dve.tensor_tensor(gd[:], gate[:], diff[:, s, :], ALU.mult).then_inc(mix_step, 1)
                dve.wait_ge(mix_step, 3 * c + 3)
                wait(dve, y_done, c - 1)
                dve.tensor_tensor(mix[:, s, :], gd[:], g.winT[:, c * BANK:(c + 1) * BANK], ALU.add).then_inc(mix_done, 1)

            def add(c, s):
                dve.wait_ge(y_done, c + 1)
                wait(dve, x_updated, c)
                dve.tensor_tensor(res[:], psY[:].rearrange("p (t d) -> p t d", t=4), bc(bo[:], 1, 4), ALU.add)\
                   .then_inc(bo_added, 1)
                dve.wait_ge(bo_added, c + 1)
                dve.tensor_tensor(g.x[:, 4 * c:4 * c + 4, :], g.x[:, 4 * c:4 * c + 4, :], res[:], ALU.add)\
                   .then_inc(x_updated, 1)

            pipeline(dve, NC, [(quotient, 0), (add, 2), (mixed, 1)])


def attention_a(nc, g, dram, tables):
    with ExitStack() as ctx:
        m = Space(nc, ctx, "a")
        z = m.sb("z", [P, NT, D])
        hT = m.sb("hT", [P, (NT + 2) * P + HALO_A + 96])
        g.vloc = m.sb("vloc", [P, NT + 2, D])
        g.qlocT = m.sb("qlocT", [P, S])
        g.klocT = m.sb("klocT", [P, HALO_A + S + BANDK])
        g.qlinT = m.sb("qlinT", [P, S])
        g.winT = m.sb("winT", [P, S])
        g.KV = m.sb("KV", [P, D])
        g.KS = m.sb("KS", [P, P])
        g.relb = m.sb("relb", [P, A_HEADS, BANDK])
        g.edge = m.sb("edge", [P, 2, BANDK])
        g.hmask = m.sb("hmask", [P, A_HEADS])
        ln = m.sb("ln", [P, 2])
        loaded, padded = m.sem("loaded"), m.sem("padded")
        with nc.Block() as block:
            loads = [(ln[:, 0:1], dram["ln_g"].unsqueeze(1)), (ln[:, 1:2], dram["ln_b"].unsqueeze(1))]

            @block.sync
            def _(sp):
                for dst, src in loads:
                    sp.dma_start(dst, src).then_inc(loaded, 16)
                sp.wait_ge(loaded, 16 * len(loads))

            @block.gpsimd
            def _(pool):
                pool.memset(hT[:, 0:HALO_A], 0.0)
                pool.memset(hT[:, HALO_A + S:], 0.0)
                pool.memset(g.klocT[:, 0:HALO_A], 0.0)
                pool.memset(g.klocT[:, HALO_A + S:], 0.0).then_inc(padded, 1)

        norm_phase(nc, "anz", g.x, z, g)
        w5 = m.sb("w5", [P, 6, D])
        cols = m.sb("cols", [P, 3])
        rows = m.sb("rows", [P, 3, D])
        loads = [(w5[:, i, :], dram[n]) for i, n in enumerate(
            ["wk_lin", "wv_lin", "wv_loc", "wq_loc", "wk_loc", "wq_lin"])]
        loads += [(cols[:, i:i + 1], dram[n].unsqueeze(1)) for i, n in enumerate(["bq_loc", "bk_loc", "bq_lin"])]
        loads += [(rows[:, i, :], dram[n].partition_broadcast(P)) for i, n in enumerate(["bk_lin", "bv_lin", "bv_loc"])]
        norm_phase(nc, "anh", z, g.vloc, g, (hT, ln[:, 0:1], ln[:, 1:2], HALO_A), loads=loads,
                   loaded=m.sem("project_loaded"))
        wg1 = m.sb("wg1", [P, 3, D])
        wg2 = m.sb("wg2", [P, D])
        wo = m.sb("wo", [P, D])
        gate_cols = m.sb("gate_cols", [P, 2])
        bo = m.sb("bo", [P, D])
        ahead = [(g.hmask[:], dram["hmask"]), (g.edge[:], dram["edge"]), (g.relb[:], dram["relb"]),
                 (wg1[:], dram["wg1"].rearrange("(c p) n -> p c n", p=P)), (wg2[:], dram["wg2"]), (wo[:], dram["wo"]),
                 (gate_cols[:, 0:1], dram["bg1"].unsqueeze(1)), (gate_cols[:, 1:2], dram["bg2"].unsqueeze(1)),
                 (bo[:], dram["bo"].partition_broadcast(P))]
        a_project_phase(nc, g, hT, (w5, cols, rows), ahead + tables)
        add_phase(nc, "axz", g.x, z)
        k = BandSems(sem_maker(nc, "awk"))
        band_phase(nc, "awb", g, a_window(nc, g, dram, ctx), k, 0)
        a_gate_phase(nc, g, hT, (wg1, wg2, wo, gate_cols, bo))


def f_first_loads(g, dram, layer):
    one = bass.ds(layer, 1)
    h = F_HD // 2
    loads = [(g.wqkv[:], dram["wqkv"][one][0])]
    for j, name in enumerate(["q_scale", "k_scale"]):
        scales = dram[name][one][0]
        loads.append((g.sc4[:, j, :], scales.partition_broadcast(P)))
        loads.append((g.sc4[:, 2 + j, 0:h], scales[h:F_HD].partition_broadcast(P)))
        loads.append((g.sc4[:, 2 + j, h:F_HD], scales[0:h].partition_broadcast(P)))
    return loads


def f_later_loads(g, dram, layer):
    one = bass.ds(layer, 1)
    loads = [(g.fwo[:], dram["fwo"][one][0].rearrange("(c p) n -> p c n", p=P)), (g.w1[:], dram["w1"][one][0]),
             (g.lnc[:, 0:1], dram["fln_g"][one].rearrange("a p -> p a")),
             (g.lnc[:, 1:2], dram["fln_b"][one].rearrange("a p -> p a")),
             (g.b2[:], dram["b2"][one][0].partition_broadcast(P))]
    for c, (at, n) in enumerate(HID_CUTS):
        loads.append((g.w2[0:n, c, :], dram["w2"][one][0, at:at + n]))
        for j in range(2):
            loads.append((g.b1[0:n, 3 * j + c:3 * j + c + 1],
                          dram["b1"][one][0, HID * j + at:HID * j + at + n].unsqueeze(1)))
    return loads


class QkvSems:

    def __init__(self, sem):
        self.y_staged = sem("y_staged")
        self.yT_done = sem("yT_done")
        self.hT_ready = sem("hT_ready")
        self.qkv_done = sem("qkv_done")
        self.raw_ready = sem("raw_ready")
        self.v_ready = sem("v_ready")
        self.sq_ready = sem("sq_ready")
        self.ss_done = sem("ss_done")
        self.rot_part = sem("rot_part")
        self.rot_done = sem("rot_done")
        self.tab_ready = sem("tab_ready")
        self.ss_clipped = sem("ss_clipped")
        self.rn_done = sem("rn_done")
        self.k_scaled = sem("k_scaled")
        self.turned = sem("turned")
        self.q_kept = sem("q_kept")
        self.k_kept = sem("k_kept")
        self.padded = sem("padded")


class MlpSems:

    def __init__(self, sem):
        self.y_staged = sem("y_staged")
        self.yT_done = sem("yT_done")
        self.hT_ready = sem("hT_ready")
        self.h_back = sem("h_back")
        self.stats_done = sem("stats_done")
        self.mv_done = sem("mv_done")
        self.eps_added = sem("eps_added")
        self.rstd_done = sem("rstd_done")
        self.normed = sem("normed")
        self.hnT_done = sem("hnT_done")
        self.hnT_ready = sem("hnT_ready")
        self.up_done = sem("up_done")
        self.gelued = sem("gelued")
        self.gated = sem("gated")
        self.down_done = sem("down_done")
        self.b2_added = sem("b2_added")
        self.added = sem("added")


def shifted_copy(act, hT, psT, s, t, zcol, hT_ready, base):
    lo, hi = slice(0, D // 2), slice(D // 2, D)
    act.copy(hT[lo, s, 0:P], psT[lo, 0:P]).then_inc(hT_ready, 1)
    act.copy(hT[hi, s, 1:P + 1], psT[hi, 0:P]).then_inc(hT_ready, 1)
    if isinstance(t, int) and t == 0:
        act.copy(hT[hi, s, 0:1], zcol[hi, :]).then_inc(hT_ready, 1)
    else:
        wait(act, hT_ready, 3 * t, 3 * base)
        act.copy(hT[hi, s, 0:1], hT[hi, 1 - s, P:P + 1]).then_inc(hT_ready, 1)


def f_qkv_phase(nc, prefix, g, k, run, loads, loaded):
    base = run * NT
    with ExitStack() as ctx:
        m = Space(nc, ctx, prefix)
        ys = m.sb("ys", [P, 2, D])
        hT = m.sb("hT", [P, 2, P + 1])
        raw = m.sb("raw", [P, 2, 2 * F_INNER])
        sq = m.sb("sq", [P, 2, 2 * F_INNER])
        ss = m.sb("ss", [P, 2, 2 * F_HEADS])
        ssc = m.sb("ssc", [P, 2 * F_HEADS])
        rn = m.sb("rn", [P, 2, 2 * F_HEADS])
        tabw = m.sb("tabw", [P, 2, 4, F_HD])
        part_c = m.sb("part_c", [P, 2 * F_INNER])
        part_s = m.sb("part_s", [P, 2 * F_INNER])
        rot = m.sb("rot", [P, 2, 2 * F_INNER])
        kn = m.sb("kn", [P, 2, F_INNER])
        psT = m.ps("psT", [P, BANK])
        psX = m.ps("psX", [P, 3, BANK])
        psR = m.ps("psR", [P, 2, 2, BANK])
        block = ctx.enter_context(nc.Block())
        H2 = F_HD // 2

        @block.sync
        def _(sp):
            for dst, src in loads:
                sp.dma_start(dst, src).then_inc(loaded, 16)

        @block.gpsimd
        def _(pool):
            pool.memset(g.KT[:, :, 0:HALO_F], 0.0)
            pool.memset(g.V[:, 0, :], 0.0).then_inc(k.padded, 1)

            def stage(t, s):
                wait_apart(pool, k.yT_done, t - 1, base)
                pool.tensor_copy(ys[:, s, :], g.y[:, t, :]).then_inc(k.y_staged, 1)

            def tables(t, s):
                wait_apart(pool, k.rot_part, 3 * (t - 1), 3 * base)
                pool.tensor_tensor(tabw[:, s], g.tab[:, t], g.sc4[:], ALU.mult).then_inc(k.tab_ready, 1)

            def norms(t, s):
                wait_apart(pool, k.ss_done, t + 1, base)
                wait_apart(pool, k.rn_done, 2 * t, 2 * base)
                wait_apart(pool, k.k_scaled, t - 1, base)
                pool.tensor_scalar(ssc[:], ss[:, s, :], 1e-24, None, ALU.max).then_inc(k.ss_clipped, 1)
                wait_apart(pool, k.ss_clipped, t + 1, base)
                pool.tensor_tensor(rn[:, s, :], ssc[:], bc(g.mhalf[:, 0], 1, 2 * F_HEADS), ALU.pow).then_inc(k.rn_done, 1)
                wait_apart(pool, k.rn_done, 2 * t + 1, 2 * base)
                pool.tensor_copy(g.qscale[:, t, :], rn[:, s, 0:F_HEADS]).then_inc(k.rn_done, 1)

            pipeline(pool, NT, [(stage, 0), (norms, 3), (tables, 1)])

        @block.tensor
        def _(pe):
            def turn_y(t, s):
                pe.wait_ge(k.y_staged, t + 1 + base)
                wait(pe, k.hT_ready, 3 * t, 3 * base)
                pe.transpose(psT[:, 0:P], ys[:, s, :], g.ident[:]).then_inc(k.yT_done, 1)

            def project(t, s):
                pe.wait_ge(k.hT_ready, 3 * t + 3 + 3 * base)
                wait(pe, k.raw_ready, t, base)
                wait(pe, k.v_ready, t, base)
                for c in range(3):
                    last = pe.matmul(psX[:, c, :], hT[:, s, 0:P], g.wqkv[:, c * BANK:(c + 1) * BANK],
                                     start=True, stop=True)
                last.then_inc(k.qkv_done, 1)

            def turn_qk(t, s):
                pe.wait_ge(k.rot_done, t + 1 + base)
                wait(pe, k.q_kept, t - 1, base)
                wait(pe, k.k_kept, t - 1, base)
                for j in range(4):
                    pe.transpose(psR[:, s, 0, j * P:(j + 1) * P], rot[:, s, j * P:(j + 1) * P], g.ident[:])
                pe.wait_ge(k.k_scaled, t + 1 + base)
                for j in range(4):
                    last = pe.transpose(psR[:, s, 1, j * P:(j + 1) * P], kn[:, s, j * P:(j + 1) * P], g.ident[:])
                last.then_inc(k.turned, 1)

            pipeline(pe, NT, [(turn_y, 1), (project, 2), (turn_qk, 4)])
            pe.wait_ge(loaded, 16 * len(loads) + 16 * len(loads) * run)

        @block.scalar
        def _(act):
            act.wait_ge(k.padded, 1 + run)

            def take_y(t, s):
                act.wait_ge(k.yT_done, t + 1 + base)
                wait(act, k.qkv_done, t - 1, base)
                shifted_copy(act, hT, psT, s, t, g.zcol, k.hT_ready, base)

            def take_qkv(t, s):
                act.wait_ge(k.qkv_done, t + 1 + base)
                wait(act, k.rot_part, 3 * (t - 1), 3 * base)
                act.copy(raw[:, s, :].rearrange("p (a n) -> p a n", a=2), psX[:, 0:2, :]).then_inc(k.raw_ready, 1)
                act.copy(g.V[:, t + 1, :], psX[:, 2, :]).then_inc(k.v_ready, 1)
                act.wait_ge(k.raw_ready, t + 1 + base)
                wait(act, k.ss_done, t - 1, base)
                act.activation(sq[:, s, :], raw[:, s, :], ACT.Square).then_inc(k.sq_ready, 1)

            def keep(t, s):
                act.wait_ge(k.turned, t + 1 + base)
                act.copy(g.QT[:, :, bass.ds(t * P, P)], psR[:, s, 0, :].rearrange("p (c n) -> p c n", c=4))\
                   .then_inc(k.q_kept, 1)
                act.copy(g.KT[:, :, bass.ds(t * P + HALO_F, P)], psR[:, s, 1, :].rearrange("p (c n) -> p c n", c=4))\
                   .then_inc(k.k_kept, 1)

            pipeline(act, NT, [(take_y, 1), (take_qkv, 2), (keep, 4)])

        @block.vector
        def _(dve):
            def sums(t, s):
                dve.wait_ge(k.sq_ready, t + 1 + base)
                wait(dve, k.rn_done, 2 * (t - 1), 2 * base)
                dve.tensor_reduce(ss[:, s, :], sq[:, s, :].rearrange("p (h d) -> p h d", d=F_HD),
                                  axis=AX.X, op=ALU.add).then_inc(k.ss_done, 1)

            def rotate(t, s):
                r4 = raw[:, s, :].rearrange("p (a h d) -> p a h d", a=2, h=F_HEADS)
                c4 = part_c[:].rearrange("p (a h d) -> p a h d", a=2, h=F_HEADS)
                s4 = part_s[:].rearrange("p (a h d) -> p a h d", a=2, h=F_HEADS)
                cos = bc(tabw[:, s, 0:2, :], 2, F_HEADS)
                sin = bc(tabw[:, s, 2:4, :], 2, F_HEADS)
                dve.wait_ge(k.tab_ready, t + 1 + base)
                wait(dve, k.rot_done, t, base)
                dve.tensor_tensor(c4, r4, cos, ALU.mult).then_inc(k.rot_part, 1)
                dve.tensor_tensor(s4[:, :, :, 0:H2], r4[:, :, :, H2:], sin[:, :, :, 0:H2], ALU.mult).then_inc(k.rot_part, 1)
                dve.tensor_tensor(s4[:, :, :, H2:], r4[:, :, :, 0:H2], sin[:, :, :, H2:], ALU.mult).then_inc(k.rot_part, 1)
                dve.wait_ge(k.rot_part, 3 * t + 3 + 3 * base)
                wait(dve, k.turned, t - 1, base)
                dve.tensor_tensor(rot[:, s, :], part_c[:], part_s[:], ALU.add).then_inc(k.rot_done, 1)

            def scale_k(t, s):
                dve.wait_ge(k.rn_done, 2 * t + 1 + 2 * base)
                dve.wait_ge(k.rot_done, t + 1 + base)
                wait(dve, k.turned, t - 1, base)
                dve.tensor_tensor(kn[:, s, :].rearrange("p (h d) -> p h d", h=F_HEADS),
                                  rot[:, s, F_INNER:].rearrange("p (h d) -> p h d", h=F_HEADS),
                                  bc(rn[:, s, F_HEADS:], 2, F_HD), ALU.mult).then_inc(k.k_scaled, 1)

            pipeline(dve, NT, [(sums, 2), (rotate, 2), (scale_k, 3)])


def f_window(g, k, run):
    w = Names()
    w.units, w.hd, w.run, w.tail = NT, F_HD, run, 0
    w.prob_offset, w.zero_queries, w.scaled = HALO_F, True, True
    w.stage_incs, w.out_tiles = 3, 4
    w.wo = g.fwo
    w.out_column = lambda s: 0

    def stage(pool, u, s, qs, scs, staged):
        q = g.QT[:, :, bass.ds(u * P, P)]
        pairs = qs[:, s].rearrange("p (c b) n -> p c b n", b=2)
        wait_apart(pool, staged, 3 * u, 3 * run * NT)
        pool.tensor_copy(scs[:, s, :], g.qscale[:, u, :]).then_inc(staged, 1)
        pool.tensor_copy(pairs[0:64, :, 0, :], q[0:64]).then_inc(staged, 1)
        wait_apart(pool, staged, 3 * u + 2, 3 * run * NT)
        pool.tensor_copy(pairs[64:128, :, 1, :], q[64:128]).then_inc(staged, 1)

    def mask(dve, u, s, half, out4, in4, out, masked):
        b = g.bandmask[:, 1 if isinstance(u, int) and u == 0 else 0, :]
        dve.tensor_tensor(out4, in4, bc(bc(b, 1, 2), 1, 2), ALU.add).then_inc(masked, 1)

    def keep_turned(act, u, s, psW, ots, k, base):
        wait(act, k.projected, u, base)
        act.copy(ots[:].rearrange("p c n -> p (c n)"), psW[:]).then_inc(k.turned_kept, 1)

    def finish(dve, u, s, psW, k, base):
        dve.wait_ge(k.projected, u + 1 + base)
        dve.tensor_tensor(g.y[:, u, :], g.y[:, u, :], psW[:, 0:D], ALU.add).then_inc(k.finished, 1)

    w.stage, w.mask, w.keep_turned, w.finish = stage, mask, keep_turned, finish
    w.keys = lambda u, s, h: g.KT[:, h // 2, bass.ds(u * P, BANDK)]
    w.vals = lambda u, s, h, b: g.V[:, u + b, h * F_HD:(h + 1) * F_HD]
    return w


def f_mlp_phase(nc, prefix, g, k, run, loads, loaded, times):
    base = run * NT
    with ExitStack() as ctx:
        m = Space(nc, ctx, prefix)
        ys = m.sb("ys", [P, 2, D])
        hT = m.sb("hT", [P, 2, P + 1])
        stats = m.sb("stats", [P, 2, 6])
        mv = m.sb("mv", [P, 2, 2])
        vare = m.sb("vare", [P, 1])
        rstd = m.sb("rstd", [P, 2])
        hn = m.sb("hn", [P, 2, D])
        hnT = m.sb("hnT", [P, 2, P])
        gg = m.sb("gg", [P, 2, 3, P])
        ug = m.sb("ug", [P, 2, 3, P])
        tmp = m.sb("tmp", [P, D])
        psA = m.ps("psA", [P, BANK])
        psB = m.ps("psB", [P, BANK])
        psC = m.ps("psC", [P, BANK])
        psU = m.ps("psU", [P, 2, 2, BANK])
        psF = m.ps("psF", [P, BANK])
        block = ctx.enter_context(nc.Block())

        @block.sync
        def _(sp):
            for dst, src in loads:
                sp.dma_start(dst, src).then_inc(loaded, 16)

        @block.gpsimd
        def _(pool):
            def stage(t, s):
                wait_apart(pool, k.yT_done, t - 1, base)
                pool.tensor_copy(ys[:, s, :], g.y[:, t, :]).then_inc(k.y_staged, 1)

            def spread(t, s):
                wait_apart(pool, k.mv_done, t + 1, base)
                wait_apart(pool, k.rstd_done, t, base)
                pool.tensor_scalar(vare[:], mv[:, s, 1:2], EPS, None, ALU.add).then_inc(k.eps_added, 1)
                wait_apart(pool, k.eps_added, t + 1, base)
                wait_apart(pool, k.normed, t - 1, base)
                pool.tensor_tensor(rstd[:, s:s + 1], vare[:], g.mhalf[:], ALU.pow).then_inc(k.rstd_done, 1)

            pipeline(pool, NT, [(stage, 0), (spread, 1)])

        @block.tensor
        def _(pe):
            def turn_y(t, s):
                pe.wait_ge(k.y_staged, t + 1 + base)
                wait(pe, k.hT_ready, 3 * t, 3 * base)
                pe.transpose(psA[:, 0:P], ys[:, s, :], g.ident[:]).then_inc(k.yT_done, 1)

            def turn_back(t, s):
                pe.wait_ge(k.hT_ready, 3 * t + 3 + 3 * base)
                wait(pe, k.normed, t, base)
                pe.transpose(psB[:, 0:P], hT[:, s, 0:P], g.ident[:]).then_inc(k.h_back, 1)

            def turn_norm(t, s):
                pe.wait_ge(k.normed, t + 1 + base)
                wait(pe, k.hnT_ready, t, base)
                pe.transpose(psC[:, 0:P], hn[:, s, :], g.ident[:]).then_inc(k.hnT_done, 1)

            def up(t, s):
                pe.wait_ge(k.hnT_ready, t + 1 + base)
                wait(pe, k.gated, 3 * (t - 1), 3 * base)
                for j in (1, 0):
                    for c, (at, n) in enumerate(HID_CUTS):
                        last = pe.matmul(psU[0:n, s, j, c * P:(c + 1) * P], g.w1[:, HID * j + at:HID * j + at + n],
                                         hnT[:, s, :], start=True, stop=True)
                last.then_inc(k.up_done, 1)

            def down(t, s):
                pe.wait_ge(k.gated, 3 * t + 3 + 3 * base)
                wait(pe, k.b2_added, t, base)
                for c, (at, n) in enumerate(HID_CUTS):
                    last = pe.matmul(psF[:, 0:D], ug[0:n, s, c, :], g.w2[0:n, c, :], start=c == 0, stop=c == 2)
                last.then_inc(k.down_done, 1)

            pipeline(pe, NT, [(turn_back, 1), (turn_y, 0), (turn_norm, 2), (up, 3), (down, 5)])
            pe.wait_ge(loaded, 16 * len(loads) * times)

        @block.scalar
        def _(act):
            def take_y(t, s):
                act.wait_ge(k.yT_done, t + 1 + base)
                wait(act, k.h_back, t - 1, base)
                shifted_copy(act, hT, psA, s, t, g.zcol, k.hT_ready, base)

            def take_norm(t, s):
                act.wait_ge(k.hnT_done, t + 1 + base)
                wait(act, k.up_done, t - 1, base)
                act.activation(hnT[:, s, :], psC[:, 0:P], ACT.Identity, bias=g.lnc[:, 1:2], scale=g.lnc[:, 0:1])\
                   .then_inc(k.hnT_ready, 1)

            def gelu(t, s):
                act.wait_ge(k.up_done, t + 1 + base)
                wait(act, k.gated, 3 * (t - 1), 3 * base)
                for c, (at, n) in enumerate(HID_CUTS):
                    act.activation(gg[0:n, s, c, :], psU[0:n, s, 1, c * P:(c + 1) * P], ACT.Gelu,
                                   bias=g.b1[0:n, 3 + c:4 + c]).then_inc(k.gelued, 1)

            pipeline(act, NT, [(take_y, 0), (take_norm, 2), (gelu, 3)])

        @block.vector
        def _(dve):
            def stats_of(t, s):
                dve.wait_ge(k.h_back, t + 1 + base)
                dve.bn_stats(stats[:, s, :], psB[:, 0:P]).then_inc(k.stats_done, 1)
                wait_apart(dve, k.stats_done, t + 1, base)
                dve.bn_aggr(mv[:, s, :], stats[:, s, :]).then_inc(k.mv_done, 1)

            def normalise(t, s):
                dve.wait_ge(k.rstd_done, t + 1 + base)
                wait(dve, k.hnT_done, t - 1, base)
                dve.tensor_scalar(hn[:, s, :], psB[:, 0:P], mv[:, s, 0:1], rstd[:, s:s + 1], ALU.subtract, ALU.mult)\
                   .then_inc(k.normed, 1)

            def gates(t, s):
                dve.wait_ge(k.gelued, 3 * t + 3 + 3 * base)
                wait(dve, k.down_done, t - 1, base)
                for c, (at, n) in enumerate(HID_CUTS):
                    dve.scalar_tensor_tensor(ug[0:n, s, c, :], psU[0:n, s, 0, c * P:(c + 1) * P],
                                             g.b1[0:n, c:c + 1], gg[0:n, s, c, :], ALU.add, ALU.mult)\
                       .then_inc(k.gated, 1)

            def finish(t, s):
                dve.wait_ge(k.down_done, t + 1 + base)
                wait(dve, k.added, t, base)
                dve.tensor_tensor(tmp[:], psF[:, 0:D], g.b2[:], ALU.add).then_inc(k.b2_added, 1)
                dve.wait_ge(k.b2_added, t + 1 + base)
                dve.tensor_tensor(g.y[:, t, :], g.y[:, t, :], tmp[:], ALU.add).then_inc(k.added, 1)

            pipeline(dve, NT, [(stats_of, 1), (finish, 6), (gates, 4), (normalise, 1)])


def ffn(nc, g, dram, app, k):
    with ExitStack() as ctx:
        m = Space(nc, ctx, f"f{app}")
        g.y = m.sb("y", [P, NT, D])
        g.V = m.sb("V", [P, NT + 1, F_INNER])
        g.QT = m.sb("QT", [P, 4, S])
        g.KT = m.sb("KT", [P, 4, HALO_F + S])
        g.qscale = m.sb("qscale", [P, NT, F_HEADS])
        g.wqkv = m.sb("wqkv", [P, 3 * F_INNER])
        g.fwo = m.sb("fwo", [P, 4, D])
        g.w1 = m.sb("w1", [P, 2 * HID])
        g.w2 = m.sb("w2", [P, 3, D])
        g.b1 = m.sb("b1", [P, 6])
        g.b2 = m.sb("b2", [P, D])
        g.lnc = m.sb("lnc", [P, 2])
        g.sc4 = m.sb("sc4", [P, 4, F_HD])
        first = f_first_loads(g, dram, 0)
        per_app = F_DEPTH + 1
        norm_phase(nc, f"f{app}n", g.x, g.y, g, loads=first, loaded=k.first_loaded,
                   loaded_before=16 * len(first) * per_app * app)
        with nc.Fori(0, F_DEPTH) as layer:
            run = layer + app * F_DEPTH
            f_qkv_phase(nc, f"f{app}q", g, k.qkv, run, f_later_loads(g, dram, layer), k.later_loaded)
            band_phase(nc, f"f{app}b", g, f_window(g, k.band, run), k.band, run * NT)
            f_mlp_phase(nc, f"f{app}m", g, k.mlp, run, f_first_loads(g, dram, (layer + 1) % F_DEPTH), k.first_loaded,
                        layer + per_app * app + 2)
        add_phase(nc, f"f{app}x", g.x, g.y)


class GroupSems:

    def __init__(self, sem):
        self.k_done = sem("k_done")
        self.kh_done = sem("kh_done")
        self.kl_done = sem("kl_done")
        self.v_done = sem("v_done")
        self.v_high = sem("v_high")
        self.v_kept = sem("v_kept")
        self.q_done = sem("q_done")
        self.q_kept = sem("q_kept")
        self.q_crossed = sem("q_crossed")
        self.q_taken = sem("q_taken")
        self.q_hi = sem("q_hi")
        self.q_top = sem("q_top")
        self.q_staged = sem("q_staged")
        self.scored = sem("scored")
        self.maxed = sem("maxed")
        self.biased = sem("biased")
        self.exped = sem("exped")
        self.transposed = sem("transposed")
        self.high_kept = sem("high_kept")
        self.low_kept = sem("low_kept")
        self.weighed = sem("weighed")
        self.summed = sem("summed")
        self.recip = sem("recip")
        self.out_kept = sem("out_kept")
        self.projected = sem("projected")
        self.added = sem("added")


def attention_b(nc, g, dram):
    with ExitStack() as ctx:
        m = Space(nc, ctx, "b")
        yT = m.sb("yT", [P, S])
        U = NT * B_HPG
        wk = m.sb("wk", [P, 2, B_HD])
        wv = m.sb("wv", [P, B_HD])
        wq = m.sb("wq", [P, B_HPG, B_HD])
        wp = m.sb("wp", [P, B_HPG, D])
        kh = m.sb("kh", [P, S], F32R)
        kl = m.sb("kl", [P, S], F32R)
        v = m.sb("v", [P, NT, 2, B_HD], F32R)
        qd = m.sb("qd", [P, U, P])
        loaded, wp_loaded = m.sem("loaded"), m.sem("wp_loaded")
        with ExitStack() as ctx_y:
            y = Space(nc, ctx_y, "by").sb("y", [P, NT, D])
            norm_phase(nc, "bn", g.x, y, g, (yT, None, None, 0), loads=b_group_loads(dram, 0, wk, wv, wq),
                       loaded=loaded)
            add_phase(nc, "bx", g.x, y)
        k = GroupSems(sem_maker(nc, "bk"))

        with nc.Fori(0, B_GROUPS) as grp:
            b_group_prepare(nc, g, dram, k, grp, wp_loaded, wk, wv, wq, wp, yT, kh, kl, v, qd)
            b_group_attend(nc, g, k, grp, kh, kl, v, qd, wp,
                           b_group_loads(dram, (grp + 1) % B_GROUPS, wk, wv, wq), loaded)


def b_group_loads(dram, grp, wk, wv, wq):
    kv_cols, q_cols = bass.ds(grp * B_HD, B_HD), bass.ds(grp * (B_HPG * B_HD), B_HPG * B_HD)
    loads = [(wk[:, i, :], dram["Wk"][:, kv_cols]) for i in range(2)] + [(wv[:], dram["Wv"][:, kv_cols])]
    loads += [(wq[:], dram["Wq"][:, q_cols].rearrange("p (h e) -> p h e", h=B_HPG))]
    return loads


def b_group_prepare(nc, g, dram, k, grp, wp_loaded, wk, wv, wq, wp, yT, kh, kl, v, qd):
    NC = S // BANK
    with ExitStack() as ctx:
        m = Space(nc, ctx, "bp")
        psK = m.ps("psK", [P, 2, BANK])
        psV = m.ps("psV", [P, 2, BANK])
        psQ = m.ps("psQ", [P, 4, BANK])
        block = ctx.enter_context(nc.Block())
        NQ = B_HPG // 2 * NC
        q5 = qd[:].rearrange("p (t h) n -> p t h n", h=B_HPG)
        scale = 1.0 / math.sqrt(B_HD)
        LO, HI = slice(0, B_HD), slice(B_HD, P)

        def queries(rows, h, c):
            return q5[rows, c * 4:(c + 1) * 4, h, :]

        def product(rows, n):
            return psQ[rows, n % 4, :].rearrange("p (t n) -> p t n", t=4)

        q_cols = bass.ds(grp * (B_HPG * B_HD), B_HPG * B_HD)

        @block.sync
        def _(sp):
            for i in range(2):
                sp.dma_start(wp[i * B_HD:(i + 1) * B_HD], dram["Wpost"][q_cols, :].rearrange("(h e) n -> e h n", e=B_HD))\
                  .then_inc(wp_loaded, 16)

        @block.tensor
        def _(pe):
            for c in range(NC):
                wait(pe, k.kl_done, c - 1, grp * NC)
                pe.matmul(psK[:, c % 2, :], wk[:], yT[:, c * BANK:(c + 1) * BANK], start=True, stop=True).then_inc(k.k_done, 1)

            for c in range(NC):
                wait(pe, k.v_kept, c - 1, grp * NC)
                for j in range(4):
                    last = pe.matmul(psV[:, c % 2, j * B_HD:(j + 1) * B_HD], yT[:, (4 * c + j) * P:(4 * c + j + 1) * P],
                                     wv[:], start=True, stop=True)
                last.then_inc(k.v_done, 1)

            for n in range(NQ):
                h, c = 2 * (n // NC), n % NC
                wait(pe, k.q_crossed, 2 * (n - 3), grp * (2 * NQ))
                pe.matmul(psQ[:, n % 4, :], wq[:, h:h + 2], yT[:, c * BANK:(c + 1) * BANK], start=True, stop=True)\
                  .then_inc(k.q_done, 1)
            pe.wait_ge(wp_loaded, 2 * 16 * grp + 2 * 16)

        @block.scalar
        def _(act):
            for c in range(NC):
                act.wait_ge(k.k_done, grp * NC + c + 1)
                act.copy(kh[:, c * BANK:(c + 1) * BANK], psK[:, c % 2, :]).then_inc(k.kh_done, 1)
            for n in range(NQ):
                h, c = 2 * (n // NC), n % NC
                act.wait_ge(k.q_done, grp * NQ + n + 1)
                act.activation(queries(LO, h, c), product(LO, n), ACT.Copy, scale=scale).then_inc(k.q_kept, 1)
                act.activation(queries(HI, h + 1, c), product(HI, n), ACT.Copy, scale=scale).then_inc(k.q_kept, 1)

        @block.vector
        def _(dve):
            for c in range(NC):
                cut = slice(c * BANK, (c + 1) * BANK)
                dve.wait_ge(k.kh_done, grp * NC + c + 1)
                dve.tensor_tensor(kl[:, cut], psK[:, c % 2, :], kh[:, cut].bitcast(F32), ALU.subtract).then_inc(k.kl_done, 1)

            for c in range(NC):
                values = psV[:, c % 2, 0:4 * B_HD].rearrange("p (t e) -> p t e", t=4)
                high, low = v[:, 4 * c:4 * c + 4, 0, :], v[:, 4 * c:4 * c + 4, 1, :]
                dve.wait_ge(k.v_done, grp * NC + c + 1)
                dve.tensor_copy(high, values).then_inc(k.v_high, 1)
                dve.wait_ge(k.v_high, grp * NC + c + 1)
                dve.tensor_tensor(low, values, high.bitcast(F32), ALU.subtract).then_inc(k.v_kept, 1)

            for n in range(NQ):
                h, c = 2 * (n // NC), n % NC
                dve.wait_ge(k.q_kept, grp * (2 * NQ) + 2 * n + 2)
                dve.tensor_scalar(queries(HI, h, c), product(LO, n), scale, None, ALU.mult).then_inc(k.q_crossed, 1)
                dve.tensor_scalar(queries(LO, h + 1, c), product(HI, n), scale, None, ALU.mult).then_inc(k.q_crossed, 1)


def b_group_attend(nc, g, k, grp, kh, kl, v, qd, wp, loads, loaded):
    with ExitStack() as ctx:
        m = Space(nc, ctx, "bt")
        U = NT * B_HPG
        qf = m.sb("qf", [P, 2, P])
        qh = m.sb("qh", [P, 2, P], F32R)
        qs = m.sb("qs", [P, 2, P], F32R)
        mx = m.sb("mx", [P, 2, 4])
        nb = m.sb("nb", [P, 2])
        probs = m.sb("probs", [P, 2, S])
        sums = m.sb("sums", [P, 4, EXPS])
        sm = m.sb("sm", [P, 1])
        rs = m.sb("rs", [P, 4])
        pth = m.sb("pth", [P, 2, NT, 2, P], F32R)
        ptl = m.sb("ptl", [P, 2, NT, 2, P], F32R)
        oT = m.sb("oT", [P, 2, 2 * P])
        psS = m.ps("psS", [P, 4, BANK])
        psT = m.ps("psT", [P, 2, BANK])
        psO = m.ps("psO", [P, BANK])
        psY = m.ps("psY", [P, BANK])
        block = ctx.enter_context(nc.Block())
        base = grp * U
        HI = slice(B_HD, P)

        @block.sync
        def _(sp):
            for dst, src in loads:
                sp.dma_start(dst, src).then_inc(loaded, 16)

        @block.gpsimd
        def _(pool):
            def stage(u, s):
                wait_apart(pool, k.scored, 4 * (u - 1), 4 * base)
                wait_apart(pool, k.q_staged, u, base)
                pool.tensor_copy(qf[:, s, :], qd[:, u, :]).then_inc(k.q_taken, 1)
                wait_apart(pool, k.q_taken, u + 1, base)
                pool.tensor_copy(qh[HI, s, :], qf[HI, s, :]).then_inc(k.q_hi, 1)
                wait_apart(pool, k.q_hi, u + 1, base)
                pool.tensor_copy(qs[0:B_HD, s, :], qf[0:B_HD, s, :]).then_inc(k.q_top, 1)
                pool.tensor_tensor(qs[HI, s, :], qf[HI, s, :], qh[HI, s, :].bitcast(F32), ALU.subtract)\
                    .then_inc(k.q_staged, 1)

            pipeline(pool, U, [(stage, 0)])

        @block.tensor
        def _(pe):
            def score(u, s, c):
                cut = slice(c * BANK, (c + 1) * BANK)
                if c == 0:
                    pe.wait_ge(k.q_staged, u + 1 + base)
                    pe.wait_ge(k.q_top, u + 1 + base)
                wait(pe, k.exped, EXPS * (u - 1) + c * EXPS // 4 + 1, EXPS * base)
                pe.matmul(psS[:, c, :], qs[:, s % 2, :], kh[:, cut], start=True, stop=False)
                pe.matmul(psS[:, c, :], qs[:, s % 2, :], kl[:, cut], start=False, stop=True).then_inc(k.scored, 1)

            def turn(u, s, q):
                pe.wait_ge(k.exped, EXPS * u + q * EXPS // 4 + 1 + EXPS * base)
                wait(pe, k.low_kept, 4 * u + q - 1, 4 * base)
                for j in range(4):
                    last = pe.transpose(psT[:, q % 2, j * P:(j + 1) * P],
                                        probs[:, s % 2, (4 * q + j) * P:(4 * q + j + 1) * P], g.ident[:])
                last.then_inc(k.transposed, 1)

            def weigh(u, s, half):
                second = s % 2
                quarter = 2 * second + half
                pe.wait_ge(k.low_kept, 4 * (u + 1 - second) + quarter + 1 + 4 * base)
                if quarter == 0:
                    wait(pe, k.out_kept, u, base)
                for kt in range(4 * quarter, 4 * quarter + 4):
                    for part in (pth, ptl):
                        last = pe.matmul(psO[:, 0:2 * P], v[:, kt], part[:, s // 2, kt],
                                         start=kt == 0 and part is pth, stop=kt == NT - 1 and part is ptl)
                last.then_inc(k.weighed, 1)

            def project(u, s):
                pe.wait_ge(k.out_kept, u + 2 - s % 2 + base)
                wait(pe, k.added, u, base)
                pe.matmul(psY[:, 0:D], oT[:, s // 2, (s % 2) * P:(s % 2 + 1) * P], wp[:, s, :],
                          start=True, stop=True).then_inc(k.projected, 1)

            def C(c, lag):
                return lambda u, s: score(u, s, c), lag

            def T(q, lag):
                return lambda u, s: turn(u, s, q), lag

            def W(half, lag):
                return lambda u, s: weigh(u, s, half), lag

            order = [T(0, 3), W(0, 5), T(1, 3), C(0, 1), T(2, 3), C(1, 1), W(1, 5), C(2, 1), T(3, 3),
                     C(3, 1), (project, 6)]
            pipeline(pe, U, order, unroll=4)
            pe.wait_ge(loaded, 16 * len(loads) * grp + 2 * 16 * len(loads))

        @block.vector
        def _(dve):
            def top(u, s, c):
                dve.wait_ge(k.scored, 4 * u + c + 1 + 4 * base)
                if c == 0:
                    wait(dve, k.biased, u - 1, base)
                dve.tensor_reduce(mx[:, s % 2, c:c + 1], psS[:, c, :], axis=AX.X, op=ALU.max).then_inc(k.maxed, 1)

            def bias(u, s):
                dve.wait_ge(k.maxed, 4 * u + 4 + 4 * base)
                wait(dve, k.exped, EXPS * (u - 1), EXPS * base)
                dve.tensor_reduce(nb[:, s % 2:s % 2 + 1], mx[:, s % 2, :], axis=AX.X, op=ALU.max, negate=True)\
                   .then_inc(k.biased, 1)

            def low(u, s, q):
                dve.wait_ge(k.high_kept, 4 * u + q + 1 + 4 * base)
                place = slice(4 * q, 4 * q + 4)
                dve.tensor_tensor(ptl[:, s // 2, place, s % 2, :], psT[:, q % 2, :].rearrange("p (t n) -> p t n", t=4),
                                  pth[:, s // 2, place, s % 2, :].bitcast(F32), ALU.subtract).then_inc(k.low_kept, 1)

            def recip(u, s):
                dve.wait_ge(k.exped, EXPS * u + EXPS + EXPS * base)
                wait(dve, k.recip, u, base)
                dve.tensor_reduce(sm[:], sums[:, s, :], axis=AX.X, op=ALU.add).then_inc(k.summed, 1)
                dve.wait_ge(k.summed, u + 1 + base)
                wait(dve, k.added, u - 3, base)
                dve.reciprocal(rs[:, s:s + 1], sm[:]).then_inc(k.recip, 1)

            def add(u, s):
                tile = (u - s) // 4 if isinstance(u, int) else (u - s) >> 2
                dve.wait_ge(k.projected, u + 1 + base)
                dve.wait_ge(k.recip, u + 1 + base)
                wait(dve, k.added, u, base)
                dve.scalar_tensor_tensor(g.x[:, tile, :], psY[:, 0:D], rs[:, s:s + 1], g.x[:, tile, :],
                                         ALU.mult, ALU.add).then_inc(k.added, 1)

            def L(q, lag):
                return lambda u, s: low(u, s, q), lag

            def M(c, lag):
                return lambda u, s: top(u, s, c), lag

            order = [L(0, 2), (add, 6), (recip, 3), M(0, 0), L(1, 2), M(1, 0), L(2, 2), M(2, 0), M(3, 0),
                     (bias, 0), L(3, 2)]
            pipeline(dve, U, order, unroll=4)

        @block.scalar
        def _(act):
            def exp(u, s, c):
                if c == 0:
                    act.wait_ge(k.biased, u + 1 + base)
                    wait(act, k.transposed, 4 * (u - 1), 4 * base)
                    wait(act, k.recip, u - 3, base)
                n = 4 // EXPS
                act.activation(probs[:, s % 2, c * n * BANK:(c + 1) * n * BANK].rearrange("p (b n) -> p b n", b=n),
                               psS[:, n * c:n * (c + 1), :], ACT.Exp, bias=nb[:, s % 2:s % 2 + 1],
                               accum_out=sums[:, s, c:c + 1]).then_inc(k.exped, 1)

            def high(u, s, q):
                act.wait_ge(k.transposed, 4 * u + q + 1 + 4 * base)
                wait(act, k.weighed, 2 * (u - s % 2 - 4) + q + 1, 2 * base)
                act.copy(pth[:, s // 2, 4 * q:4 * q + 4, s % 2, :], psT[:, q % 2, :].rearrange("p (t n) -> p t n", t=4))\
                   .then_inc(k.high_kept, 1)

            def keep(u, s):
                if s % 2 == 0:
                    return
                act.wait_ge(k.weighed, 2 * u + 2 + 2 * base)
                wait(act, k.projected, u - 3, base)
                act.copy(oT[:, s // 2, :], psO[:, 0:2 * P]).then_inc(k.out_kept, 2)

            def H(q, lag):
                return lambda u, s: high(u, s, q), lag

            def E(c, lag):
                return lambda u, s: exp(u, s, c), lag

            order = [H(1, 3), E(2, 2), H(2, 3), E(3, 2), (keep, 5), H(3, 3), H(0, 2), E(0, 1), E(1, 1)]
            pipeline(act, U, order, unroll=4)


def store_phase(nc, g, out):
    with nc.semaphore("stored") as stored, nc.Block() as block:
        @block.sync
        def _(sp):
            sp.dma_start(out[0].rearrange("(t p) d -> p t d", p=P), g.x[:]).then_inc(stored, 16)
            sp.wait_ge(stored, 16)


def build(nc, dram, out):
    g = Names()
    with ExitStack() as ctx:
        LAUNCH.ctx = ctx
        m = Space(nc, ctx, "g")
        g.x = m.sb("x", [P, NT, D])
        g.ident = m.sb("ident", [P, P])
        g.zcol = m.sb("zcol", [P, 1])
        g.mhalf = m.sb("mhalf", [P, 1])
        g.tab = m.sb("tab", [P, NT, 4, F_HD])
        g.bandmask = m.sb("bandmask", [P, 2, BANDK])
        LAUNCH.marks, LAUNCH.constants_made = m.sem("marks"), m.sem("constants_made")
        LAUNCH.norm = NormSems(sem_maker(nc, "n"))
        LAUNCH.norm.runs = LAUNCH.norm.runs_T = 0
        tables = [(g.tab[:], dram["tables"].rearrange("(t p) a d -> p t a d", p=P)),
                  (g.bandmask[:], dram["bandmask"])]
        x_load = (g.x[:], dram["x"][0].rearrange("(t p) d -> p t d", p=P))
        load_phase(nc, g, [x_load])
        attention_a(nc, g, dram, tables)
        k = Names()
        k.first_loaded, k.later_loaded = m.sem("first_loaded"), m.sem("later_loaded")
        k.qkv, k.band, k.mlp = (QkvSems(sem_maker(nc, "fq")), BandSems(sem_maker(nc, "fb")),
                                MlpSems(sem_maker(nc, "fm")))
        ffn(nc, g, dram, 0, k)
        attention_b(nc, g, dram)
        ffn(nc, g, dram, 1, k)
        store_phase(nc, g, out)


_A = "L0_attn_a_"
_NAMES = {"x": _A + "x", "wq_lin": _A + "wq_lin", "bq_lin": _A + "bq_lin", "wk_lin": _A + "wk_lin",
          "bk_lin": _A + "bk_lin", "wv_lin": _A + "wv_lin", "bv_lin": _A + "bv_lin", "wq_loc": _A + "wq_loc",
          "bq_loc": _A + "bq_loc", "wk_loc": _A + "wk_loc", "bk_loc": _A + "bk_loc", "wv_loc": _A + "wv_loc",
          "bv_loc": _A + "bv_loc", "wo": _A + "wo", "bo": _A + "bo", "wg1": _A + "wg1", "bg1": _A + "bg1",
          "wg2": _A + "wg2", "bg2": _A + "bg2", "ln_g": _A + "ln_g", "ln_b": _A + "ln_b",
          "Wq": "L0_attn_b_Wq", "Wk": "L0_attn_b_Wk", "Wv": "L0_attn_b_Wv", "Wpost": "L0_attn_b_Wpost",
          "wqkv": "L0_ffn_wqkv", "q_scale": "L0_ffn_q_scale", "k_scale": "L0_ffn_k_scale", "fwo": "L0_ffn_wo",
          "fln_g": "L0_ffn_ln_g", "fln_b": "L0_ffn_ln_b", "w1": "L0_ffn_w1", "b1": "L0_ffn_b1",
          "w2": "L0_ffn_w2", "b2": "L0_ffn_b2"}


def constants():
    f = np.float32
    half = np.arange(0, F_HD, 2, dtype=f)
    inv = (f(1.0) / np.power(f(10000.0), half / f(F_HD))).astype(f)
    t = np.arange(S, dtype=f)
    fr = (t[:, None] * inv[None, :]).astype(f)
    b = ((half + f(0.4 * F_HD)) / f(1.4 * F_HD)).astype(f)
    scale = np.power(b[None, :], ((t - S // 2) / f(32.0)).astype(f)[:, None]).astype(f)
    cos, sin = np.cos(fr).astype(f), np.sin(fr).astype(f)
    tab = np.zeros((S, 4, F_HD), f)
    for j, sc in enumerate((scale, f(1.0) / scale)):
        gain = f((8.0, 1.0)[j])
        tab[:, j] = gain * np.concatenate([cos * sc, cos * sc], 1)
        tab[:, 2 + j] = gain * np.concatenate([-sin * sc, sin * sc], 1)
    r, c = np.arange(P)[:, None], np.arange(BANDK)[None, :]
    band = np.where((c >= r) & (c <= r + HALO_F), 0.0, NEG).astype(f)
    band0 = np.where(c >= HALO_F, band, f(NEG)).astype(f)
    edge = np.zeros((P, 2, BANDK), f)
    edge[:, 0, :HALO_A] = NEG
    edge[:, 1, HALO_A + P:] = NEG
    hmask = (np.arange(D)[:, None] // A_HD == np.arange(A_HEADS)[None, :]).astype(f)
    return {"tables": tab, "bandmask": np.stack([band, band0], 1), "edge": edge, "hmask": hmask}


def band_of(rel_bias):
    r, c = np.arange(P)[:, None], np.arange(BANDK)[None, :]
    inside = (c >= r) & (c <= r + 2 * HALO_A)
    at = np.where(inside, c - r + HALO_A, 0)
    rows = rel_bias[at]
    return np.ascontiguousarray(np.where(inside[:, :, None], rows, np.float32(NEG)).transpose(0, 2, 1))


def kernel(**inputs):
    import concourse.bacc as _bacc
    from concourse.bass_utils import run_bass_kernel_spmd as _run

    arrays = {n: np.ascontiguousarray(inputs[full]) for n, full in _NAMES.items()}
    arrays["relb"] = band_of(np.asarray(inputs[_A + "rel_bias"]))
    arrays.update({n: np.ascontiguousarray(a) for n, a in constants().items()})
    nc = _bacc.Bacc("TRN2", target_bir_lowering=False, num_devices=1)
    dram = {n: nc.dram_tensor(f"in_{n}", a.shape, F32, kind="ExternalInput").ap() for n, a in arrays.items()}
    shape = (1, S, D)
    out = nc.dram_tensor("out_x", shape, F32, kind="ExternalOutput").ap()
    build(nc, dram, out)
    r = _run(nc, [{f"in_{n}": a for n, a in arrays.items()}], core_ids=[0])
    return r.results[0]["out_x"]
```
